# Optimizing a Trainium2 kernel written in Bass

```python
import numpy as np
import jax
import jax.numpy as jnp

def _softmax(x, axis=-1):
    return jax.nn.softmax(x, axis=axis)

def _gelu(x):
    return jax.nn.gelu(x, approximate=True)

def _silu(x):
    return jax.nn.silu(x)

def _sigmoid(x):
    return jax.nn.sigmoid(x)

def _layernorm(x, axis=-1, eps=1e-05):
    m = jnp.mean(x, axis=axis, keepdims=True)
    v = jnp.var(x, axis=axis, keepdims=True)
    return (x - m) / jnp.sqrt(v + eps)

def _scatter_add(tgt, idx, src, axis=0):
    return tgt.at[idx].add(src)

def _segment_sum(src, seg, n):
    return jax.ops.segment_sum(src, seg, n)
kernel_name = 'mk_vit_tower_d2_tok_img768_r4_dc9360'

def setup_inputs(seed: int=0):
    np.random.seed(seed)
    _w = jnp.asarray

    def _rec_inputs():
        import jax
        import jax.numpy as jnp
        _rk = jax.random.key(seed)
        x = -0.00016672 + 0.999947 * jax.random.normal(jax.random.fold_in(_rk, 1), (64, 3, 96, 96), jnp.float32)
        return x
    x = _rec_inputs()

    def _L0_tok_setup():
        import jax, jax.numpy as jnp
        import numpy as np
        B, C, H, Wd = (64, 3, 96, 96)
        PH = PW = 16
        NH, NW = (H // PH, Wd // PW)
        NP = NH * NW
        PD = C * PH * PW
        ED = 192
        EPS = 1e-05

        def layernorm(x, g, b):
            mu = jnp.mean(x, axis=-1, keepdims=True)
            var = jnp.mean(jnp.square(x - mu), axis=-1, keepdims=True)
            return (x - mu) * jax.lax.rsqrt(var + EPS) * g + b
        key = jax.random.key(seed)
        ks = jax.random.split(key, 6)
        return {'x': jax.random.normal(ks[0], (B, C, H, Wd), dtype=jnp.float32), 'ln1_g': jnp.ones((PD,), jnp.float32), 'ln1_b': jnp.zeros((PD,), jnp.float32), 'W': jax.random.normal(ks[1], (PD, ED), dtype=jnp.float32) * 0.02, 'b': jnp.zeros((ED,), jnp.float32), 'ln2_g': jnp.ones((ED,), jnp.float32), 'ln2_b': jnp.zeros((ED,), jnp.float32), 'cls_token': jax.random.normal(ks[2], (ED,), dtype=jnp.float32), 'pos_embed': jax.random.normal(ks[3], (1, NP + 1, ED), dtype=jnp.float32) * 0.02}
    _L0_tok_all = _L0_tok_setup()
    _L0_tok_in = {k: v for k, v in _L0_tok_all.items() if k in ('ln1_g', 'ln1_b', 'W', 'b', 'ln2_g', 'ln2_b', 'cls_token', 'pos_embed')}
    del _L0_tok_all

    def _L0_attn_setup():
        import jax, jax.numpy as jnp
        import numpy as np
        B, T, DM = (4, 512, 192)
        H, D = (4, 64)
        DIM = H * D

        def _feature_map(x):
            return jax.nn.elu(x) + 1.0
        key = jax.random.key(seed)
        kx, kq, kk, kv, ko, kg = jax.random.split(key, 6)
        s = 0.02
        return {'x': jax.random.normal(kx, (B, T, DM), jnp.float32), 'Wq': jax.random.normal(kq, (DM, DIM), jnp.float32) * s, 'Wk': jax.random.normal(kk, (DM, DIM), jnp.float32) * s, 'Wv': jax.random.normal(kv, (DM, DIM), jnp.float32) * s, 'Wo': jax.random.normal(ko, (DIM, DM), jnp.float32) * s, 'Wg': jax.random.normal(kg, (DM, DM), jnp.float32) * s}
    _L0_attn_all = _L0_attn_setup()
    _L0_attn_in = {k: v for k, v in _L0_attn_all.items() if k in ('Wq', 'Wk', 'Wv', 'Wo', 'Wg')}
    del _L0_attn_all

    def _L0_ffn_setup():
        import jax, jax.numpy as jnp
        import numpy as np
        B, M, D = (32, 196, 192)
        N, P, H = (64, 1, 768)
        EPS = 1e-12

        def _l2norm(v, axis):
            n = jnp.sqrt(jnp.sum(v * v, axis=axis, keepdims=True))
            return v / jnp.maximum(n, EPS)
        key = jax.random.key(seed)
        ks = jax.random.split(key, 7)
        x = jax.random.normal(ks[0], (B, M, D), dtype=jnp.float32)
        phi = jax.random.normal(ks[1], (D, N, P), dtype=jnp.float32) * (1.0 / D ** 0.5)
        scale = jnp.ones((1,), dtype=jnp.float32)
        w1 = jax.random.normal(ks[2], (N, D, H), dtype=jnp.float32) * (1.0 / D ** 0.5)
        b1 = jnp.zeros((N, H), dtype=jnp.float32)
        w2 = jax.random.normal(ks[3], (N, H, D), dtype=jnp.float32) * (1.0 / H ** 0.5)
        b2 = jnp.zeros((N, D), dtype=jnp.float32)
        return {'x': x, 'phi': phi, 'scale': scale, 'w1': w1, 'b1': b1, 'w2': w2, 'b2': b2}
    _L0_ffn_all = _L0_ffn_setup()
    _L0_ffn_in = {k: v for k, v in _L0_ffn_all.items() if k in ('phi', 'scale', 'w1', 'b1', 'w2', 'b2')}
    del _L0_ffn_all

    def _L1_attn_setup():
        import jax, jax.numpy as jnp
        import numpy as np
        KERNEL = 5
        NUM_HEADS = 4

        def _window_starts(L, k):
            pad = k // 2
            return jnp.clip(jnp.arange(L) - pad, 0, L - k)

        def _neighborhood_attention_2d(xs, qkv_w, qkv_b, rpb, proj_w, proj_b):
            H, W, D = xs.shape
            nh, k = (NUM_HEADS, KERNEL)
            dh = D // nh
            qkv = xs @ qkv_w.T + qkv_b
            qkv = qkv.reshape(H, W, 3, nh, dh).transpose(2, 3, 0, 1, 4)
            q, kmat, vmat = (qkv[0], qkv[1], qkv[2])
            q = q * dh ** (-0.5)
            sh = _window_starts(H, k)
            sw = _window_starts(W, k)
            off = jnp.arange(k)
            idx_h = sh[:, None] + off[None, :]
            idx_w = sw[:, None] + off[None, :]
            kk = kmat[:, idx_h][:, :, :, idx_w]
            vv = vmat[:, idx_h][:, :, :, idx_w]
            logits = jnp.einsum('nhwd,nhawbd->nhwab', q, kk)
            bh = idx_h - jnp.arange(H)[:, None] + (k - 1)
            bw = idx_w - jnp.arange(W)[:, None] + (k - 1)
            bias = rpb[:, bh[:, None, :, None], bw[None, :, None, :]]
            logits = logits + bias
            attn = jax.nn.softmax(logits.reshape(nh, H, W, k * k), axis=-1).reshape(nh, H, W, k, k)
            out = jnp.einsum('nhwab,nhawbd->nhwd', attn, vv)
            out = out.transpose(1, 2, 0, 3).reshape(H, W, D)
            return out @ proj_w.T + proj_b
        H, W = (96, 96)
        IN_D, HID, OUT_D = (192, 96, 192)
        key = jax.random.key(seed)
        ks = jax.random.split(key, 16)
        s = 0.02
        return {'x': jax.random.normal(ks[0], (H, W, IN_D), dtype=jnp.float32), 'fc1_w': jax.random.normal(ks[1], (HID, IN_D), dtype=jnp.float32) * s, 'fc1_b': jnp.zeros((HID,), dtype=jnp.float32), 'convA_w': jax.random.normal(ks[2], (64, HID), dtype=jnp.float32) * s, 'convA_b': jnp.zeros((64,), dtype=jnp.float32), 'convB_w': jax.random.normal(ks[3], (HID, 64), dtype=jnp.float32) * s, 'convB_b': jnp.zeros((HID,), dtype=jnp.float32), 'qkv_w': jax.random.normal(ks[4], (3 * HID, HID), dtype=jnp.float32) * s, 'qkv_b': jnp.zeros((3 * HID,), dtype=jnp.float32), 'rpb': jax.random.normal(ks[5], (NUM_HEADS, 2 * KERNEL - 1, 2 * KERNEL - 1), dtype=jnp.float32) * s, 'proj_w': jax.random.normal(ks[6], (HID, HID), dtype=jnp.float32) * s, 'proj_b': jnp.zeros((HID,), dtype=jnp.float32), 'fc2_w': jax.random.normal(ks[7], (OUT_D, HID), dtype=jnp.float32) * s, 'fc2_b': jnp.zeros((OUT_D,), dtype=jnp.float32)}
    _L1_attn_all = _L1_attn_setup()
    _L1_attn_in = {k: v for k, v in _L1_attn_all.items() if k in ('fc1_w', 'fc1_b', 'convA_w', 'convA_b', 'convB_w', 'convB_b', 'qkv_w', 'qkv_b', 'rpb', 'proj_w', 'proj_b', 'fc2_w', 'fc2_b')}
    del _L1_attn_all

    def _L1_ffn_setup():
        import jax, jax.numpy as jnp
        import numpy as np
        import math
        B, S, D = (4, 1024, 192)
        E = 8
        TOP_K = 2
        H = 512
        CAP_F = 1.25
        EPS = 1e-06
        ALPHA = 1.0
        key = jax.random.key(seed)
        k0, k1, k2, k3 = jax.random.split(key, 4)
        x = jax.random.normal(k0, (B, S, D), jnp.float32)
        gate_w = jax.random.normal(k1, (E, D), jnp.float32) * 0.02
        w13 = jax.random.normal(k2, (E, 2 * H, D), jnp.float32) * 0.02
        w2 = jax.random.normal(k3, (E, D, H), jnp.float32) * 0.02
        norm_w = jnp.ones((E, D), jnp.float32)
        return {'x': x, 'gate_w': gate_w, 'w13': w13, 'w2': w2, 'norm_w': norm_w}
    _L1_ffn_all = _L1_ffn_setup()
    _L1_ffn_in = {k: v for k, v in _L1_ffn_all.items() if k in ('gate_w', 'w13', 'w2', 'norm_w')}
    del _L1_ffn_all
    return {'x': x, 'L0_tok_ln1_g': _L0_tok_in['ln1_g'], 'L0_tok_ln1_b': _L0_tok_in['ln1_b'], 'L0_tok_W': _L0_tok_in['W'], 'L0_tok_b': _L0_tok_in['b'], 'L0_tok_ln2_g': _L0_tok_in['ln2_g'], 'L0_tok_ln2_b': _L0_tok_in['ln2_b'], 'L0_tok_cls_token': _L0_tok_in['cls_token'], 'L0_tok_pos_embed': _L0_tok_in['pos_embed'], 'L0_attn_Wq': _L0_attn_in['Wq'], 'L0_attn_Wk': _L0_attn_in['Wk'], 'L0_attn_Wv': _L0_attn_in['Wv'], 'L0_attn_Wo': _L0_attn_in['Wo'], 'L0_attn_Wg': _L0_attn_in['Wg'], 'L0_ffn_phi': _L0_ffn_in['phi'], 'L0_ffn_scale': _L0_ffn_in['scale'], 'L0_ffn_w1': _L0_ffn_in['w1'], 'L0_ffn_b1': _L0_ffn_in['b1'], 'L0_ffn_w2': _L0_ffn_in['w2'], 'L0_ffn_b2': _L0_ffn_in['b2'], 'L1_attn_fc1_w': _L1_attn_in['fc1_w'], 'L1_attn_fc1_b': _L1_attn_in['fc1_b'], 'L1_attn_convA_w': _L1_attn_in['convA_w'], 'L1_attn_convA_b': _L1_attn_in['convA_b'], 'L1_attn_convB_w': _L1_attn_in['convB_w'], 'L1_attn_convB_b': _L1_attn_in['convB_b'], 'L1_attn_qkv_w': _L1_attn_in['qkv_w'], 'L1_attn_qkv_b': _L1_attn_in['qkv_b'], 'L1_attn_rpb': _L1_attn_in['rpb'], 'L1_attn_proj_w': _L1_attn_in['proj_w'], 'L1_attn_proj_b': _L1_attn_in['proj_b'], 'L1_attn_fc2_w': _L1_attn_in['fc2_w'], 'L1_attn_fc2_b': _L1_attn_in['fc2_b'], 'L1_ffn_gate_w': _L1_ffn_in['gate_w'], 'L1_ffn_w13': _L1_ffn_in['w13'], 'L1_ffn_w2': _L1_ffn_in['w2'], 'L1_ffn_norm_w': _L1_ffn_in['norm_w']}

def reference(x, L0_tok_ln1_g, L0_tok_ln1_b, L0_tok_W, L0_tok_b, L0_tok_ln2_g, L0_tok_ln2_b, L0_tok_cls_token, L0_tok_pos_embed, L0_attn_Wq, L0_attn_Wk, L0_attn_Wv, L0_attn_Wo, L0_attn_Wg, L0_ffn_phi, L0_ffn_scale, L0_ffn_w1, L0_ffn_b1, L0_ffn_w2, L0_ffn_b2, L1_attn_fc1_w, L1_attn_fc1_b, L1_attn_convA_w, L1_attn_convA_b, L1_attn_convB_w, L1_attn_convB_b, L1_attn_qkv_w, L1_attn_qkv_b, L1_attn_rpb, L1_attn_proj_w, L1_attn_proj_b, L1_attn_fc2_w, L1_attn_fc2_b, L1_ffn_gate_w, L1_ffn_w13, L1_ffn_w2, L1_ffn_norm_w):
    import jax
    import jax.numpy as jnp

    def _L0_tok_ref(x, ln1_g, ln1_b, W, b, ln2_g, ln2_b, cls_token, pos_embed):
        import jax, jax.numpy as jnp
        import numpy as np
        B, C, H, Wd = (64, 3, 96, 96)
        PH = PW = 16
        NH, NW = (H // PH, Wd // PW)
        NP = NH * NW
        PD = C * PH * PW
        ED = 192
        EPS = 1e-05

        def layernorm(x, g, b):
            mu = jnp.mean(x, axis=-1, keepdims=True)
            var = jnp.mean(jnp.square(x - mu), axis=-1, keepdims=True)
            return (x - mu) * jax.lax.rsqrt(var + EPS) * g + b
        bsz = x.shape[0]
        p = x.reshape(bsz, C, NH, PH, NW, PW)
        p = p.transpose(0, 2, 4, 3, 5, 1).reshape(bsz, NP, PD)
        out = layernorm(p, ln1_g, ln1_b)
        out = jnp.einsum('bnp,pe->bne', out, W) + b
        out = layernorm(out, ln2_g, ln2_b)
        cls = jnp.broadcast_to(cls_token, (bsz, 1, ED))
        out = jnp.concatenate([cls, out], axis=1)
        out = out + pos_embed
        return out

    def _L0_attn_ref(x, Wq, Wk, Wv, Wo, Wg):
        import jax, jax.numpy as jnp
        import numpy as np
        B, T, DM = (4, 512, 192)
        H, D = (4, 64)
        DIM = H * D

        def _feature_map(x):
            return jax.nn.elu(x) + 1.0
        Bx, Tx, _ = x.shape
        q = _feature_map((x @ Wq).reshape(Bx, Tx, H, D))
        k = _feature_map((x @ Wk).reshape(Bx, Tx, H, D))
        v = (x @ Wv).reshape(Bx, Tx, H, D)
        qT = q.transpose(1, 0, 2, 3)
        kT = k.transpose(1, 0, 2, 3)
        vT = v.transpose(1, 0, 2, 3)
        S0 = jnp.zeros((Bx, H, D, D), x.dtype)
        z0 = jnp.zeros((Bx, H, D), x.dtype)

        def step(carry, inp):
            S, z = carry
            qi, ki, vi = inp
            S = S + ki[..., :, None] * vi[..., None, :]
            z = z + ki
            num = jnp.einsum('bhd,bhde->bhe', qi, S)
            den = jnp.maximum(jnp.sum(qi * z, axis=-1), 1e-06)
            return ((S, z), num / den[..., None])
        (_, _), outT = jax.lax.scan(step, (S0, z0), (qT, kT, vT))
        out = outT.transpose(1, 0, 2, 3).reshape(Bx, Tx, DIM)
        gate = jax.nn.sigmoid(x @ Wg)
        return out @ Wo * gate

    def _L0_ffn_ref(x, phi, scale, w1, b1, w2, b2):
        import jax, jax.numpy as jnp
        import numpy as np
        B, M, D = (32, 196, 192)
        N, P, H = (64, 1, 768)
        EPS = 1e-12

        def _l2norm(v, axis):
            n = jnp.sqrt(jnp.sum(v * v, axis=axis, keepdims=True))
            return v / jnp.maximum(n, EPS)
        xn = _l2norm(x, axis=2)
        phin = scale * _l2norm(phi, axis=0)
        logits = jnp.einsum('bmd,dnp->bmnp', xn, phin)
        d = jax.nn.softmax(logits, axis=1)
        b_, m_, n_, p_ = logits.shape
        c = jax.nn.softmax(logits.reshape(b_, m_, n_ * p_), axis=-1).reshape(b_, m_, n_, p_)
        xs = jnp.einsum('bmd,bmnp->bnpd', xn, d)
        h = jax.nn.gelu(jnp.einsum('bnpd,ndh->bnph', xs, w1) + b1[None, :, None, :], approximate=False)
        ys = jnp.einsum('bnph,nhd->bnpd', h, w2) + b2[None, :, None, :]
        y = jnp.einsum('bnpd,bmnp->bmd', ys, c)
        return y

    def _L1_attn_ref(x, fc1_w, fc1_b, convA_w, convA_b, convB_w, convB_b, qkv_w, qkv_b, rpb, proj_w, proj_b, fc2_w, fc2_b):
        import jax, jax.numpy as jnp
        import numpy as np
        KERNEL = 5
        NUM_HEADS = 4

        def _window_starts(L, k):
            pad = k // 2
            return jnp.clip(jnp.arange(L) - pad, 0, L - k)

        def _neighborhood_attention_2d(xs, qkv_w, qkv_b, rpb, proj_w, proj_b):
            H, W, D = xs.shape
            nh, k = (NUM_HEADS, KERNEL)
            dh = D // nh
            qkv = xs @ qkv_w.T + qkv_b
            qkv = qkv.reshape(H, W, 3, nh, dh).transpose(2, 3, 0, 1, 4)
            q, kmat, vmat = (qkv[0], qkv[1], qkv[2])
            q = q * dh ** (-0.5)
            sh = _window_starts(H, k)
            sw = _window_starts(W, k)
            off = jnp.arange(k)
            idx_h = sh[:, None] + off[None, :]
            idx_w = sw[:, None] + off[None, :]
            kk = kmat[:, idx_h][:, :, :, idx_w]
            vv = vmat[:, idx_h][:, :, :, idx_w]
            logits = jnp.einsum('nhwd,nhawbd->nhwab', q, kk)
            bh = idx_h - jnp.arange(H)[:, None] + (k - 1)
            bw = idx_w - jnp.arange(W)[:, None] + (k - 1)
            bias = rpb[:, bh[:, None, :, None], bw[None, :, None, :]]
            logits = logits + bias
            attn = jax.nn.softmax(logits.reshape(nh, H, W, k * k), axis=-1).reshape(nh, H, W, k, k)
            out = jnp.einsum('nhwab,nhawbd->nhwd', attn, vv)
            out = out.transpose(1, 2, 0, 3).reshape(H, W, D)
            return out @ proj_w.T + proj_b
        xs = x @ fc1_w.T + fc1_b
        a = xs @ convA_w.T + convA_b
        b = a @ convB_w.T + convB_b
        xs = b * 1.0 + xs
        xs = jax.nn.gelu(xs, approximate=False)
        xs = _neighborhood_attention_2d(xs, qkv_w, qkv_b, rpb, proj_w, proj_b)
        xs = xs @ fc2_w.T + fc2_b
        return x + xs

    def _L1_ffn_ref(x, gate_w, w13, w2, norm_w):
        import jax, jax.numpy as jnp
        import numpy as np
        import math
        B, S, D = (4, 1024, 192)
        E = 8
        TOP_K = 2
        H = 512
        CAP_F = 1.25
        EPS = 1e-06
        ALPHA = 1.0
        Bx, Sx, Dx = x.shape
        N = Bx * Sx
        cap = int(math.ceil(CAP_F * TOP_K * N / E))
        xf = x.reshape(N, Dx)
        logits = xf.astype(jnp.float32) @ gate_w.T
        probs = jax.nn.softmax(logits, axis=-1)
        top_p, top_i = jax.lax.top_k(probs, TOP_K)
        w = top_p / jnp.sum(top_p, axis=-1, keepdims=True)
        flat_e = top_i.reshape(-1)
        onehot = jax.nn.one_hot(flat_e, E, dtype=jnp.int32)
        pos = jnp.take_along_axis(jnp.cumsum(onehot, axis=0) - 1, flat_e[:, None], axis=1)[:, 0]
        keep = pos < cap
        didx = flat_e * cap + jnp.minimum(pos, cap - 1)
        safe = jnp.where(keep, didx, E * cap)
        x_rep = jnp.repeat(xf, TOP_K, axis=0)
        buf = jnp.zeros((E * cap + 1, Dx), x.dtype).at[safe].set(x_rep)
        buf = buf[:-1].reshape(E, cap, Dx)
        z = 2.0 * buf
        z = z * jax.lax.rsqrt(jnp.mean(z * z, axis=-1, keepdims=True) + EPS)
        z = z * norm_w[:, None, :]
        gu = jnp.einsum('ecd,ehd->ech', z, w13)
        g, u = jnp.split(gu, 2, axis=-1)
        y = buf + ALPHA * jnp.einsum('ech,edh->ecd', jax.nn.silu(g) * u, w2)
        y_tok = y.reshape(E * cap, Dx)[didx]
        cw = (w.reshape(-1) * keep.astype(w.dtype)).astype(x.dtype)
        out = (cw[:, None] * y_tok).reshape(N, TOP_K, Dx).sum(axis=1)
        return out.reshape(Bx, Sx, Dx)
    h = _L0_tok_ref(x, L0_tok_ln1_g, L0_tok_ln1_b, L0_tok_W, L0_tok_b, L0_tok_ln2_g, L0_tok_ln2_b, L0_tok_cls_token, L0_tok_pos_embed)
    h = h + _L0_attn_ref(_layernorm(h, axis=-1), L0_attn_Wq, L0_attn_Wk, L0_attn_Wv, L0_attn_Wo, L0_attn_Wg)
    h = h + _L0_ffn_ref(_layernorm(h, axis=-1), L0_ffn_phi, L0_ffn_scale, L0_ffn_w1, L0_ffn_b1, L0_ffn_w2, L0_ffn_b2)
    h = h + _L1_attn_ref(_layernorm(h, axis=-1), L1_attn_fc1_w, L1_attn_fc1_b, L1_attn_convA_w, L1_attn_convA_b, L1_attn_convB_w, L1_attn_convB_b, L1_attn_qkv_w, L1_attn_qkv_b, L1_attn_rpb, L1_attn_proj_w, L1_attn_proj_b, L1_attn_fc2_w, L1_attn_fc2_b)
    h = h + _L1_ffn_ref(_layernorm(h, axis=-1), L1_ffn_gate_w, L1_ffn_w13, L1_ffn_w2, L1_ffn_norm_w)
    return h

_drawn_inputs = setup_inputs


def setup_inputs(seed=0):
    import zlib

    import numpy as np

    out = dict(_drawn_inputs(seed))
    spreads = {'L0_tok_ln1_g': (1.0, 0.2),
     'L0_tok_ln1_b': (0.0, 0.1),
     'L0_tok_b': (0.0, 0.1),
     'L0_tok_ln2_g': (1.0, 0.2),
     'L0_tok_ln2_b': (0.0, 0.1),
     'L0_ffn_b1': (0.0, 0.8),
     'L0_ffn_b2': (0.0, 0.588),
     'L1_attn_fc1_b': (0.0, 0.8),
     'L1_attn_convA_b': (0.0, 0.8),
     'L1_attn_convB_b': (0.0, 0.8),
     'L1_attn_qkv_b': (0.0, 0.8),
     'L1_attn_proj_b': (0.0, 0.789),
     'L1_attn_fc2_b': (0.0, 0.1),
     'L1_ffn_norm_w': (1.0, 0.6)}
    factors = {'L0_tok_pos_embed': 2.759,
     'L0_attn_Wq': 8.0,
     'L0_attn_Wk': 8.0,
     'L0_attn_Wv': 3.066,
     'L0_attn_Wo': 3.214,
     'L0_attn_Wg': 8.0,
     'L0_ffn_phi': 8.0,
     'L0_ffn_w1': 8.0,
     'L0_ffn_w2': 8.0,
     'L1_attn_fc1_w': 8.0,
     'L1_attn_convA_w': 8.0,
     'L1_attn_convB_w': 8.0,
     'L1_attn_qkv_w': 8.0,
     'L1_attn_rpb': 8.0,
     'L1_attn_proj_w': 8.0,
     'L1_attn_fc2_w': 4.572,
     'L1_ffn_w13': 8.0,
     'L1_ffn_w2': 8.0}
    for name, (base, spread) in spreads.items():
        noise = np.random.default_rng([zlib.crc32(name.encode()), seed]).standard_normal(out[name].shape)
        drawn = base * np.exp(spread * noise) if base else spread * noise
        out[name] = jnp.asarray(drawn.astype(out[name].dtype))
    for name, factor in factors.items():
        out[name] = (out[name] * factor).astype(out[name].dtype)
    return out
```

```python
from contextlib import ExitStack

import concourse.bass as bass
from concourse import mybir
from concourse.alu_op_type import AluOpType as ALU
import numpy as np

ACT = mybir.ActivationFunctionType
AX = mybir.AxisListType
F32 = mybir.dt.float32
I32 = mybir.dt.int32

B, C_IN, IMG, PATCH = 64, 3, 96, 16
NP_ = (IMG // PATCH) ** 2
S = NP_ + 1
PD = C_IN * PATCH * PATCH
ED = 192
HALF = ED // 2
GB = 3
TP = GB * S
T = 22
NROW = T * TP
KC = PD // 128
NH, DH = 4, 64
NE, HID = 64, 768
HB = HID // 128
NPAIR = NE // 2
RING = 4
QKW = 2 * NH * DH
VGW = NH * DH + ED
WN, CONV, NHN = 96, 64, 4
DN = WN // NHN
WIN = 5
KR = GB + WIN - 1
KW = KR * S
PADR = WIN // 2
XCOLS = (T * GB + 2 * PADR) * S
VT = T + 4
EX, EH = 8, 512
CAP = int(np.ceil(1.25 * 2 * B * S / EX))
SJ = 6
SP_ = -(-CAP // SJ)
HS = SJ * SP_ // 2
CAPP = SJ * SP_
SKIP = 1.0e6

PACK_A = [("ident", 128, 128), ("g1", 128, KC), ("b1", 128, KC), ("wtok", 128, KC * ED),
          ("btok", TP, ED), ("g2m", TP, ED), ("b2m", TP, ED), ("pos", TP, ED), ("cls", TP, ED)]

PACK_B = [("wqk", HALF, 2 * QKW), ("wvg", HALF, 2 * VGW), ("wo", 128, 2 * ED), ("causal", TP, 2 * TP),
          ("phi", HALF, 2 * NE), ("scale", HALF, 1), ("image", TP, GB), ("b2r", 128, ED), ("b1s", 128, NE * HB),
          ("ones", 128, 128)]

PACK_C = [("fc1", HALF, 2 * WN), ("conva", WN, CONV), ("convb", CONV, WN), ("wq", WN, WN), ("wk", WN, WN),
          ("wv", WN, WN), ("proj", WN, WN), ("fc2", WN, ED), ("bv", TP, WN), ("bfc2", TP, ED),
          ("bfc1", WN, 1), ("bconva", CONV, 1), ("bconvb", WN, 1), ("bq", WN, 1), ("bk", WN, 1), ("bproj", WN, 1),
          ("head", WN, NHN), ("router", HALF, 2 * EX), ("before", TP, TP), ("index", TP, EX), ("real", TP, T), ("ones", TP, TP),
          ("gain", HALF, 2 * EX)]


def columns(pack):
    at, off = {}, 0
    for name, rows, cols in pack:
        at[name] = (rows, off, cols)
        off += cols
    return at, off


def after(t, k):
    return not isinstance(t, int) or t >= k


def over_tiles(eng, stages, n, unroll=2, tail=0):
    lags = max(lag for lag, _ in stages)
    head = -(-(lags + 2) // unroll) * unroll
    stop = head + (n - tail - head) // unroll * unroll

    def turn(s):
        for lag, step in stages:
            if 0 <= s - lag < n:
                step(s - lag, (s - lag) % unroll)

    for s in range(head):
        turn(s)
    with eng.Fori(head, stop - unroll + 1, unroll) as i:
        for u in range(unroll):
            for lag, step in stages:
                step(i + (u - lag), (u - lag) % unroll)
    for s in range(stop, n + lags):
        turn(s)


def tower(nc, ins, rows_out):
    with ExitStack() as ctx:
        scope = [ctx]

        def sb(name, shape, dt=F32):
            return scope[-1].enter_context(nc.sbuf_tensor(name, shape, dt))

        def open_scope():
            scope.append(ExitStack())

        def close_scope():
            scope.pop().close()

        def sem(name):
            return ctx.enter_context(nc.semaphore(name))

        bank = [ctx.enter_context(nc.psum_tensor(f"bank{i}", [128, 512], F32)) for i in range(8)]

        h = sb("h", [TP, T, ED])
        colA, nA = columns(PACK_A)
        ca = sb("ca", [128, nA])

        def of(pack, at, name):
            rows, off, cols = at[name]
            return pack[0:rows, off:off + cols]

        A = {name: of(ca, colA, name) for name in colA}
        ident = A["ident"]
        wtok = A["wtok"].rearrange("p (k e) -> p k e", k=KC)
        eps5 = sb("eps5", [128, 1])

        tick = sb("tick", [TP, 8])
        act_tick = sb("act_tick", [128, 1])
        hst = sb("hst", [TP, T, 6])
        hmean = sb("hmean", [TP, T])
        hvar = sb("hvar", [TP, T])
        hdif = sb("hdif", [TP, T])
        hsd = sb("hsd", [TP, T])
        hrs = sb("hrs", [TP, T])
        hn = [sb(f"hn{b}", [TP, ED]) for b in range(2)]
        hnT = [sb(f"hnT{b}", [HALF, 2, TP]) for b in range(2)]

        colC, nC = columns(PACK_C)
        cc = sb("cc", [128, nC])
        Cc = {name: of(cc, colC, name) for name in colC}

        open_scope()
        colB, nB = columns(PACK_B)
        cb = sb("cb", [128, nB])
        Bc = {name: of(cb, colB, name) for name in colB}
        wqk = Bc["wqk"].rearrange("p (c n) -> p c n", c=2)
        wvg = Bc["wvg"].rearrange("p (c n) -> p c n", c=2)
        wo = Bc["wo"].rearrange("p (c n) -> p c n", c=2)
        causal = Bc["causal"].rearrange("p (c n) -> p c n", c=2)
        xy = sb("xy", [HALF, 2, NE, T * GB])
        phisq = sb("phisq", [HALF, 2, NE])
        ce = sb("ce", [TP, T, NE])
        image = Bc["image"]
        w1s = [sb(f"w1s{q}", [HALF, 2, 2, HID]) for q in range(RING // 2)]
        w2s = [sb(f"w2s{q}", [128, 2, HB, ED]) for q in range(RING // 2)]
        b1s = Bc["b1s"].rearrange("p (n j) -> p n j", n=NE)

        open_scope()
        xt = [sb(f"xt{b}", [TP, PD]) for b in range(2)]
        xh = [sb(f"xh{b}", [TP, PD]) for b in range(2)]
        xhT = [sb(f"xhT{b}", [128, KC, TP]) for b in range(2)]
        wtok_g = sb("wtok_g", [128, KC, ED])
        tok_bias = sb("tok_bias", [TP, ED])
        pos_bias = sb("pos_bias", [TP, ED])
        xst = [sb(f"xst{b}", [TP, 2, 6]) for b in range(2)]
        xmv = [sb(f"xmv{b}", [TP, 2]) for b in range(2)]
        xsd = [sb(f"xsd{b}", [TP, 1]) for b in range(2)]
        xrs = [sb(f"xrs{b}", [TP, 1]) for b in range(2)]
        y = [sb(f"y{b}", [TP, ED]) for b in range(2)]
        yn = [sb(f"yn{b}", [TP, ED]) for b in range(2)]
        yst = [sb(f"yst{b}", [TP, 6]) for b in range(2)]
        ymv = [sb(f"ymv{b}", [TP, 2]) for b in range(2)]
        ysd = [sb(f"ysd{b}", [TP, 1]) for b in range(2)]
        yrs = [sb(f"yrs{b}", [TP, 1]) for b in range(2)]
        close_scope()

        open_scope()
        gate = sb("gate", [TP, T, ED])
        fe = [sb(f"fe{b}", [128, 4, TP]) for b in range(2)]
        fr = [sb(f"fr{b}", [128, 4, TP]) for b in range(2)]
        qk = [sb(f"qk{b}", [128, 4, TP]) for b in range(2)]
        vx = [sb(f"vx{b}", [TP, NH, DH + 1]) for b in range(2)]
        am = [sb(f"am{b}", [TP, NH, TP]) for b in range(2)]
        den = [sb(f"den{b}", [TP, NH]) for b in range(2)]
        rden = [sb(f"rden{b}", [TP, NH]) for b in range(2)]
        on = [sb(f"on{b}", [TP, NH, DH]) for b in range(2)]
        oT = [sb(f"oT{b}", [128, 2, TP]) for b in range(2)]
        rg = [sb(f"rg{b}", [TP, ED]) for b in range(2)]
        close_scope()

        open_scope()
        phin = sb("phin", [HALF, 2, NE])
        phinv = sb("phinv", [HALF, NE])
        hnorm = sb("hnorm", [TP, T])
        xn = [sb(f"xn{q}", [TP, ED]) for q in range(4)]
        cneg = [sb(f"cneg{b}", [TP, 1]) for b in range(2)]
        cexp = [sb(f"cexp{b}", [TP, NE]) for b in range(2)]
        csum = [sb(f"csum{b}", [TP, 1]) for b in range(2)]
        crec = [sb(f"crec{b}", [TP, 1]) for b in range(2)]
        dmax = [sb(f"dmax{b}", [NE, GB]) for b in range(2)]
        dlog = [sb(f"dlog{b}", [NE, GB, S]) for b in range(2)]
        dexp = [sb(f"dexp{b}", [NE, GB, S]) for b in range(2)]
        dsum = [sb(f"dsum{b}", [NE, GB]) for b in range(2)]
        drec = [sb(f"drec{b}", [NE, GB]) for b in range(2)]
        dT = [sb(f"dT{b}", [128, GB, S]) for b in range(2)]
        dw = [sb(f"dw{b}", [TP, GB, NE]) for b in range(2)]

        w1s += [sb(f"w1s{q}", [HALF, 2, 2, HID]) for q in range(RING // 2, RING)]
        w2s += [sb(f"w2s{q}", [128, 2, HB, ED]) for q in range(RING // 2, RING)]
        xs = [sb(f"xs{b}", [HALF, 2, 2, B]) for b in range(2)]
        eh = [sb(f"eh{b}", [128, HB, 128]) for b in range(2)]
        eg = [sb(f"eg{b}", [128, HB, 2, B]) for b in range(2)]
        eo = [sb(f"eo{b}", [128, ED]) for b in range(2)]

        cw = [sb(f"cw{b}", [TP, GB, NE]) for b in range(2)]
        e1 = [sb(f"e1{q}", [128, ED]) for q in range(4)]
        e2 = [sb(f"e2{q}", [NE, ED]) for q in range(4)]
        c1 = [sb(f"c1{b}", [128, TP]) for b in range(2)]
        c2 = [sb(f"c2{b}", [NE, TP]) for b in range(2)]
        close_scope()
        close_scope()

        open_scope()
        zero = sb("zero", [SP_, SJ * ED])
        w13 = [sb(f"w13{b}", [HALF, 2, 2 * EH]) for b in range(2)]
        w2r = [sb(f"w2r{b}", [128, EH // 128, ED]) for b in range(2)]

        open_scope()
        masks = sb("masks", [TP, 4, KW])
        near = [sb(f"near{v}", [TP, NHN, KW]) for v in range(2)]
        bias = [sb(f"bias{v}", [TP, NHN, KW]) for v in range(4)]
        xg = sb("xg", [WN, XCOLS])
        kT = sb("kT", [WN, XCOLS])
        vn = sb("vn", [TP, VT, NHN, DN + 1])
        fx = [sb(f"fx{q}", [WN, TP]) for q in range(4)]
        fa = [sb(f"fa{b}", [CONV, TP]) for b in range(2)]
        fs = [sb(f"fs{b}", [WN, TP]) for b in range(2)]
        vsrc = [sb(f"vsrc{b}", [WN, TP]) for b in range(2)]
        qx = [sb(f"qx{b}", [WN, NHN, TP]) for b in range(2)]
        nl = [sb(f"nl{b}", [TP, NHN, KW]) for b in range(2)]
        nm = [sb(f"nm{b}", [TP, NHN]) for b in range(2)]
        nn = [sb(f"nn{b}", [TP, NHN]) for b in range(2)]
        pTa = [sb(f"pTa{b}", [TP, NHN, 2, TP]) for b in range(2)]
        pTb = [sb(f"pTb{b}", [S, NHN, TP]) for b in range(2)]
        nr = [sb(f"nr{b}", [TP, NHN]) for b in range(2)]
        no = [sb(f"no{b}", [TP, NHN, DN]) for b in range(2)]
        noT = [sb(f"noT{b}", [WN, TP]) for b in range(2)]
        nz = [sb(f"nz{b}", [WN, TP]) for b in range(2)]
        h2 = [sb(f"h2{b}", [TP, ED]) for b in range(2)]
        close_scope()

        open_scope()
        zk = sb("zk", [TP, T, ED])
        zsq = sb("zsq", [TP, T])
        zrt = sb("zrt", [TP, T])
        zs = sb("zs", [TP, T])
        eps6 = sb("eps6", [TP, 1])
        top = sb("top", [TP, 2, T])
        eq = sb("eq", [TP, T, EX])
        key = sb("key", [TP, T, EX])
        lg2 = sb("lg2", [TP, T, EX])
        expert = sb("expert", [TP, 2, T])
        hot = sb("hot", [TP, 2, T, EX])
        hots = sb("hots", [TP, T, EX])
        sums = [sb(f"sums{b}", [TP, T, EX]) for b in range(2)]
        place = sb("place", [TP, T, EX])
        picked = sb("picked", [TP, 2, T, EX])
        pk = sb("pk", [TP, 2, T])
        kept = sb("kept", [TP, 2, T])
        slot = sb("slot", [TP, 2, T])
        away = sb("away", [TP, 2, T])
        last_slot = sb("last_slot", [TP, 2, T])
        to = sb("to", [TP, 2, T], I32)
        frm = sb("frm", [TP, 2, T], I32)
        wexp = sb("wexp", [TP, T])
        wdif = sb("wdif", [TP, T])
        wsum = sb("wsum", [TP, T])
        wts = sb("wts", [TP, 2, T])
        own = sb("own", [TP, 2, T])
        zr = [sb(f"zr{b}", [SP_, SJ, ED]) for b in range(2)]
        zT = [sb(f"zT{b}", [HALF, 2, CAPP]) for b in range(2)]
        sg = [sb(f"sg{b}", [128, CAPP // 2]) for b in range(2)]
        hT = sb("hT", [128, EH // 128, CAPP])
        yr = [sb(f"yr{b}", [SP_, SJ, ED]) for b in range(2)]
        back = [[sb(f"back{k}{q}", [TP, ED]) for q in range(4)] for k in range(2)]
        acc = [sb(f"acc{b}", [TP, ED]) for b in range(2)]
        close_scope()
        close_scope()

        ys = nc.dram_tensor("ys", [NPAIR, 2 * B, ED], F32, kind="Internal").ap()
        ys_of = ys.rearrange("p (e m) d -> (p e) m d", e=2)

        buf = nc.dram_tensor("buf", [EX * CAPP, ED], F32, kind="Internal").ap()
        ybuf = nc.dram_tensor("ybuf", [EX * CAPP, ED], F32, kind="Internal").ap()

        buf_of = buf.rearrange("(e p j) d -> e p (j d)", e=EX, p=SP_)
        ybuf_of = ybuf.rearrange("(e p j) d -> e p (j d)", e=EX, p=SP_)

        s_cci = sem("constants_c_in")
        s_bz = sem("buffer_zeroed")
        s_nin = sem("near_tables_in")
        s_nb = sem("near_biases_ready")
        s_pad = sem("near_padding_set")
        s_f1 = sem("fc1_product")
        s_f1c = sem("fc1_biased")
        s_fA = sem("conva_product")
        s_fAc = sem("conva_biased")
        s_fB = sem("convb_product")
        s_fs = sem("convb_biased_summed")
        s_fg = sem("near_gelu")
        s_fK = sem("key_product")
        s_fKc = sem("keys_stored")
        s_fv = sem("value_source_copied")
        s_fV = sem("value_product")
        s_fVc = sem("values_stored")
        s_nQ = sem("query_product")
        s_nq = sem("queries_spread")
        s_nS = sem("near_scores")
        s_nl = sem("near_logits")
        s_nm = sem("near_maxima_negated")
        s_ne = sem("near_exp")
        s_nT = sem("near_weights_transposed")
        s_nTa = sem("near_wT_copied_act")
        s_nTd = sem("near_wT_copied_dve")
        s_nA = sem("near_av")
        s_nr = sem("near_reciprocal")
        s_no = sem("near_out_normalized")
        s_noT = sem("near_out_transposed")
        s_noc = sem("near_oT_copied")
        s_nP = sem("near_projected")
        s_nz = sem("near_projection_biased")
        s_nF = sem("fc2_product")
        s_ha = sem("h_plus_normalized")
        s_nh2 = sem("h_plus_fc2_bias")
        s_w13 = [sem(f"w13_in{b}") for b in range(2)]
        s_w2r = [sem(f"w2r_in{b}") for b in range(2)]
        s_gz = sem("z_stored")
        s_gl = sem("router_logits")
        s_r = sem("routing_steps")
        s_re = sem("routing_exp")
        s_rt = sem("routing_results")
        s_rp = sem("routing_prefix_product")
        s_sc = sem("rows_scattered")
        s_zr = [sem(f"slot_rows_in{b}") for b in range(2)]
        s_zT = sem("slot_rows_transposed")
        s_zc = [sem("zT_stored_act"), sem("zT_stored_dve")]
        s_gu = sem("gate_up_product")
        s_sg = sem("gate_silu")
        s_hT = sem("hidden_stored")
        s_yp = sem("routed_output_product")
        s_yc = [sem("routed_output_copied_act"), sem("routed_output_copied_dve")]
        s_eo = [sem(f"expert_output_out{b}") for b in range(2)]
        n_eo = 16 * NPAIR // 2
        s_g = [sem(f"rows_gathered{q}") for q in range(4)]
        s_o1 = sem("output_steps")
        s_o = sem("output_ready")

        s_ph = sem("norm_constants_steps")
        s_phn = sem("phi_norms")
        s_phs = sem("phi_norm_roots")
        s_cns = sem("dispatch_norm_roots")
        s_cl = sem("dispatch_logits")
        s_ccm = sem("combine_max")
        s_cce = sem("combine_exp")
        s_ccr = sem("combine_reciprocal")
        s_ccw = sem("combine_weights")
        s_cdm = sem("dispatch_max")
        s_cdl = sem("dispatch_shifted")
        s_cde = sem("dispatch_exp")
        s_cds = sem("dispatch_sum_steps")
        s_cdT = sem("dispatch_weights_T")
        s_cdt = sem("dispatch_weights_transposed")
        s_cdw = sem("dispatch_weights_spread")
        s_cxs = sem("expert_input_product")
        s_cxc = sem("expert_input_stored")
        s_w1 = [sem(f"w1_in_then_expert_rows_in{q}") for q in range(RING)]
        n_w1 = 16 * NPAIR // RING
        s_w2 = [sem(f"w2_in{q}") for q in range(RING)]
        s_dx = sem("expert_inputs_staged")
        s_dh = sem("expert_hidden_product")
        s_dc = [sem("expert_hidden_copied_act"), sem("expert_hidden_copied_dve")]
        s_dt = sem("expert_hidden_transposed")
        s_db = sem("expert_hidden_biased")
        s_dg = sem("expert_hidden_gelu")
        s_dy = sem("expert_output_product")
        s_do = sem("expert_output_stored")
        s_eb = sem("expert_outputs_biased")
        s_ecw = sem("combine_weights_spread")
        s_eT = sem("combine_transposed")
        s_eTa = sem("combine_copied_act")
        s_eTd = sem("combine_copied_dve")
        s_ey = sem("combine_product")

        s_ln = sem("ln_constants_steps")
        s_cbi = sem("constants_b_in")
        s_hst = sem("h_stats")
        s_hsd = sem("h_std")
        s_b1 = sem("vx_ones_set")
        s_hn = sem("h_normalized")
        s_hTr = sem("h_transposed")
        s_hTc = sem("hT_copied")
        s_bqk = sem("attn_qk_product")
        s_bvg = sem("attn_vg_product")
        s_bf = sem("attn_exp_relu")
        s_bq = sem("attn_qk_features")
        s_bv = sem("attn_v_gate")
        s_bs = sem("attn_scores")
        s_bam = sem("attn_scores_masked")
        s_bav = sem("attn_av")
        s_bd = sem("attn_den_steps")
        s_bon = sem("attn_out_normalized")
        s_boT = sem("attn_out_transposed")
        s_boc = sem("attn_oT_copied")
        s_bwo = sem("attn_projected")
        s_brg = sem("attn_gated")

        s_ca = sem("constants_a_in")
        s_eps = sem("eps_set")
        s_wg = sem("wtok_scaled")
        s_cb = sem("tok_bias_product")
        s_tb = sem("tok_bias_ready")
        s_pb = sem("pos_bias_ready")
        s_x = [sem(f"x_in_then_output_out{b}") for b in range(2)]
        n_x = 16 * T // 2
        s_xst = sem("x_stats")
        s_xmv = sem("x_mean_var")
        s_xsd = sem("x_std")
        s_xrs = sem("x_rstd")
        s_xh = sem("x_normalized")
        s_xT = sem("x_transposed")
        s_xTa = sem("xT_copied_act")
        s_xTd = sem("xT_copied_dve")
        s_typ = sem("y_product")
        s_y = sem("y_biased")
        s_yst = sem("y_stats")
        s_ymv = sem("y_mean_var")
        s_ysd = sem("y_std")
        s_yrs = sem("y_rstd")
        s_yn = sem("y_normalized")
        s_yg = sem("y_gained")
        s_h = sem("h_updated")

        def embed_sp(sp):
            sp.dma_start(ca[:], ins["ca"]).then_inc(s_ca, 16)
            sp.dma_start(cb[:], ins["cb"]).then_inc(s_cbi, 16)
            sp.dma_start(cc[:], ins["cc"]).then_inc(s_cci, 16)

            def load_x(t, b):
                if after(t, 2):
                    sp.wait_ge(s_xh, t - 1)
                sp.dma_start(xt[b][:], ins["x"][t]).then_inc(s_x[b], 16)

            over_tiles(sp, [(0, load_x)], T)

        def embed_pool(pool):
            nc.gpsimd.memset(eps5[:], 1e-5).then_inc(s_eps, 1)

            def gain(t, b):
                pool.wait_ge(s_yn, t + 1)
                pool.wait_ge(s_pb, 2)
                nc.gpsimd.tensor_tensor(yn[b][:], yn[b][:], A["g2m"], ALU.mult).then_inc(s_yg, 1)
                pool.wait_ge(s_yg, t + 1)
                nc.gpsimd.tensor_tensor(h[:, t, :], yn[b][:], pos_bias[:], ALU.add).then_inc(s_h, 1)

            over_tiles(pool, [(0, gain)], T)
            for b in range(2):
                nc.gpsimd.memset(vx[b][:, :, DH:DH + 1], 1.0).then_inc(s_b1, 1)

        def h_std(act, layer):
            act.wait_ge(s_ln, 5 * layer + 4)
            nc.scalar.activation(hsd[:], hvar[:], ACT.Sqrt, bias=eps5[0:TP, :]).then_inc(s_hsd, 1)

        def h_norm_constants(dve, layer):
            n0 = 5 * layer
            dve.wait_ge(s_hst, T * (layer + 1))
            nc.vector.tensor_tensor(hmean[:], hst[:, :, 1], hst[:, :, 4], ALU.add)
            nc.vector.tensor_tensor(hdif[:], hst[:, :, 1], hst[:, :, 4], ALU.subtract)
            nc.vector.tensor_tensor(hvar[:], hst[:, :, 2], hst[:, :, 5], ALU.add).then_inc(s_ln, 1)
            dve.wait_ge(s_ln, n0 + 1)
            nc.vector.tensor_scalar(hmean[:], hmean[:], 0.5, None, ALU.mult)
            nc.vector.tensor_scalar(hvar[:], hvar[:], 1.0 / ED, None, ALU.mult)
            nc.vector.scalar_tensor_tensor(out=hdif[:], in0=hdif[:], scalar=0.25, in1=hdif[:], op0=ALU.mult, op1=ALU.mult).then_inc(s_ln, 2)
            dve.wait_ge(s_ln, n0 + 3)
            nc.vector.tensor_tensor(hvar[:], hvar[:], hdif[:], ALU.add).then_inc(s_ln, 1)
            dve.wait_ge(s_hsd, layer + 1)
            nc.vector.reciprocal(hrs[:], hsd[:]).then_inc(s_ln, 1)

        def attention_act(act):
            h_std(act, 0)

            def copy_hT(t, b):
                act.wait_ge(s_hTr, t + 1)
                if after(t, 2):
                    act.wait_ge(s_bvg, t - 1)
                nc.scalar.copy(hnT[b][:], bank[0][0:HALF, 0:2 * TP].rearrange("p (c q) -> p c q", c=2)).then_inc(s_hTc, 1)

            def features(t, b):
                act.wait_ge(s_bqk, t + 1)
                if after(t, 2):
                    act.wait_ge(s_bq, t - 1)
                p = bank[1][:, 0:4 * TP].rearrange("p (c q) -> p c q", c=4)
                nc.scalar.activation(fe[b][:], p, ACT.Exp)
                nc.scalar.activation(fr[b][:], p, ACT.Relu).then_inc(s_bf, 1)

            def values(t, b):
                act.wait_ge(s_bvg, t + 1)
                if after(t, 2):
                    act.wait_ge(s_bav, t - 1)
                else:
                    act.wait_ge(s_b1, 2)
                nc.scalar.activation(gate[:, t, :], bank[2][0:TP, NH * DH:VGW], ACT.Tanh, scale=0.5)
                nc.scalar.copy(vx[b][:, :, 0:DH], bank[2][0:TP, 0:NH * DH].rearrange("p (h d) -> p h d", h=NH)).then_inc(s_bv, 1)

            def copy_oT(t, b):
                act.wait_ge(s_boT, t + 1)
                if after(t, 2):
                    act.wait_ge(s_bwo, t - 1)
                nc.scalar.copy(oT[b][:], bank[6][:, 0:2 * TP].rearrange("p (c q) -> p c q", c=2)).then_inc(s_boc, 1)

            over_tiles(act, [(0, copy_hT), (3, copy_oT), (1, features), (1, values)], T)

        def embed_act(act):
            act.wait_ge(s_eps, 1)

            def std_x(t, b):
                act.wait_ge(s_xmv, t + 1)
                if after(t, 2):
                    act.wait_ge(s_xrs, t - 1)
                nc.scalar.activation(xsd[b][:], xmv[b][:, 1:2], ACT.Sqrt, bias=eps5[0:TP, :]).then_inc(s_xsd, 1)

            def copy_xT(t, b):
                act.wait_ge(s_xT, 2 * t + 1)
                if after(t, 2):
                    act.wait_ge(s_typ, t - 1)
                nc.scalar.copy(xhT[b][:, 0:3, :], bank[0][:, 0:3 * TP].rearrange("p (k q) -> p k q", k=3)).then_inc(s_xTa, 1)

            def std_y(t, b):
                act.wait_ge(s_ymv, t + 1)
                if after(t, 2):
                    act.wait_ge(s_yrs, t - 1)
                nc.scalar.activation(ysd[b][:], ymv[b][:, 1:2], ACT.Sqrt, bias=eps5[0:TP, :]).then_inc(s_ysd, 1)

            over_tiles(act, [(0, std_x), (2, copy_xT), (3, std_y)], T)

        def embed_dve(dve):
            dve.wait_ge(s_ca, 16)
            for k in range(KC):
                last = nc.vector.tensor_scalar(wtok_g[:, k, :], wtok[:, k, :], A["g1"][:, k:k + 1], None, ALU.mult)
            last.then_inc(s_wg, 1)
            nc.vector.tensor_tensor(pos_bias[:], A["pos"], A["b2m"], ALU.add).then_inc(s_pb, 1)
            dve.wait_ge(s_pb, 1)
            nc.vector.tensor_tensor(pos_bias[:], pos_bias[:], A["cls"], ALU.add).then_inc(s_pb, 1)
            dve.wait_ge(s_cb, 1)
            nc.vector.tensor_tensor(tok_bias[:], A["btok"], bank[7][0:TP, 0:ED], ALU.add).then_inc(s_tb, 1)

            def stats_x(t, b):
                dve.wait_ge(s_x[b], (t - b) * 8 + 16)
                if after(t, 2):
                    dve.wait_ge(s_xmv, t - 1)
                nc.vector.bn_stats(xst[b][:, 0, :], xt[b][:, 0:PD // 2])
                nc.vector.bn_stats(xst[b][:, 1, :], xt[b][:, PD // 2:PD]).then_inc(s_xst, 1)
                dve.wait_ge(s_xst, t + 1)
                nc.vector.memset(tick[:, 4:5], 0.0)
                nc.vector.bn_aggr(xmv[b][:], xst[b][:]).then_inc(s_xmv, 1)

            def norm_x(t, b):
                dve.wait_ge(s_xsd, t + 1)
                nc.vector.reciprocal(xrs[b][:], xsd[b][:]).then_inc(s_xrs, 1)
                dve.wait_ge(s_xrs, t + 1)
                if after(t, 2):
                    dve.wait_ge(s_xT, 2 * t - 2)
                nc.vector.tensor_scalar(xh[b][:], xt[b][:], xmv[b][:, 0:1], xrs[b][:], ALU.subtract, ALU.mult).then_inc(s_xh, 1)

            def copy_xT(t, b):
                dve.wait_ge(s_xT, 2 * t + 2)
                if after(t, 2):
                    dve.wait_ge(s_typ, t - 1)
                nc.vector.tensor_copy(xhT[b][:, 3:6, :], bank[1][:, 0:3 * TP].rearrange("p (k q) -> p k q", k=3)).then_inc(s_xTd, 1)

            def bias_y(t, b):
                dve.wait_ge(s_typ, t + 1)
                dve.wait_ge(s_tb, 1)
                if after(t, 2):
                    dve.wait_ge(s_yn, t - 1)
                nc.vector.tensor_tensor(y[b][:], bank[2 + b][0:TP, 0:ED], tok_bias[:], ALU.add).then_inc(s_y, 1)
                dve.wait_ge(s_y, t + 1)
                nc.vector.bn_stats(yst[b][:], y[b][:]).then_inc(s_yst, 1)
                dve.wait_ge(s_yst, t + 1)
                nc.vector.memset(tick[:, 5:6], 0.0)
                nc.vector.bn_aggr(ymv[b][:], yst[b][:]).then_inc(s_ymv, 1)

            def norm_y(t, b):
                dve.wait_ge(s_ysd, t + 1)
                nc.vector.reciprocal(yrs[b][:], ysd[b][:]).then_inc(s_yrs, 1)
                dve.wait_ge(s_yrs, t + 1)
                if after(t, 2):
                    dve.wait_ge(s_h, t - 1)
                nc.vector.tensor_scalar(yn[b][:], y[b][:], ymv[b][:, 0:1], yrs[b][:], ALU.subtract, ALU.mult).then_inc(s_yn, 1)

            def stats_h(t, b):
                dve.wait_ge(s_h, t + 1)
                nc.vector.bn_stats(hst[:, t, :], h[:, t, :]).then_inc(s_hst, 1)

            over_tiles(dve, [(0, stats_x), (1, norm_x), (2, copy_xT), (3, bias_y), (4, norm_y), (5, stats_h)], T)

        def attention_dve(dve):
            h_norm_constants(dve, 0)
            dve.wait_ge(s_ln, 5)
            dve.wait_ge(s_cbi, 16)
            phi = Bc["phi"].rearrange("p (c n) -> p c n", c=2)
            nc.vector.tensor_tensor(phisq[:], phi, phi, ALU.mult).then_inc(s_ph, 1)

            def normalize(t, b):
                if after(t, 2):
                    dve.wait_ge(s_hTr, t - 1)
                nc.vector.tensor_scalar(hn[b][:], h[:, t, :], hmean[:, bass.ds(t, 1)], hrs[:, bass.ds(t, 1)], ALU.subtract, ALU.mult).then_inc(s_hn, 1)

            def feature(t, b):
                dve.wait_ge(s_bf, t + 1)
                if after(t, 2):
                    dve.wait_ge(s_bs, t - 1)
                nc.vector.scalar_tensor_tensor(out=qk[b][:], in0=fe[b][:], scalar=1.0, in1=fr[b][:], op0=ALU.min, op1=ALU.add).then_inc(s_bq, 1)

            def mask(t, b):
                dve.wait_ge(s_bs, t + 1)
                if after(t, 2):
                    dve.wait_ge(s_bav, t - 1)
                for half in range(2):
                    last = nc.vector.tensor_tensor(am[b][:, 2 * half:2 * half + 2, :], bank[3 + half][0:TP, 0:2 * TP].rearrange("p (c q) -> p c q", c=2), causal, ALU.mult)
                last.then_inc(s_bam, 1)

            def normalize_out(t, b):
                p = bank[5][0:TP, 0:NH * (DH + 1)].rearrange("p (h d) -> p h d", h=NH)
                dve.wait_ge(s_bav, t + 1)
                nc.vector.tensor_scalar(den[b][:], p[:, :, DH], 1e-6, None, ALU.max).then_inc(s_bd, 1)
                dve.wait_ge(s_bd, 2 * t + 1)
                nc.vector.reciprocal(rden[b][:], den[b][:]).then_inc(s_bd, 1)
                dve.wait_ge(s_bd, 2 * t + 2)
                if after(t, 2):
                    dve.wait_ge(s_boT, t - 1)
                nc.vector.tensor_tensor(on[b][:], p[:, :, 0:DH], rden[b][:].unsqueeze(2).to_broadcast([TP, NH, DH]), ALU.mult).then_inc(s_bon, 1)

            def residual(t, b):
                dve.wait_ge(s_bwo, t + 1)
                nc.vector.scalar_tensor_tensor(out=rg[b][:], in0=gate[:, t, :], scalar=1.0, in1=bank[7][0:TP, 0:ED], op0=ALU.add, op1=ALU.mult).then_inc(s_brg, 1)
                dve.wait_ge(s_brg, t + 1)
                nc.vector.scalar_tensor_tensor(out=h[:, t, :], in0=rg[b][:], scalar=0.5, in1=h[:, t, :], op0=ALU.mult, op1=ALU.add).then_inc(s_h, 1)
                dve.wait_ge(s_h, T + t + 1)
                nc.vector.bn_stats(hst[:, t, :], h[:, t, :]).then_inc(s_hst, 1)

            over_tiles(dve, [(0, normalize), (3, normalize_out), (2, mask), (1, feature), (3, residual)], T)

        def embed_pe(pe):
            pe.wait_ge(s_ca, 16)
            for k in range(KC):
                last = nc.tensor.matmul(bank[7][0:TP, 0:ED], A["b1"][:, k:k + 1].to_broadcast([128, TP]), wtok[:, k, :],
                                        start=(k == 0), stop=(k == KC - 1))
            last.then_inc(s_cb, 1)
            pe.wait_ge(s_wg, 1)

            def transpose_x(t, b):
                pe.wait_ge(s_xh, t + 1)
                for half in range(2):
                    if after(t, 1):
                        pe.wait_ge(s_xTd if half else s_xTa, t)
                    for k in range(3):
                        last = nc.tensor.transpose(bank[half][:, k * TP:(k + 1) * TP], xh[b][:, (3 * half + k) * 128:(3 * half + k + 1) * 128], ident[0:TP, 0:TP])
                    last.then_inc(s_xT, 1)

            def product(t, b):
                pe.wait_ge(s_xTa, t + 1)
                pe.wait_ge(s_xTd, t + 1)
                if after(t, 2):
                    pe.wait_ge(s_y, t - 1)
                for k in range(KC):
                    last = nc.tensor.matmul(bank[2 + b][0:TP, 0:ED], xhT[b][:, k, :], wtok_g[:, k, :], start=(k == 0), stop=(k == KC - 1))
                last.then_inc(s_typ, 1)

            over_tiles(pe, [(1, transpose_x), (2, product)], T)

        def attention_pe(pe):
            pe.wait_ge(s_cbi, 16)

            def transpose_h(t, b):
                pe.wait_ge(s_hn, t + 1)
                if after(t, 1):
                    pe.wait_ge(s_hTc, t)
                for c in range(2):
                    last = nc.tensor.transpose(bank[0][0:HALF, c * TP:(c + 1) * TP], hn[b][:, c * HALF:(c + 1) * HALF], ident[0:TP, 0:TP])
                last.then_inc(s_hTr, 1)

            def products(t, b):
                pe.wait_ge(s_hTc, t + 1)
                if after(t, 1):
                    pe.wait_ge(s_bf, t)
                for j in range(4):
                    for c in range(2):
                        last = nc.tensor.matmul(bank[1][:, j * TP:(j + 1) * TP], wqk[:, c, j * 128:(j + 1) * 128], hnT[b][:, c, :], start=(c == 0), stop=(c == 1))
                last.then_inc(s_bqk, 1)
                if after(t, 1):
                    pe.wait_ge(s_bv, t)
                for c in range(2):
                    last = nc.tensor.matmul(bank[2][0:TP, 0:VGW], hnT[b][:, c, :], wvg[:, c, :], start=(c == 0), stop=(c == 1))
                last.then_inc(s_bvg, 1)

            def scores(t, b):
                pe.wait_ge(s_bq, t + 1)
                if after(t, 1):
                    pe.wait_ge(s_bam, t)
                for j in range(2):
                    for r in range(2):
                        last = nc.tensor.matmul(bank[3 + r][0:TP, j * TP:(j + 1) * TP], qk[b][64 * r:64 * r + 64, 2 + j, :], qk[b][64 * r:64 * r + 64, j, :], start=True, stop=True)
                last.then_inc(s_bs, 1)

            def values(t, b):
                pe.wait_ge(s_bam, t + 1)
                pe.wait_ge(s_bv, t + 1)
                if after(t, 1):
                    pe.wait_ge(s_bon, t)
                for head in range(NH):
                    last = nc.tensor.matmul(bank[5][0:TP, head * (DH + 1):(head + 1) * (DH + 1)], am[b][:, 2 * (head % 2) + head // 2, :], vx[b][:, head, :], start=True, stop=True)
                last.then_inc(s_bav, 1)

            def transpose_o(t, b):
                pe.wait_ge(s_bon, t + 1)
                if after(t, 1):
                    pe.wait_ge(s_boc, t)
                for j in range(2):
                    last = nc.tensor.transpose(bank[6][:, j * TP:(j + 1) * TP], on[b][:, 2 * j:2 * j + 2, :].rearrange("p h d -> p (h d)"), ident[0:TP, 0:TP])
                last.then_inc(s_boT, 1)

            def project(t, b):
                pe.wait_ge(s_boc, t + 1)
                if after(t, 1):
                    pe.wait_ge(s_brg, t)
                for j in range(2):
                    last = nc.tensor.matmul(bank[7][0:TP, 0:ED], oT[b][:, j, :], wo[:, j, :], start=(j == 0), stop=(j == 1))
                last.then_inc(s_bwo, 1)

            over_tiles(pe, [(0, transpose_h), (2, scores), (3, transpose_o), (1, products), (2, values), (3, project)], T)

        def dispatch_act(act):
            act.wait_ge(s_phn, 1)
            nc.scalar.activation(phinv[:], bank[7][0:HALF, 0:NE], ACT.Sqrt).then_inc(s_phs, 1)
            h_std(act, 1)
            act.wait_ge(s_ln, 5 + 4)
            nc.scalar.activation(hnorm[:], hvar[:], ACT.Sqrt, scale=float(ED)).then_inc(s_cns, 1)

            def copy_T(t, q):
                b = q % 2
                act.wait_ge(s_hTr, T + t + 1)
                if after(t, 2):
                    act.wait_ge(s_cl, t - 1)
                nc.scalar.copy(hnT[b][:], bank[0][0:HALF, 0:2 * TP].rearrange("p (c q) -> p c q", c=2)).then_inc(s_hTc, 1)

            def exps(t, q):
                b = q % 2
                act.wait_ge(s_ccm, t + 1)
                if after(t, 2):
                    act.wait_ge(s_ccw, t - 1)
                nc.scalar.activation(cexp[b][:], bank[1][0:TP, 0:NE], ACT.Exp, bias=cneg[b][:], accum_out=csum[b][:]).then_inc(s_cce, 1)
                act.wait_ge(s_cdl, t + 1)
                nc.scalar.activation(dexp[b][:], dlog[b][:], ACT.Exp).then_inc(s_cde, 1)

            def store(t, q):
                b = q % 2
                act.wait_ge(s_cxs, t + 1)
                p = bank[4][0:HALF, 0:2 * GB * NE].rearrange("p (c g n) -> p c g n", c=2, g=GB)
                for c in range(2):
                    last = nc.scalar.copy(xy[:, c, :, bass.ds(t * GB, GB)].rearrange("p n g -> p g n"), p[:, c])
                last.then_inc(s_cxc, 1)

            over_tiles(act, [(0, copy_T), (3, store), (1, exps)], T, unroll=4)

        def dispatch_dve(dve):
            dve.wait_ge(s_phs, 1)
            nc.vector.tensor_scalar(phinv[:], phinv[:], 1e-12, None, ALU.max).then_inc(s_ph, 1)
            dve.wait_ge(s_ph, 2)
            nc.vector.reciprocal(phinv[:], phinv[:]).then_inc(s_ph, 1)
            dve.wait_ge(s_ph, 3)
            nc.vector.tensor_scalar(phinv[:], phinv[:], Bc["scale"], None, ALU.mult).then_inc(s_ph, 1)
            dve.wait_ge(s_ph, 4)
            for b in range(2):
                nc.vector.memset(dT[b][NE:128], 0.0)
            nc.vector.tensor_tensor(phin[:], Bc["phi"].rearrange("p (c n) -> p c n", c=2), phinv[:].unsqueeze(1).to_broadcast([HALF, 2, NE]), ALU.mult).then_inc(s_ph, 1)
            h_norm_constants(dve, 1)
            dve.wait_ge(s_ln, 10)
            dve.wait_ge(s_cns, 1)
            nc.vector.tensor_tensor(hnorm[:], hnorm[:], hrs[:], ALU.mult).then_inc(s_ph, 1)
            dve.wait_ge(s_ph, 6)
            nc.vector.tensor_scalar(hnorm[:], hnorm[:], 1e-12, None, ALU.max).then_inc(s_ph, 1)
            dve.wait_ge(s_ph, 7)
            nc.vector.reciprocal(hnorm[:], hnorm[:]).then_inc(s_ph, 1)
            dve.wait_ge(s_ph, 8)
            nc.vector.tensor_tensor(hnorm[:], hnorm[:], hrs[:], ALU.mult).then_inc(s_ph, 1)
            dve.wait_ge(s_ph, 9)

            def normalize(t, q):
                b = q % 2
                if after(t, 4):
                    dve.wait_ge(s_cxs, t - 3)
                nc.vector.tensor_scalar(xn[q][:], h[:, t, :], hmean[:, bass.ds(t, 1)], hnorm[:, bass.ds(t, 1)], ALU.subtract, ALU.mult).then_inc(s_hn, 1)

            def maxima(t, q):
                b = q % 2
                dve.wait_ge(s_cl, t + 1)
                if after(t, 2):
                    dve.wait_ge(s_cce, t - 1)
                nc.vector.tensor_reduce(cneg[b][:], bank[1][0:TP, 0:NE], AX.X, ALU.max, negate=True).then_inc(s_ccm, 1)
                p = bank[2][0:NE, 0:TP].rearrange("p (g m) -> p g m", g=GB)
                nc.vector.tensor_reduce(dmax[b][:], p, AX.X, ALU.max).then_inc(s_cdm, 1)
                dve.wait_ge(s_cdm, t + 1)
                if after(t, 2):
                    dve.wait_ge(s_cde, t - 1)
                nc.vector.tensor_tensor(dlog[b][:], p, dmax[b][:].unsqueeze(2).to_broadcast([NE, GB, S]), ALU.subtract).then_inc(s_cdl, 1)

            def weights(t, q):
                b = q % 2
                dve.wait_ge(s_cce, t + 1)
                nc.vector.reciprocal(crec[b][:], csum[b][:]).then_inc(s_ccr, 1)
                dve.wait_ge(s_cde, t + 1)
                nc.vector.tensor_reduce(dsum[b][:], dexp[b][:], AX.X, ALU.add).then_inc(s_cds, 1)
                dve.wait_ge(s_ccr, t + 1)
                nc.vector.tensor_scalar(ce[:, t, :], cexp[b][:], crec[b][:], None, ALU.mult).then_inc(s_ccw, 1)
                dve.wait_ge(s_cds, 2 * t + 1)
                nc.vector.reciprocal(drec[b][:], dsum[b][:]).then_inc(s_cds, 1)
                dve.wait_ge(s_cds, 2 * t + 2)
                if after(t, 2):
                    dve.wait_ge(s_cdt, t - 1)
                nc.vector.tensor_tensor(dT[b][0:NE], dexp[b][:], drec[b][:].unsqueeze(2).to_broadcast([NE, GB, S]), ALU.mult).then_inc(s_cdT, 1)

            def spread(t, q):
                b = q % 2
                dve.wait_ge(s_cdt, t + 1)
                if after(t, 2):
                    dve.wait_ge(s_cxs, t - 1)
                nc.vector.tensor_tensor(dw[b][:], bank[3][0:TP, 0:NE].unsqueeze(1).to_broadcast([TP, GB, NE]), image.unsqueeze(2).to_broadcast([TP, GB, NE]), ALU.mult).then_inc(s_cdw, 1)

            over_tiles(dve, [(0, normalize), (2, spread), (1, maxima), (1, weights)], T, unroll=4)

        def dispatch_pe(pe):
            pe.wait_ge(s_ph, 1)
            pe.wait_ge(s_brg, T)
            for c in range(2):
                last = nc.tensor.matmul(bank[7][0:HALF, 0:NE], Bc["ones"][0:HALF, 0:HALF], phisq[:, c, :], start=(c == 0), stop=(c == 1))
            last.then_inc(s_phn, 1)
            pe.wait_ge(s_ph, 5)

            def transpose_x(t, q):
                b = q % 2
                pe.wait_ge(s_hn, T + t + 1)
                if after(t, 1):
                    pe.wait_ge(s_hTc, T + t)
                for c in range(2):
                    last = nc.tensor.transpose(bank[0][0:HALF, c * TP:(c + 1) * TP], xn[q][:, c * HALF:(c + 1) * HALF], ident[0:TP, 0:TP])
                last.then_inc(s_hTr, 1)

            def logits(t, q):
                b = q % 2
                pe.wait_ge(s_hTc, T + t + 1)
                if after(t, 1):
                    pe.wait_ge(s_cce, t)
                    pe.wait_ge(s_cdl, t)
                for c in range(2):
                    nc.tensor.matmul(bank[1][0:TP, 0:NE], hnT[b][:, c, :], phin[:, c, :], start=(c == 0), stop=(c == 1))
                for c in range(2):
                    last = nc.tensor.matmul(bank[2][0:NE, 0:TP], phin[:, c, :], hnT[b][:, c, :], start=(c == 0), stop=(c == 1))
                last.then_inc(s_cl, 1)

            def transpose_d(t, q):
                b = q % 2
                pe.wait_ge(s_cdT, t + 1)
                if after(t, 1):
                    pe.wait_ge(s_cdw, t)
                nc.tensor.transpose(bank[3][0:TP, 0:128], dT[b][:].rearrange("p g m -> p (g m)"), ident).then_inc(s_cdt, 1)

            def inputs(t, q):
                b = q % 2
                pe.wait_ge(s_cdw, t + 1)
                if after(t, 1):
                    pe.wait_ge(s_cxc, t)
                for c in range(2):
                    last = nc.tensor.matmul(bank[4][0:HALF, c * GB * NE:(c + 1) * GB * NE], xn[q][:, c * HALF:(c + 1) * HALF], dw[b][:].rearrange("p g n -> p (g n)"), start=True, stop=True)
                last.then_inc(s_cxs, 1)

            over_tiles(pe, [(0, transpose_x), (2, transpose_d), (1, logits), (2, inputs)], T, unroll=4)

        def experts_sp(sp):
            def load(p, q):
                if isinstance(p, int) and p == RING // 2:
                    sp.wait_ge(s_h, 2 * T)
                if after(p, RING):
                    sp.wait_ge(s_dh, p - RING + 1)
                sp.dma_start(w1s[q][:], ins["w1"][p]).then_inc(s_w1[q], 16)
                if after(p, RING):
                    sp.wait_ge(s_dy, p - RING + 1)
                sp.dma_start(w2s[q][:], ins["w2"][p]).then_inc(s_w2[q], 16)

            def store(p, q):
                b = q % 2
                sp.wait_ge(s_do, p + 1)
                sp.dma_start(ys[p], eo[b][:]).then_inc(s_eo[b], 16)

            over_tiles(sp, [(0, load), (RING, store)], NPAIR, unroll=RING)

        def experts_pool(pool):
            pool.wait_ge(s_cxc, T)

            def stage(p, q):
                b = q % 2
                if after(p, 2):
                    pool.wait_ge(s_dh, p - 1)
                nc.gpsimd.tensor_copy(xs[b][:], xy[:, :, bass.ds(2 * p, 2), 0:B]).then_inc(s_dx, 1)

            over_tiles(pool, [(0, stage)], NPAIR, unroll=RING)

        def experts_act(act):
            def copy_h(p, q):
                b = q % 2
                act.wait_ge(s_dh, p + 1)
                if after(p, 2):
                    act.wait_ge(s_dt, p - 1)
                nc.scalar.copy(eh[b][:, 0:HB // 2], hidden_bank(b, 0)).then_inc(s_dc[0], 1)

            def gelu(p, q):
                b = q % 2
                act.wait_ge(s_db, p + 1)
                nc.scalar.activation(eg[b][:], eg[b][:], ACT.Gelu).then_inc(s_dg, 1)

            def output(p, q):
                b = q % 2
                act.wait_ge(s_dy, p + 1)
                if after(p, 2):
                    act.wait_ge(s_eo[b], 8 * (p - b))
                nc.scalar.copy(eo[b][:], bank[6 + b][:, 0:ED]).then_inc(s_do, 1)

            over_tiles(act, [(0, copy_h), (1, gelu), (2, output)], NPAIR, unroll=RING)

        def hidden_bank(b, part):
            return bank[2 * b + part][:, 0:HB // 2 * 128].rearrange("p (j k) -> p j k", j=HB // 2)

        def experts_dve(dve):
            def copy_h(p, q):
                b = q % 2
                dve.wait_ge(s_dh, p + 1)
                if after(p, 2):
                    dve.wait_ge(s_dt, p - 1)
                nc.vector.tensor_copy(eh[b][:, HB // 2:HB], hidden_bank(b, 1)).then_inc(s_dc[1], 1)

            def bias(p, q):
                b = q % 2
                dve.wait_ge(s_dt, p + 1)
                if after(p, 2):
                    dve.wait_ge(s_dy, p - 1)
                for g in range(2):
                    js = slice(g * HB // 2, (g + 1) * HB // 2)
                    h4 = bank[4 + g][:, 0:HB // 2 * 128].rearrange("p (j e m) -> p j e m", j=HB // 2, e=2)
                    b4 = b1s[:, bass.ds(2 * p, 2), js].rearrange("p e j -> p j e").unsqueeze(3).to_broadcast([128, HB // 2, 2, B])
                    last = nc.vector.tensor_tensor(eg[b][:, js], h4, b4, ALU.add)
                last.then_inc(s_db, 1)

            over_tiles(dve, [(0, copy_h), (1, bias)], NPAIR, unroll=RING)

        def experts_pe(pe):
            pe.wait_ge(s_cxc, T)

            def hidden(p, q):
                b = q % 2
                pe.wait_ge(s_w1[q], 16 // RING * (p - q) + 16)
                pe.wait_ge(s_dx, p + 1)
                if after(p, 2):
                    pe.wait_ge(s_dc[0], p - 1)
                    pe.wait_ge(s_dc[1], p - 1)
                for part in range(2):
                    cols = slice(part * HID // 2, (part + 1) * HID // 2)
                    for c in range(2):
                        for e in range(2):
                            last = nc.tensor.matmul(bank[2 * b + part][e * B:(e + 1) * B, 0:HID // 2], xs[b][:, c, e, :], w1s[q][:, e, c, cols], start=(c == 0), stop=(c == 1))
                last.then_inc(s_dh, 1)

            def transposes(p, q):
                b = q % 2
                pe.wait_ge(s_dc[0], p + 1)
                pe.wait_ge(s_dc[1], p + 1)
                if after(p, 1):
                    pe.wait_ge(s_db, p)
                for j in range(HB):
                    k = j % (HB // 2) * 128
                    last = nc.tensor.transpose(bank[4 + j // (HB // 2)][:, k:k + 128], eh[b][:, j, :], ident)
                last.then_inc(s_dt, 1)

            def output(p, q):
                b = q % 2
                pe.wait_ge(s_w2[q], 16 // RING * (p - q) + 16)
                pe.wait_ge(s_dg, p + 1)
                if after(p, 2):
                    pe.wait_ge(s_do, p - 1)
                for j in range(HB):
                    for e in range(2):
                        last = nc.tensor.matmul(bank[6 + b][e * B:(e + 1) * B, 0:ED], eg[b][:, j, e, :], w2s[q][:, e, j, :], start=(j == 0), stop=(j == HB - 1))
                last.then_inc(s_dy, 1)

            over_tiles(pe, [(0, hidden), (1, transposes), (2, output)], NPAIR, unroll=RING)

        def combine_sp(sp):
            for b in range(2):
                sp.wait_ge(s_eo[b], 16 * NPAIR // 2)

            def load(t, q):
                if after(t, 4):
                    sp.wait_ge(s_ey, t - 3)
                m = t * GB
                sp.dma_start(e1[q][0:NE], ys_of[:, bass.ds(m, 1), :]).then_inc(s_w1[q], 16)
                if not (isinstance(t, int) and t == T - 1):
                    sp.dma_start(e1[q][NE:2 * NE], ys_of[:, bass.ds(m + 1, 1), :]).then_inc(s_w1[q], 16)
                    sp.dma_start(e2[q][:], ys_of[:, bass.ds(m + 2, 1), :]).then_inc(s_w1[q], 16)

            over_tiles(sp, [(0, load)], T, unroll=4, tail=1)

        def combine_pool(pool):
            def bias(t, q):
                pool.wait_ge(s_w1[q], 12 * (t - q) + n_w1 + (48 if not (isinstance(t, int) and t == T - 1) else 16))
                nc.gpsimd.tensor_tensor(e1[q][:], e1[q][:], Bc["b2r"], ALU.add)
                nc.gpsimd.tensor_tensor(e2[q][:], e2[q][:], Bc["b2r"][0:NE], ALU.add).then_inc(s_eb, 1)

            over_tiles(pool, [(0, bias)], T, unroll=4, tail=1)

        def combine_act(act):
            def copy(t, b):
                act.wait_ge(s_eT, t + 1)
                if after(t, 2):
                    act.wait_ge(s_ey, t - 1)
                nc.scalar.copy(c1[b][:], bank[6][:, 0:TP]).then_inc(s_eTa, 1)

            over_tiles(act, [(0, copy)], T)

        def combine_dve(dve):
            def spread(t, b):
                if after(t, 2):
                    dve.wait_ge(s_eT, t - 1)
                nc.vector.tensor_tensor(cw[b][:], ce[:, t, :].unsqueeze(1).to_broadcast([TP, GB, NE]), image.unsqueeze(2).to_broadcast([TP, GB, NE]), ALU.mult).then_inc(s_ecw, 1)

            def copy(t, b):
                dve.wait_ge(s_eT, t + 1)
                if after(t, 2):
                    dve.wait_ge(s_ey, t - 1)
                nc.vector.tensor_copy(c2[b][:], bank[7][0:NE, 0:TP]).then_inc(s_eTd, 1)

            def residual(t, b):
                dve.wait_ge(s_ey, t + 1)
                nc.vector.tensor_tensor(h[:, t, :], h[:, t, :], bank[b][0:TP, 0:ED], ALU.add).then_inc(s_h, 1)
                dve.wait_ge(s_h, 2 * T + t + 1)
                nc.vector.bn_stats(hst[:, t, :], h[:, t, :]).then_inc(s_hst, 1)

            over_tiles(dve, [(0, spread), (1, copy), (2, residual)], T)

        def combine_pe(pe):
            pe.wait_ge(s_do, NPAIR)

            def transposes(t, q):
                b = q % 2
                pe.wait_ge(s_ecw, t + 1)
                if after(t, 1):
                    pe.wait_ge(s_eTa, t)
                    pe.wait_ge(s_eTd, t)
                spread = cw[b][:].rearrange("p g n -> p (g n)")
                nc.tensor.transpose(bank[6][:, 0:TP], spread[:, 0:128], ident[0:TP, 0:TP])
                nc.tensor.transpose(bank[7][0:NE, 0:TP], spread[:, 128:3 * NE], ident[0:TP, 0:TP]).then_inc(s_eT, 1)

            def product(t, q):
                b = q % 2
                pe.wait_ge(s_eTa, t + 1)
                pe.wait_ge(s_eTd, t + 1)
                pe.wait_ge(s_eb, t + 1)
                if after(t, 2):
                    pe.wait_ge(s_h, 2 * T + t - 1)
                nc.tensor.matmul(bank[b][0:TP, 0:ED], c1[b][:], e1[q][:], start=True, stop=False)
                nc.tensor.matmul(bank[b][0:TP, 0:ED], c2[b][:], e2[q][:], start=False, stop=True).then_inc(s_ey, 1)

            over_tiles(pe, [(0, transposes), (1, product)], T, unroll=4)

        def value_columns(j):
            return j * TP if not isinstance(j, int) or j <= T else (B - WIN + PADR) * S + (j - T - 1) * TP

        def near_sp(sp):
            sp.wait_ge(s_ey, T)
            sp.dma_start(masks[:], ins["masks"]).then_inc(s_nin, 16)
            for v in range(2):
                sp.dma_start(near[v][:], ins["near"][v]).then_inc(s_nin, 16)
            sp.wait_ge(s_pad, 1)
            for e in range(EX):
                sp.dma_start(buf_of[e], zero[:]).then_inc(s_bz, 16)
            for b in range(2):
                sp.dma_start(w13[b][:], ins["w13"][b]).then_inc(s_w13[b], 16)
                sp.dma_start(w2r[b][:], ins["w2r"][b]).then_inc(s_w2r[b], 16)

        def near_pool(pool):
            pool.wait_ge(s_ey, T)
            nc.gpsimd.memset(zero[:], 0.0)
            nc.gpsimd.memset(xg[:, 0:PADR * S], 0.0)
            nc.gpsimd.memset(xg[:, XCOLS - PADR * S:XCOLS], 0.0)
            nc.gpsimd.memset(kT[:, 0:PADR * S], 0.0)
            nc.gpsimd.memset(kT[:, XCOLS - PADR * S:XCOLS], 0.0)
            nc.gpsimd.memset(vn[:, :, :, DN:DN + 1], 1.0).then_inc(s_pad, 1)
            pool.wait_ge(s_pad, 1)

            def source(j, q):
                b = q % 2
                if after(j, T + 1) and isinstance(j, int):
                    pool.wait_ge(s_fg, T)
                else:
                    pool.wait_ge(s_fg, j + 1 if after(j, 0) and not (isinstance(j, int) and j == T) else T)
                if after(j, 2):
                    pool.wait_ge(s_fV, j - 1)
                nc.gpsimd.tensor_copy(vsrc[b][:], xg[:, bass.ds(value_columns(j), TP)]).then_inc(s_fv, 1)

            def add_normalized(t, q):
                if isinstance(t, int) and t >= T:
                    return
                pool.wait_ge(s_hn, 2 * T + t + 1)
                nc.gpsimd.tensor_tensor(h[:, t, :], h[:, t, :], hn[q % 2][:], ALU.add).then_inc(s_ha, 1)

            over_tiles(pool, [(0, add_normalized), (4, source)], VT, unroll=4, tail=4)
            pool.wait_ge(s_ha, T)

            def residual(t, b):
                if after(t, 2):
                    pool.wait_ge(s_h, 3 * T + t - 1)
                nc.gpsimd.tensor_tensor(h2[b][:], h[:, t, :], Cc["bfc2"], ALU.add).then_inc(s_nh2, 1)

            over_tiles(pool, [(0, residual)], T, tail=2)

        def near_act(act):
            h_std(act, 2)

            def copy_T(t, q):
                b = q % 2
                act.wait_ge(s_hTr, 2 * T + t + 1)
                if after(t, 2):
                    act.wait_ge(s_f1, t - 1)
                nc.scalar.copy(hnT[b][:], bank[0][0:HALF, 0:2 * TP].rearrange("p (c q) -> p c q", c=2)).then_inc(s_hTc, 1)

            def conva(t, q):
                b = q % 2
                act.wait_ge(s_fA, t + 1)
                if after(t, 2):
                    act.wait_ge(s_fB, t - 1)
                nc.scalar.activation(fa[b][:], bank[2][0:CONV, 0:TP], ACT.Identity, bias=Cc["bconva"]).then_inc(s_fAc, 1)

            def gelu(t, q):
                b = q % 2
                act.wait_ge(s_fs, t + 1)
                nc.scalar.activation(xg[:, bass.ds(PADR * S + t * TP, TP)], fs[b][:], ACT.Gelu).then_inc(s_fg, 1)

            over_tiles(act, [(0, copy_T), (2, conva), (3, gelu)], T, unroll=4)

        def near_dve(dve):
            h_norm_constants(dve, 2)
            dve.wait_ge(s_ln, 15)
            dve.wait_ge(s_cci, 16)
            dve.wait_ge(s_pad, 1)

            def normalize(t, q):
                b = q % 2
                if after(t, 2):
                    dve.wait_ge(s_hTr, 2 * T + t - 1)
                    dve.wait_ge(s_ha, t - 1)
                nc.vector.tensor_scalar(hn[b][:], h[:, t, :], hmean[:, bass.ds(t, 1)], hrs[:, bass.ds(t, 1)], ALU.subtract, ALU.mult).then_inc(s_hn, 1)

            def fc1(t, q):
                dve.wait_ge(s_f1, t + 1)
                if after(t, 4):
                    dve.wait_ge(s_fs, t - 3)
                    dve.wait_ge(s_fA, t - 3)
                nc.vector.tensor_scalar(fx[q][:], bank[1][0:WN, 0:TP], Cc["bfc1"], None, ALU.add).then_inc(s_f1c, 1)

            def convb(t, q):
                b = q % 2
                dve.wait_ge(s_fB, t + 1)
                if after(t, 2):
                    dve.wait_ge(s_fg, t - 1)
                nc.vector.scalar_tensor_tensor(out=fs[b][:], in0=bank[3][0:WN, 0:TP], scalar=Cc["bconvb"], in1=fx[q][:], op0=ALU.add, op1=ALU.add).then_inc(s_fs, 1)

            def keys(t, q):
                dve.wait_ge(s_fK, t + 1)
                nc.vector.tensor_scalar(kT[:, bass.ds(PADR * S + t * TP, TP)], bank[4][0:WN, 0:TP], Cc["bk"], None, ALU.add).then_inc(s_fKc, 1)

            def values(j, q):
                dve.wait_ge(s_fV, j + 1)
                nc.vector.tensor_tensor(vn[:, j, :, 0:DN], bank[5][0:TP, 0:WN].rearrange("p (h d) -> p h d", h=NHN), Cc["bv"].rearrange("p (h d) -> p h d", h=NHN), ALU.add).then_inc(s_fVc, 1)

            over_tiles(dve, [(0, normalize), (1, fc1), (3, convb), (4, keys), (5, values)], T, unroll=4)
            for j in range(T, VT):
                values(j, j % 4)

            dve.wait_ge(s_nin, 48)
            for v in range(4):
                last = nc.vector.tensor_tensor(bias[v][:], near[v == 3][:], masks[:, v, :].unsqueeze(1).to_broadcast([TP, NHN, KW]), ALU.add)
            last.then_inc(s_nb, 1)
            dve.wait_ge(s_nb, 1)

            def spread(t, b):
                dve.wait_ge(s_nQ, t + 1)
                if after(t, 2):
                    dve.wait_ge(s_nS, 4 * t - 4)
                nc.vector.scalar_tensor_tensor(out=qx[b][:], in0=bank[0][0:WN, 0:TP].unsqueeze(1).to_broadcast([WN, NHN, TP]), scalar=Cc["bq"], in1=Cc["head"].unsqueeze(2).to_broadcast([WN, NHN, TP]), op0=ALU.add, op1=ALU.mult).then_inc(s_nq, 1)

            def logits(t, b):
                v = {0: 0, T - 2: 2, T - 1: 3}.get(t, 1) if isinstance(t, int) else 1
                if after(t, 2):
                    dve.wait_ge(s_nT, t - 1)
                    dve.wait_ge(s_ne, t - 1)
                for head in range(NHN):
                    dve.wait_ge(s_nS, 4 * t + head + 1)
                    nc.vector.memset(tick[:, head:head + 1], 0.0)
                    nc.vector.tensor_tensor_reduce(nl[b][:, head, :], bank[1 + head % 2][0:TP, 0:KW], bias[v][:, head, :], 1.0, -3.0e38, ALU.add, ALU.max, nm[b][:, head:head + 1]).then_inc(s_nl, 1)
                dve.wait_ge(s_nl, 4 * t + 4)
                nc.vector.tensor_scalar(nn[b][:], nm[b][:], -1.0, None, ALU.mult).then_inc(s_nm, 1)

            def copy_w(t, b):
                dve.wait_ge(s_nT, t + 1)
                if after(t, 2):
                    dve.wait_ge(s_nA, t - 1)
                nc.vector.tensor_copy(pTa[b][:, 2:4], bank[4][0:TP, 0:4 * TP].rearrange("p (h c q) -> p h c q", h=2, c=2)).then_inc(s_nTd, 1)

            def normalize_out(t, b):
                p = bank[6][0:TP, 0:NHN * (DN + 1)].rearrange("p (h d) -> p h d", h=NHN)
                dve.wait_ge(s_nA, t + 1)
                nc.vector.reciprocal(nr[b][:], p[:, :, DN]).then_inc(s_nr, 1)
                dve.wait_ge(s_nr, t + 1)
                if after(t, 2):
                    dve.wait_ge(s_noT, t - 1)
                nc.vector.tensor_tensor(no[b][:], p[:, :, 0:DN], nr[b][:].unsqueeze(2).to_broadcast([TP, NHN, DN]), ALU.mult).then_inc(s_no, 1)

            def residual(t, b):
                dve.wait_ge(s_nF, t + 1)
                dve.wait_ge(s_nh2, t + 1)
                nc.vector.tensor_tensor(h[:, t, :], bank[7][0:TP, 0:ED], h2[b][:], ALU.add).then_inc(s_h, 1)
                dve.wait_ge(s_h, 3 * T + t + 1)
                nc.vector.bn_stats(hst[:, t, :], h[:, t, :]).then_inc(s_hst, 1)

            over_tiles(dve, [(0, spread), (3, normalize_out), (1, logits), (2, copy_w), (3, residual)], T, tail=2)

        def near_act2(act):
            def exps(t, b):
                act.wait_ge(s_nm, t + 1)
                for head in range(NHN):
                    last = nc.scalar.activation(nl[b][:, head, :], nl[b][:, head, :], ACT.Exp, bias=nn[b][:, head:head + 1])
                last.then_inc(s_ne, 1)

            def copy_w(t, b):
                act.wait_ge(s_nT, t + 1)
                if after(t, 2):
                    act.wait_ge(s_nA, t - 1)
                nc.scalar.copy(pTa[b][:, 0:2], bank[3][0:TP, 0:4 * TP].rearrange("p (h c q) -> p h c q", h=2, c=2))
                nc.scalar.copy(pTb[b][:], bank[5][0:S, 0:4 * TP].rearrange("p (h q) -> p h q", h=NHN)).then_inc(s_nTa, 1)

            def copy_oT(t, b):
                act.wait_ge(s_noT, t + 1)
                if after(t, 2):
                    act.wait_ge(s_nP, t - 1)
                nc.scalar.copy(noT[b][:], bank[7][0:WN, 0:TP]).then_inc(s_noc, 1)

            def proj(t, b):
                act.wait_ge(s_nP, t + 1)
                if after(t, 2):
                    act.wait_ge(s_nF, t - 1)
                nc.scalar.activation(nz[b][:], bank[7][0:WN, 0:TP], ACT.Identity, bias=Cc["bproj"]).then_inc(s_nz, 1)

            over_tiles(act, [(3, copy_oT), (3, proj), (2, copy_w), (1, exps)], T, tail=2)

        def near_pe(pe):
            pe.wait_ge(s_cci, 16)
            pe.wait_ge(s_h, 2 * T + T)

            def transpose_h(t, q):
                b = q % 2
                pe.wait_ge(s_hn, 2 * T + t + 1)
                if after(t, 1):
                    pe.wait_ge(s_hTc, 2 * T + t)
                for c in range(2):
                    last = nc.tensor.transpose(bank[0][0:HALF, c * TP:(c + 1) * TP], hn[b][:, c * HALF:(c + 1) * HALF], ident[0:TP, 0:TP])
                last.then_inc(s_hTr, 1)

            def fc1(t, q):
                b = q % 2
                pe.wait_ge(s_hTc, 2 * T + t + 1)
                if after(t, 1):
                    pe.wait_ge(s_f1c, t)
                for c in range(2):
                    last = nc.tensor.matmul(bank[1][0:WN, 0:TP], Cc["fc1"][:, c * WN:(c + 1) * WN], hnT[b][:, c, :], start=(c == 0), stop=(c == 1))
                last.then_inc(s_f1, 1)

            def conva(t, q):
                pe.wait_ge(s_f1c, t + 1)
                if after(t, 1):
                    pe.wait_ge(s_fAc, t)
                nc.tensor.matmul(bank[2][0:CONV, 0:TP], Cc["conva"], fx[q][:], start=True, stop=True).then_inc(s_fA, 1)

            def convb(t, q):
                pe.wait_ge(s_fAc, t + 1)
                if after(t, 1):
                    pe.wait_ge(s_fs, t)
                nc.tensor.matmul(bank[3][0:WN, 0:TP], Cc["convb"], fa[q % 2][:], start=True, stop=True).then_inc(s_fB, 1)

            def keys(t, q):
                pe.wait_ge(s_fg, t + 1)
                if after(t, 1):
                    pe.wait_ge(s_fKc, t)
                nc.tensor.matmul(bank[4][0:WN, 0:TP], Cc["wk"], xg[:, bass.ds(PADR * S + t * TP, TP)], start=True, stop=True).then_inc(s_fK, 1)

            def values(j, q):
                pe.wait_ge(s_fv, j + 1)
                if after(j, 1):
                    pe.wait_ge(s_fVc, j)
                nc.tensor.matmul(bank[5][0:TP, 0:WN], vsrc[q % 2][:], Cc["wv"], start=True, stop=True).then_inc(s_fV, 1)

            over_tiles(pe, [(0, transpose_h), (1, fc1), (2, conva), (3, convb), (4, keys), (5, values)], T, unroll=4)
            for j in range(T, VT):
                values(j, j % 4)
            pe.wait_ge(s_fKc, T)
            pe.wait_ge(s_fVc, VT)
            pe.wait_ge(s_hTc, 2 * T + T)

            def query(t, b):
                if after(t, 1):
                    pe.wait_ge(s_nq, t)
                nc.tensor.matmul(bank[0][0:WN, 0:TP], Cc["wq"], xg[:, bass.ds(PADR * S + t * TP, TP)], start=True, stop=True).then_inc(s_nQ, 1)

            def scores(t, b, heads):
                first = (B - WIN + PADR) * S if isinstance(t, int) and t == T - 1 else t * TP
                pe.wait_ge(s_nq, t + 1)
                for head in heads:
                    if after(t, 1) or head >= 2:
                        pe.wait_ge(s_nl, 4 * t + head - 1)
                    nc.tensor.matmul(bank[1 + head % 2][0:TP, 0:KW], qx[b][:, head, :], kT[:, bass.ds(first, KW)], start=True, stop=True).then_inc(s_nS, 1)

            def transpose_w(t, b):
                pe.wait_ge(s_ne, t + 1)
                if after(t, 1):
                    pe.wait_ge(s_nTa, t)
                    pe.wait_ge(s_nTd, t)
                for head in range(NHN):
                    for c in range(2):
                        k = (head % 2 * 2 + c) * TP
                        nc.tensor.transpose(bank[3 + head // 2][0:TP, k:k + TP], nl[b][:, head, c * TP:(c + 1) * TP], ident[0:TP, 0:TP])
                    last = nc.tensor.transpose(bank[5][0:S, head * TP:(head + 1) * TP], nl[b][:, head, 2 * TP:KW], ident[0:TP, 0:TP])
                last.then_inc(s_nT, 1)

            def values_out(t, b):
                pe.wait_ge(s_nTa, t + 1)
                pe.wait_ge(s_nTd, t + 1)
                if after(t, 1):
                    pe.wait_ge(s_no, t)
                j = T + 1 if isinstance(t, int) and t == T - 1 else t
                for head in range(NHN):
                    o = bank[6][0:TP, head * (DN + 1):(head + 1) * (DN + 1)]
                    nc.tensor.matmul(o, pTa[b][:, head, 0, :], vn[:, j, head, :], start=True, stop=False)
                    nc.tensor.matmul(o, pTa[b][:, head, 1, :], vn[:, j + 1, head, :], start=False, stop=False)
                    last = nc.tensor.matmul(o, pTb[b][:, head, :], vn[0:S, j + 2, head, :], start=False, stop=True)
                last.then_inc(s_nA, 1)

            def transpose_o(t, b):
                pe.wait_ge(s_no, t + 1)
                if after(t, 1):
                    pe.wait_ge(s_h, 3 * T + t)
                nc.tensor.transpose(bank[7][0:WN, 0:TP], no[b][:].rearrange("p h d -> p (h d)"), ident[0:TP, 0:TP]).then_inc(s_noT, 1)

            def proj(t, b):
                pe.wait_ge(s_noc, t + 1)
                nc.tensor.matmul(bank[7][0:WN, 0:TP], Cc["proj"], noT[b][:], start=True, stop=True).then_inc(s_nP, 1)

            def fc2(t, b):
                pe.wait_ge(s_nz, t + 1)
                nc.tensor.matmul(bank[7][0:TP, 0:ED], nz[b][:], Cc["fc2"], start=True, stop=True).then_inc(s_nF, 1)

            over_tiles(pe, [(0, query), (3, transpose_o), (1, lambda t, b: scores(t, b, (0, 1))), (3, proj),
                            (1, lambda t, b: scores(t, b, (2, 3))), (3, fc2), (2, transpose_w), (2, values_out)], T, tail=2)

        def route_act(act):
            h_std(act, 3)
            act.wait_ge(s_ph, 9 + 2)
            nc.scalar.activation(zrt[:], zsq[:], ACT.Sqrt, bias=eps6[:], scale=4.0).then_inc(s_hsd, 1)

            def copy_T(t, b):
                act.wait_ge(s_hTr, 3 * T + t + 1)
                if after(t, 2):
                    act.wait_ge(s_gl, t - 1)
                nc.scalar.copy(hnT[b][:], bank[0][0:HALF, 0:2 * TP].rearrange("p (c q) -> p c q", c=2)).then_inc(s_hTc, 1)

            over_tiles(act, [(0, copy_T)], T)
            act.wait_ge(s_rt, 1)
            nc.scalar.activation(wexp[:], wdif[:], ACT.Exp).then_inc(s_re, 1)

        def route_pe(pe):
            def transpose_h(t, b):
                pe.wait_ge(s_hn, 3 * T + t + 1)
                if after(t, 1):
                    pe.wait_ge(s_hTc, 3 * T + t)
                for c in range(2):
                    last = nc.tensor.transpose(bank[0][0:HALF, c * TP:(c + 1) * TP], hn[b][:, c * HALF:(c + 1) * HALF], ident[0:TP, 0:TP])
                last.then_inc(s_hTr, 1)

            def router(t, b):
                pe.wait_ge(s_hTc, 3 * T + t + 1)
                for c in range(2):
                    last = nc.tensor.matmul(bank[1][0:TP, bass.ds(t * EX, EX)], hnT[b][:, c, :], Cc["router"][:, c * EX:(c + 1) * EX], start=(c == 0), stop=(c == 1))
                last.then_inc(s_gl, 1)

            over_tiles(pe, [(0, transpose_h), (1, router)], T)
            pe.wait_ge(s_rt, 2)
            marks = hots[:].rearrange("p t e -> p (t e)")
            nc.tensor.matmul(bank[2][0:TP, 0:T * EX], Cc["before"], marks, start=True, stop=True)
            nc.tensor.matmul(bank[3][0:TP, 0:T * EX], Cc["ones"], marks, start=True, stop=True).then_inc(s_rp, 1)

        def route_dve(dve):
            h_norm_constants(dve, 3)
            dve.wait_ge(s_ln, 20)
            nc.vector.memset(eps6[:], 1e-6)
            nc.vector.tensor_tensor(zsq[:], hvar[:], hrs[:], ALU.mult).then_inc(s_ph, 1)
            dve.wait_ge(s_ph, 9 + 1)
            nc.vector.tensor_tensor(zsq[:], zsq[:], hrs[:], ALU.mult).then_inc(s_ph, 1)
            dve.wait_ge(s_hsd, 5)
            nc.vector.reciprocal(zs[:], zrt[:]).then_inc(s_ph, 1)
            dve.wait_ge(s_ph, 9 + 3)
            nc.vector.scalar_tensor_tensor(out=zs[:], in0=zs[:], scalar=2.0, in1=hrs[:], op0=ALU.mult, op1=ALU.mult).then_inc(s_ph, 1)
            dve.wait_ge(s_ph, 9 + 4)

            def normalize(t, b):
                if after(t, 2):
                    dve.wait_ge(s_hTr, 3 * T + t - 1)
                nc.vector.tensor_scalar(hn[b][:], h[:, t, :], hmean[:, bass.ds(t, 1)], hrs[:, bass.ds(t, 1)], ALU.subtract, ALU.mult).then_inc(s_hn, 1)
                nc.vector.tensor_scalar(zk[:, t, :], h[:, t, :], hmean[:, bass.ds(t, 1)], zs[:, bass.ds(t, 1)], ALU.subtract, ALU.mult).then_inc(s_gz, 1)

            over_tiles(dve, [(0, normalize)], T)

            per_row = lambda a: a.unsqueeze(2).to_broadcast([TP, T, EX])
            index = Cc["index"].unsqueeze(1).to_broadcast([TP, T, EX])
            real = Cc["real"].unsqueeze(1).to_broadcast([TP, 2, T])
            dve.wait_ge(s_gl, T)
            logits = bank[1][0:TP, 0:T * EX].rearrange("p (t e) -> p t e", e=EX)
            r = 0
            for k in range(2):
                lg = lg2[:] if k else logits
                nc.vector.tensor_reduce(top[:, k, :], lg, AX.X, ALU.max).then_inc(s_r, 1)
                dve.wait_ge(s_r, r + 1)
                if k == 1:
                    nc.vector.tensor_tensor(wdif[:], top[:, 1, :], top[:, 0, :], ALU.subtract).then_inc(s_rt, 1)
                nc.vector.tensor_tensor(eq[:], lg, per_row(top[:, k, :]), ALU.is_equal).then_inc(s_r, 1)
                dve.wait_ge(s_r, r + 2)
                nc.vector.scalar_tensor_tensor(out=key[:], in0=eq[:], scalar=-float(EX), in1=index, op0=ALU.mult, op1=ALU.add).then_inc(s_r, 1)
                dve.wait_ge(s_r, r + 3)
                nc.vector.tensor_reduce(expert[:, k, :], key[:], AX.X, ALU.min).then_inc(s_r, 1)
                dve.wait_ge(s_r, r + 4)
                nc.vector.tensor_tensor(hot[:, k], key[:], per_row(expert[:, k, :]), ALU.is_equal).then_inc(s_r, 1)
                dve.wait_ge(s_r, r + 5)
                r += 5
                if k == 0:
                    nc.vector.scalar_tensor_tensor(out=lg2[:], in0=hot[:, 0], scalar=-1e30, in1=logits, op0=ALU.mult, op1=ALU.add).then_inc(s_r, 1)
                    dve.wait_ge(s_r, r + 1)
                    r += 1
            nc.vector.tensor_tensor(hots[:], hot[:, 0], hot[:, 1], ALU.add).then_inc(s_r, 1)
            dve.wait_ge(s_r, r + 1)
            nc.vector.tensor_tensor(hots[:], hots[:], per_row(Cc["real"]), ALU.mult).then_inc(s_rt, 1)

            dve.wait_ge(s_rp, 1)
            prior = bank[2][0:TP, 0:T * EX].rearrange("p (t e) -> p t e", e=EX)
            totals = bank[3][0:TP, 0:T * EX].rearrange("p (t e) -> p t e", e=EX)
            nc.vector.memset(sums[0][:, 0:1, :], 0.0)
            nc.vector.tensor_copy(sums[0][:, 1:T, :], totals[:, 0:T - 1, :]).then_inc(s_r, 1)
            r += 2
            dve.wait_ge(s_r, r)
            step, b = 1, 0
            while step < T:
                nc.vector.tensor_copy(sums[1 - b][:, 0:step, :], sums[b][:, 0:step, :])
                nc.vector.tensor_tensor(sums[1 - b][:, step:T, :], sums[b][:, step:T, :], sums[b][:, 0:T - step, :], ALU.add).then_inc(s_r, 1)
                r += 1
                dve.wait_ge(s_r, r)
                step, b = 2 * step, 1 - b
            nc.vector.tensor_tensor(place[:], prior, sums[b][:], ALU.add).then_inc(s_r, 1)
            dve.wait_ge(s_r, r + 1)
            nc.vector.tensor_tensor(picked[:], hot[:], place[:].unsqueeze(1).to_broadcast([TP, 2, T, EX]), ALU.mult).then_inc(s_r, 1)
            dve.wait_ge(s_r, r + 2)
            nc.vector.tensor_reduce(pk[:], picked[:], AX.X, ALU.add).then_inc(s_r, 1)
            dve.wait_ge(s_r, r + 3)
            nc.vector.scalar_tensor_tensor(out=kept[:], in0=pk[:], scalar=float(CAP), in1=real, op0=ALU.is_lt, op1=ALU.mult)
            nc.vector.scalar_tensor_tensor(out=slot[:], in0=expert[:], scalar=float(CAPP), in1=pk[:], op0=ALU.mult, op1=ALU.add)
            nc.vector.tensor_scalar(last_slot[:], pk[:], float(CAP - 1), float(EX * CAPP), ALU.min, ALU.add).then_inc(s_r, 1)
            dve.wait_ge(s_r, r + 4)
            nc.vector.tensor_scalar(away[:], kept[:], -SKIP, SKIP + EX * CAPP, ALU.mult, ALU.add)
            nc.vector.scalar_tensor_tensor(out=last_slot[:], in0=expert[:], scalar=float(CAPP), in1=last_slot[:], op0=ALU.mult, op1=ALU.add).then_inc(s_r, 1)
            dve.wait_ge(s_r, r + 5)
            nc.vector.tensor_tensor(slot[:], slot[:], away[:], ALU.add).then_inc(s_r, 1)
            dve.wait_ge(s_r, r + 6)
            nc.vector.tensor_copy(to[:], slot[:])
            nc.vector.tensor_copy(frm[:], last_slot[:]).then_inc(s_rt, 1)

            dve.wait_ge(s_re, 1)
            nc.vector.tensor_scalar(wsum[:], wexp[:], 1.0, None, ALU.add).then_inc(s_r, 1)
            dve.wait_ge(s_r, r + 7)
            nc.vector.reciprocal(wts[:, 0, :], wsum[:]).then_inc(s_r, 1)
            dve.wait_ge(s_r, r + 8)
            nc.vector.tensor_tensor(wts[:, 1, :], wexp[:], wts[:, 0, :], ALU.mult).then_inc(s_r, 1)
            dve.wait_ge(s_r, r + 9)
            nc.vector.tensor_tensor(wts[:], wts[:], kept[:], ALU.mult).then_inc(s_r, 1)
            dve.wait_ge(s_r, r + 10)
            nc.vector.tensor_tensor(wsum[:], wts[:, 0, :], wts[:, 1, :], ALU.add).then_inc(s_r, 1)
            dve.wait_ge(s_r, r + 11)
            nc.vector.tensor_tensor(wsum[:], wsum[:], hrs[:], ALU.mult).then_inc(s_r, 1)
            dve.wait_ge(s_r, r + 12)
            nc.vector.tensor_scalar(own[:, 0, :], wsum[:], 1.0, None, ALU.add)
            nc.vector.tensor_tensor(own[:, 1, :], wsum[:], hmean[:], ALU.mult).then_inc(s_rt, 1)

        def rows_pool(pool):
            pool.wait_ge(s_rt, 3)
            pool.wait_ge(s_gz, T)
            pool.wait_ge(s_bz, 16 * EX)
            for t in range(T):
                for k in range(2):
                    nc.gpsimd.indirect_dma_start(buf, bass.IndirectOffsetOnAxis(ap=to[:, k, t:t + 1], axis=0), zk[:, t, :], None, bounds_check=EX * CAPP - 1, oob_is_err=False).then_inc(s_sc, 16)
            for b in range(2):
                pool.wait_ge(s_eo[b], n_eo + 16 * EX // 2)
            for t in range(T):
                if t >= 4:
                    pool.wait_ge(s_o, t - 3)
                for k in range(2):
                    nc.gpsimd.indirect_dma_start(back[k][t % 4][:], None, ybuf, bass.IndirectOffsetOnAxis(ap=frm[:, k, t:t + 1], axis=0), bounds_check=EX * CAPP - 1, oob_is_err=False).then_inc(s_g[t % 4], 16)

        def routed_sp(sp):
            sp.wait_ge(s_sc, 16 * 2 * T)

            def load(e, b):
                if after(e, 2):
                    sp.wait_ge(s_zT, 4 * e - 4)
                sp.dma_start(zr[b][:].rearrange("p j d -> p (j d)"), buf_of[e]).then_inc(s_zr[b], 16)
                if after(e, 2):
                    sp.wait_ge(s_gu, 16 * e - 16)
                    sp.dma_start(w13[b][:], ins["w13"][e]).then_inc(s_w13[b], 16)
                    sp.wait_ge(s_yp, SJ * (e - 1))
                    sp.dma_start(w2r[b][:], ins["w2r"][e]).then_inc(s_w2r[b], 16)

            def store(e, b):
                sp.wait_ge(s_yc[0], SJ // 2 * (e + 1))
                sp.wait_ge(s_yc[1], SJ // 2 * (e + 1))
                sp.dma_start(ybuf_of[e], yr[b][:].rearrange("p j d -> p (j d)")).then_inc(s_eo[b], 16)

            over_tiles(sp, [(0, load), (2, store)], EX)

            def result(t, b):
                sp.wait_ge(s_o, t + 1)
                if after(t, T - 1) and isinstance(t, int):
                    sp.dma_start(rows_out[t * TP:B * S], acc[b][0:B * S - t * TP]).then_inc(s_x[b], 16)
                else:
                    sp.dma_start(rows_out[bass.ds(t * TP, TP)], acc[b][:]).then_inc(s_x[b], 16)

            over_tiles(sp, [(0, result)], T, tail=1)
            for b in range(2):
                sp.wait_ge(s_x[b], n_x + 16 * T // 2)

        def routed_pe(pe):
            def transposes(e, b):
                pe.wait_ge(s_zr[b], 8 * (e - b) + 16)
                for g in range(2):
                    for c in range(2):
                        if after(e, 1) or g:
                            pe.wait_ge(s_zc[c], 2 * e + g)
                        for j in range(SJ // 2):
                            last = nc.tensor.transpose(bank[c][0:HALF, j * SP_:(j + 1) * SP_], zr[b][:, g * SJ // 2 + j, c * HALF:(c + 1) * HALF], ident[0:SP_, 0:SP_])
                        last.then_inc(s_zT, 1)

            def gate_up(e, b):
                pe.wait_ge(s_w13[b], 8 * (e - b) + 16)
                for half in range(2):
                    for c in range(2):
                        pe.wait_ge(s_zc[c], 2 * e + half + 1)
                    for m in range(EH // 128):
                        k = half * (EH // 128) + m
                        if after(e, 1) or k >= 2:
                            pe.wait_ge(s_hT, 8 * e + k - 1)
                        for part in range(2):
                            at = part * EH + m * 128
                            for c in range(2):
                                last = nc.tensor.matmul(bank[2 + 2 * (m % 2) + part][:, 0:HS], w13[b][:, c, at:at + 128], zT[b][:, c, half * HS:(half + 1) * HS], start=(c == 0), stop=(c == 1))
                            last.then_inc(s_gu, 1)

            def outputs(e, b):
                pe.wait_ge(s_w2r[b], 8 * (e - b) + 16)
                for j in range(SJ):
                    pe.wait_ge(s_hT, 8 * e + 4 * (j * 2 // SJ + 1))
                    if after(e, 1) or j >= 2:
                        pe.wait_ge(s_yc[j % 2], SJ // 2 * e + j // 2)
                    for m in range(EH // 128):
                        last = nc.tensor.matmul(bank[6 + j % 2][0:SP_, 0:ED], hT[:, m, j * SP_:(j + 1) * SP_], w2r[b][:, m, :], start=(m == 0), stop=(m == EH // 128 - 1))
                    last.then_inc(s_yp, 1)

            over_tiles(pe, [(1, gate_up), (0, transposes), (1, outputs)], EX)

        def routed_act(act):
            def store_z(e, b):
                for g in range(2):
                    act.wait_ge(s_zT, 4 * e + 2 * g + 1)
                    if after(e, 2):
                        act.wait_ge(s_gu, 16 * e - 16)
                    nc.scalar.copy(act_tick[:], eps5[:])
                    nc.scalar.activation(zT[b][:, 0, g * HS:(g + 1) * HS], bank[0][0:HALF, 0:HS], ACT.Copy, scale=Cc["gain"][:, bass.ds(e, 1)]).then_inc(s_zc[0], 1)

            def silu(e, b):
                for k in range(8):
                    act.wait_ge(s_gu, 16 * e + 2 * k + 1)
                    if after(e, 1) or k >= 2:
                        act.wait_ge(s_hT, 8 * e + k - 1)
                    nc.scalar.activation(sg[k % 2][:], bank[2 + 2 * (k % 2)][:, 0:HS], ACT.Silu).then_inc(s_sg, 1)

            def copy_y(e, b):
                for j in range(0, SJ, 2):
                    act.wait_ge(s_yp, SJ * e + j + 1)
                    if after(e, 2):
                        act.wait_ge(s_eo[b], 8 * (e - b) + n_eo)
                    nc.scalar.copy(yr[b][:, j, :], bank[6][0:SP_, 0:ED]).then_inc(s_yc[0], 1)

            over_tiles(act, [(1, silu), (0, store_z), (1, copy_y)], EX)

        def routed_dve(dve):
            def store_z(e, b):
                for g in range(2):
                    dve.wait_ge(s_zT, 4 * e + 2 * g + 2)
                    if after(e, 2):
                        dve.wait_ge(s_gu, 16 * e - 16)
                    nc.vector.tensor_scalar(zT[b][:, 1, g * HS:(g + 1) * HS], bank[1][0:HALF, 0:HS], Cc["gain"][:, bass.ds(e + EX, 1)], None, ALU.mult).then_inc(s_zc[1], 1)

            def hidden(e, b):
                for k in range(8):
                    half, m = k // 4, k % 4
                    dve.wait_ge(s_sg, 8 * e + k + 1)
                    dve.wait_ge(s_gu, 16 * e + 2 * k + 2)
                    if after(e, 1):
                        dve.wait_ge(s_yp, SJ * e)
                    nc.vector.tensor_tensor(hT[:, m, half * HS:(half + 1) * HS], sg[k % 2][:], bank[3 + 2 * (k % 2)][:, 0:HS], ALU.mult).then_inc(s_hT, 1)

            def copy_y(e, b):
                for j in range(1, SJ, 2):
                    dve.wait_ge(s_yp, SJ * e + j + 1)
                    if after(e, 2):
                        dve.wait_ge(s_eo[b], 8 * (e - b) + n_eo)
                    nc.vector.tensor_copy(yr[b][:, j, :], bank[7][0:SP_, 0:ED]).then_inc(s_yc[1], 1)

            over_tiles(dve, [(1, hidden), (0, store_z), (1, copy_y)], EX)

            dve.wait_ge(s_rt, 4)

            def add(t, q):
                b = q % 2
                dve.wait_ge(s_g[q], 8 * (t - q) + 32)
                if after(t, 2):
                    dve.wait_ge(s_x[b], 8 * (t - b) + n_x)
                nc.vector.tensor_scalar(acc[b][:], h[:, t, :], own[:, 0, bass.ds(t, 1)], own[:, 1, bass.ds(t, 1)], ALU.mult, ALU.subtract).then_inc(s_o1, 1)
                dve.wait_ge(s_o1, 2 * t + 1)
                nc.vector.scalar_tensor_tensor(out=acc[b][:], in0=back[0][q][:], scalar=wts[:, 0, bass.ds(t, 1)], in1=acc[b][:], op0=ALU.mult, op1=ALU.add).then_inc(s_o1, 1)
                dve.wait_ge(s_o1, 2 * t + 2)
                nc.vector.scalar_tensor_tensor(out=acc[b][:], in0=back[1][q][:], scalar=wts[:, 1, bass.ds(t, 1)], in1=acc[b][:], op0=ALU.mult, op1=ALU.add).then_inc(s_o, 1)

            over_tiles(dve, [(0, add)], T, unroll=4)

        block = ctx.enter_context(nc.Block())

        @block.sync
        def _(sp):
            embed_sp(sp)
            sp.wait_ge(s_cbi, 16)
            experts_sp(sp)
            combine_sp(sp)
            near_sp(sp)
            routed_sp(sp)

        @block.gpsimd
        def _(pool):
            embed_pool(pool)
            experts_pool(pool)
            combine_pool(pool)
            near_pool(pool)
            rows_pool(pool)

        @block.scalar
        def _(act):
            embed_act(act)
            attention_act(act)
            dispatch_act(act)
            experts_act(act)
            combine_act(act)
            near_act(act)
            near_act2(act)
            route_act(act)
            routed_act(act)

        @block.vector
        def _(dve):
            embed_dve(dve)
            attention_dve(dve)
            dispatch_dve(dve)
            experts_dve(dve)
            combine_dve(dve)
            near_dve(dve)
            route_dve(dve)
            routed_dve(dve)

        @block.tensor
        def _(pe):
            embed_pe(pe)
            attention_pe(pe)
            dispatch_pe(pe)
            experts_pe(pe)
            combine_pe(pe)
            near_pe(pe)
            route_pe(pe)
            routed_pe(pe)


def pack_rows(pack, parts):
    at, n = columns(pack)
    a = np.zeros((128, n), np.float32)
    for name, (rows, off, cols) in at.items():
        a[0:rows, off:off + cols] = parts[name]
    return a


def lay_out(i):
    f = {k: np.asarray(v) for k, v in i.items()}
    x = f["x"].reshape(B, C_IN, 6, PATCH, 6, PATCH).transpose(0, 2, 4, 3, 5, 1).reshape(B, NP_, PD)
    xr = np.zeros((T * GB, S, PD), np.float32)
    xr[0:B, 1:] = x
    per_image = lambda first, rest: np.tile(np.concatenate([first, rest]), (GB, 1))
    zero = np.zeros((1, ED), np.float32)
    rows = lambda v, n: np.tile(v[None, :], (n, 1))
    cls = f["L0_tok_cls_token"][None, :]
    ca = pack_rows(PACK_A, {
        "ident": np.eye(128, dtype=np.float32),
        "g1": f["L0_tok_ln1_g"].reshape(KC, 128).T, "b1": f["L0_tok_ln1_b"].reshape(KC, 128).T,
        "wtok": f["L0_tok_W"].reshape(KC, 128, ED).transpose(1, 0, 2).reshape(128, KC * ED),
        "btok": rows(f["L0_tok_b"], TP),
        "g2m": per_image(zero, rows(f["L0_tok_ln2_g"], NP_)), "b2m": per_image(zero, rows(f["L0_tok_ln2_b"], NP_)),
        "pos": np.tile(f["L0_tok_pos_embed"][0], (GB, 1)), "cls": per_image(cls, np.zeros((NP_, ED), np.float32)),
    })
    chunks = lambda w, n=2: w.reshape(n, -1, w.shape[1]).transpose(1, 0, 2).reshape(w.shape[0] // n, -1)
    wq, wk = (f["L0_attn_Wq"], f["L0_attn_Wk"])
    own = np.arange(TP)[:, None] // S == np.arange(TP)[None, :] // S
    causal = (own & (np.arange(TP)[:, None] <= np.arange(TP)[None, :])).astype(np.float32)
    cb = pack_rows(PACK_B, {
        "wqk": chunks(np.concatenate([wq, wk], 1)), "wvg": chunks(np.concatenate([f["L0_attn_Wv"], f["L0_attn_Wg"]], 1)),
        "wo": chunks(f["L0_attn_Wo"]), "causal": np.tile(causal, (1, 2)),
        "phi": chunks(f["L0_ffn_phi"][:, :, 0]), "scale": np.tile(f["L0_ffn_scale"][None, :], (HALF, 1)),
        "image": (np.arange(TP)[:, None] // S == np.arange(GB)[None, :]).astype(np.float32),
        "b2r": np.tile(f["L0_ffn_b2"], (2, 1)), "b1s": f["L0_ffn_b1"].reshape(NE, HB, 128).transpose(2, 0, 1).reshape(128, NE * HB),
        "ones": np.ones((128, 128), np.float32),
    })
    w1 = f["L0_ffn_w1"].reshape(NPAIR, 2, 2, HALF, HID).transpose(0, 3, 1, 2, 4)
    w2 = f["L0_ffn_w2"].reshape(NPAIR, 2, HB, 128, ED).transpose(0, 3, 1, 2, 4)
    col = lambda v: v[:, None]
    w = np.arange(TP)
    row, tok = w // S, w % S
    krow, ktok = np.arange(KW) // S, np.arange(KW) % S
    masks, near = np.zeros((TP, 4, KW), np.float32), np.zeros((2, TP, NHN, KW), np.float32)
    rpb = f["L1_attn_rpb"]
    for v, (q0, k0) in enumerate([(0, -PADR), (GB, GB - PADR), ((T - 2) * GB, (T - 2) * GB - PADR), ((T - 1) * GB, B - WIN)]):
        qr = q0 + row
        hs, ws = np.clip(qr - PADR, 0, B - WIN)[:, None], np.clip(tok - PADR, 0, S - WIN)[:, None]
        kr = (k0 + krow)[None, :]
        inside = (kr >= hs) & (kr < hs + WIN) & (ktok[None] >= ws) & (ktok[None] < ws + WIN)
        masks[:, v][(qr < B)[:, None] & ~inside] = -1e30
        if v in (1, 3):
            dr, dt = kr - qr[:, None] + WIN - 1, ktok[None] - tok[:, None] + WIN - 1
            ok = (dr >= 0) & (dr < 2 * WIN - 1) & (dt >= 0) & (dt < 2 * WIN - 1)
            for n in range(NHN):
                near[v // 2, :, n] = np.where(ok, rpb[n][np.where(ok, dr, 0), np.where(ok, dt, 0)], 0)
    qkv, bqkv = f["L1_attn_qkv_w"], f["L1_attn_qkv_b"]
    cc = pack_rows(PACK_C, {
        "fc1": chunks(f["L1_attn_fc1_w"].T), "conva": f["L1_attn_convA_w"].T, "convb": f["L1_attn_convB_w"].T,
        "wq": qkv[0:WN].T, "wk": qkv[WN:2 * WN].T, "wv": qkv[2 * WN:].T, "proj": f["L1_attn_proj_w"].T,
        "fc2": f["L1_attn_fc2_w"].T, "bv": rows(bqkv[2 * WN:], TP), "bfc2": rows(f["L1_attn_fc2_b"], TP),
        "bfc1": col(f["L1_attn_fc1_b"]), "bconva": col(f["L1_attn_convA_b"]), "bconvb": col(f["L1_attn_convB_b"]),
        "bq": col(bqkv[0:WN]), "bk": col(bqkv[WN:2 * WN]), "bproj": col(f["L1_attn_proj_b"]),
        "head": (np.arange(WN)[:, None] // DN == np.arange(NHN)[None, :]).astype(np.float32) * np.float32(DN ** -0.5),
        "router": chunks(f["L1_ffn_gate_w"].T), "before": (w[:, None] < w[None, :]).astype(np.float32),
        "index": np.tile(np.arange(EX, dtype=np.float32)[None, :], (TP, 1)),
        "real": (w[:, None] + TP * np.arange(T)[None, :] < B * S).astype(np.float32),
        "ones": np.ones((TP, TP), np.float32), "gain": chunks(f["L1_ffn_norm_w"].T),
    })
    w13 = f["L1_ffn_w13"].transpose(0, 2, 1).reshape(EX, 2, HALF, 2 * EH).transpose(0, 2, 1, 3)
    w2r = f["L1_ffn_w2"].transpose(0, 2, 1).reshape(EX, EH // 128, 128, ED).transpose(0, 2, 1, 3)
    return {"cc": cc, "masks": masks, "near": near, "w13": np.ascontiguousarray(w13), "w2r": np.ascontiguousarray(w2r),
            "w1": np.ascontiguousarray(w1), "w2": np.ascontiguousarray(w2), "x": xr.reshape(T, TP, PD), "ca": ca, "cb": cb}


_INS = ("cc", "masks", "near", "w13", "w2r", "w1", "w2", "x", "ca", "cb")


def kernel(**inputs):
    import numpy as _np
    import concourse.bacc as _bacc
    from concourse import mybir as _mybir
    from concourse.bass_utils import run_bass_kernel_spmd as _run

    nc = _bacc.Bacc("TRN2", target_bir_lowering=False, num_devices=1)
    laid = lay_out(inputs)
    arrays, args = {}, {}
    for name in _INS:
        a = _np.ascontiguousarray(laid[name])
        arrays[f"in_{name}_dram"] = a
        args[name] = nc.dram_tensor(f"in_{name}_dram", a.shape, _mybir.dt.from_np(a.dtype), kind="ExternalInput").ap()
    out = nc.dram_tensor("out_0_dram", (B * S, ED), _mybir.dt.float32, kind="ExternalOutput").ap()
    tower(nc, args, out)
    r = _run(nc, [arrays], core_ids=[0])
    return r.results[0]["out_0_dram"].reshape(B, S, ED)
```

```python
from contextlib import ExitStack

import concourse.bass as bass
from concourse import mybir
from concourse.alu_op_type import AluOpType as ALU
import numpy as np

ACT = mybir.ActivationFunctionType
AX = mybir.AxisListType
F32 = mybir.dt.float32
I32 = mybir.dt.int32

B, C_IN, IMG, PATCH = 64, 3, 96, 16
NP_ = (IMG // PATCH) ** 2
S = NP_ + 1
PD = C_IN * PATCH * PATCH
ED = 192
HALF = ED // 2
GB = 3
TP = GB * S
T = 22
NROW = T * TP
KC = PD // 128
NH, DH = 4, 64
NE, HID = 64, 768
HB = HID // 128
NPAIR = NE // 2
RING = 4
QKW = 2 * NH * DH
VGW = NH * DH + ED
WN, CONV, NHN = 96, 64, 4
DN = WN // NHN
WIN = 5
KR = GB + WIN - 1
KW = KR * S
PADR = WIN // 2
XCOLS = (T * GB + 2 * PADR) * S
VT = T + 4
VW = 32
PAIR = 2 * TP
EX, EH = 8, 512
CAP = int(np.ceil(1.25 * 2 * B * S / EX))
SJ = 6
SP_ = -(-CAP // SJ)
HS = SJ * SP_ // 2
CAPP = SJ * SP_
SKIP = 1.0e6

PACK_A = [("ident", 128, 128), ("g1", 128, KC), ("b1", 128, KC), ("wtok", 128, KC * ED),
          ("btok", TP, ED), ("g2m", TP, ED), ("b2m", TP, ED), ("pos", TP, ED), ("cls", TP, ED)]

PACK_B = [("wqk", HALF, 2 * QKW), ("wvg", HALF, 2 * VGW), ("wo", 128, 2 * ED), ("causal", TP, 2 * TP),
          ("phi", HALF, 2 * NE), ("scale", HALF, 1), ("image", TP, GB), ("b2r", 128, ED), ("b1s", 128, NE * HB)]

PACK_C = [("fc1", HALF, 2 * WN), ("conva", WN, CONV), ("convb", CONV, WN), ("wq", WN, WN), ("wk", WN, WN),
          ("wv", WN, WN), ("proj", NHN * VW, WN), ("fc2", WN, ED), ("bv", TP, WN), ("bfc2", TP, ED),
          ("bfc1", WN, 1), ("bconva", CONV, 1), ("bconvb", WN, 1), ("bq", WN, 1), ("bk", WN, 1), ("bproj", WN, 1),
          ("head", WN, NHN), ("router", HALF, 2 * EX), ("before", TP, TP), ("index", TP, EX), ("real", TP, T),
          ("gain", HALF, 2 * EX)]


def columns(pack):
    at, off = {}, 0
    for name, rows, cols in pack:
        at[name] = (rows, off, cols)
        off += cols
    return at, off


def after(t, k):
    return not isinstance(t, int) or t >= k


def over_tiles(eng, stages, n, unroll=2, tail=0):
    lags = max(lag for lag, _ in stages)
    head = -(-(lags + 2) // unroll) * unroll
    stop = head + (n - tail - head) // unroll * unroll

    def turn(s):
        for lag, step in stages:
            if 0 <= s - lag < n:
                step(s - lag, (s - lag) % unroll)

    for s in range(head):
        turn(s)
    with eng.Fori(head, stop - unroll + 1, unroll) as i:
        for u in range(unroll):
            for lag, step in stages:
                step(i + (u - lag), (u - lag) % unroll)
    for s in range(stop, n + lags):
        turn(s)


def tower(nc, ins, rows_out):
    with ExitStack() as ctx:
        scope = [ctx]

        def sb(name, shape, dt=F32):
            return scope[-1].enter_context(nc.sbuf_tensor(name, shape, dt))

        def open_scope():
            scope.append(ExitStack())

        def close_scope():
            scope.pop().close()

        def sem(name):
            return ctx.enter_context(nc.semaphore(name))

        bank = [ctx.enter_context(nc.psum_tensor(f"bank{i}", [128, 512], F32)) for i in range(8)]

        h = sb("h", [TP, T, ED])
        colA, nA = columns(PACK_A)
        ca = sb("ca", [128, nA])

        def of(pack, at, name):
            rows, off, cols = at[name]
            return pack[0:rows, off:off + cols]

        A = {name: of(ca, colA, name) for name in colA}
        ident = A["ident"]
        wtok = A["wtok"].rearrange("p (k e) -> p k e", k=KC)
        eps5 = sb("eps5", [128, 1])
        ones = sb("ones", [128, 128])

        tick = sb("tick", [TP, 8])
        act_tick = sb("act_tick", [128, 1])
        hst = sb("hst", [TP, T, 6])
        hmean = sb("hmean", [TP, T])
        hvar = sb("hvar", [TP, T])
        hdif = sb("hdif", [TP, T])
        hsd = sb("hsd", [TP, T])
        hrs = sb("hrs", [TP, T])
        hn = [sb(f"hn{b}", [TP, ED]) for b in range(2)]
        hnT = [sb(f"hnT{b}", [HALF, 2, TP]) for b in range(2)]

        colC, nC = columns(PACK_C)
        cc = sb("cc", [128, nC])
        Cc = {name: of(cc, colC, name) for name in colC}

        open_scope()
        colB, nB = columns(PACK_B)
        cb = sb("cb", [128, nB])
        Bc = {name: of(cb, colB, name) for name in colB}
        wqk = Bc["wqk"].rearrange("p (c n) -> p c n", c=2)
        wvg = Bc["wvg"].rearrange("p (c n) -> p c n", c=2)
        wo = Bc["wo"].rearrange("p (c n) -> p c n", c=2)
        causal = Bc["causal"].rearrange("p (c n) -> p c n", c=2)
        xy = sb("xy", [HALF, 2, NE, T * GB])
        phisq = sb("phisq", [HALF, 2, NE])
        ce = sb("ce", [TP, T, NE])
        image = Bc["image"]
        w1s = [sb(f"w1s{q}", [HALF, 2, 2, HID]) for q in range(RING // 2)]
        w2s = [sb(f"w2s{q}", [128, 2, HB, ED]) for q in range(RING // 2)]
        b1s = Bc["b1s"].rearrange("p (n j) -> p n j", n=NE)

        open_scope()
        xt = [sb(f"xt{q}", [TP, PD]) for q in range(4)]
        xT = [sb(f"xT{q}", [128, KC, TP]) for q in range(4)]
        wsums = sb("wsums", [TP, ED])
        xnm = [sb(f"xnm{b}", [TP, 1]) for b in range(2)]
        yb = [sb(f"yb{b}", [TP, ED]) for b in range(2)]
        wtok_g = sb("wtok_g", [128, KC, ED])
        tok_bias = sb("tok_bias", [TP, ED])
        pos_bias = sb("pos_bias", [TP, ED])
        xst = [sb(f"xst{b}", [TP, 2, 6]) for b in range(2)]
        xmv = [sb(f"xmv{b}", [TP, 2]) for b in range(2)]
        xsd = [sb(f"xsd{b}", [TP, 1]) for b in range(2)]
        xrs = [sb(f"xrs{b}", [TP, 1]) for b in range(2)]
        y = [sb(f"y{b}", [TP, ED]) for b in range(2)]
        yn = [sb(f"yn{b}", [TP, ED]) for b in range(2)]
        yst = [sb(f"yst{b}", [TP, 6]) for b in range(2)]
        ymv = [sb(f"ymv{b}", [TP, 2]) for b in range(2)]
        ysd = [sb(f"ysd{b}", [TP, 1]) for b in range(2)]
        yrs = [sb(f"yrs{b}", [TP, 1]) for b in range(2)]
        close_scope()

        open_scope()
        gate = sb("gate", [TP, T, ED])
        fe = [sb(f"fe{b}", [128, 4, TP]) for b in range(2)]
        fr = [sb(f"fr{b}", [128, 4, TP]) for b in range(2)]
        qk = [sb(f"qk{b}", [128, 4, TP]) for b in range(2)]
        vx = [sb(f"vx{b}", [TP, NH, DH]) for b in range(2)]
        am = [sb(f"am{b}", [TP, NH, TP]) for b in range(2)]
        den = [sb(f"den{b}", [128, 2, TP]) for b in range(2)]
        rden = [sb(f"rden{b}", [128, 2, TP]) for b in range(2)]
        oT = [sb(f"oT{b}", [128, 2, TP]) for b in range(2)]
        rg = [sb(f"rg{b}", [TP, ED]) for b in range(2)]
        close_scope()

        open_scope()
        phin = sb("phin", [HALF, 2, NE])
        phinv = sb("phinv", [HALF, NE])
        hnorm = sb("hnorm", [TP, T])
        xn = [sb(f"xn{q}", [TP, ED]) for q in range(4)]
        cneg = [sb(f"cneg{b}", [TP, 1]) for b in range(2)]
        cexp = [sb(f"cexp{b}", [TP, NE]) for b in range(2)]
        csum = [sb(f"csum{b}", [TP, 1]) for b in range(2)]
        crec = [sb(f"crec{b}", [TP, 1]) for b in range(2)]
        dmax = [sb(f"dmax{b}", [NE, GB]) for b in range(2)]
        dlog = [sb(f"dlog{b}", [NE, GB, S]) for b in range(2)]
        dexp = [sb(f"dexp{b}", [NE, GB, S]) for b in range(2)]
        dsum = [sb(f"dsum{b}", [NE, GB]) for b in range(2)]
        drec = [sb(f"drec{b}", [NE, GB]) for b in range(2)]
        dT = [sb(f"dT{b}", [128, GB, S]) for b in range(2)]
        dw = [sb(f"dw{b}", [TP, GB, NE]) for b in range(2)]

        w1s += [sb(f"w1s{q}", [HALF, 2, 2, HID]) for q in range(RING // 2, RING)]
        w2s += [sb(f"w2s{q}", [128, 2, HB, ED]) for q in range(RING // 2, RING)]
        xs = [sb(f"xs{b}", [HALF, 2, 2, B]) for b in range(2)]
        eh = [sb(f"eh{b}", [128, HB, 128]) for b in range(2)]
        eg = [sb(f"eg{b}", [128, HB, 2, B]) for b in range(2)]
        eo = [sb(f"eo{b}", [128, ED]) for b in range(2)]

        cw = [sb(f"cw{b}", [TP, GB, NE]) for b in range(2)]
        e1 = [sb(f"e1{q}", [128, ED]) for q in range(4)]
        e2 = [sb(f"e2{q}", [NE, ED]) for q in range(4)]
        c1 = [sb(f"c1{b}", [128, TP]) for b in range(2)]
        c2 = [sb(f"c2{b}", [NE, TP]) for b in range(2)]
        close_scope()
        close_scope()

        open_scope()
        zero = sb("zero", [SP_, SJ * ED])
        w13 = [sb(f"w13{b}", [HALF, 2, 2 * EH]) for b in range(2)]
        w2r = [sb(f"w2r{b}", [128, EH // 128, ED]) for b in range(2)]

        open_scope()
        masks = sb("masks", [TP, 4, KW])
        near = [sb(f"near{v}", [TP, NHN, KW]) for v in range(2)]
        bias = [sb(f"bias{v}", [TP, NHN, KW]) for v in range(4)]
        xg = sb("xg", [WN, XCOLS])
        kT = sb("kT", [WN, XCOLS])
        hp = [sb(f"hp{b}", [TP, 2, ED]) for b in range(2)]
        hpT = [sb(f"hpT{b}", [HALF, 2, PAIR]) for b in range(2)]
        fx = [sb(f"fx{b}", [WN, PAIR]) for b in range(2)]
        fa = [sb(f"fa{b}", [CONV, PAIR]) for b in range(2)]
        fs = [sb(f"fs{b}", [WN, PAIR]) for b in range(2)]
        vsrc = [sb(f"vsrc{b}", [WN, TP]) for b in range(2)]
        vn = [sb(f"vn{q}", [TP, NHN, VW]) for q in range(4)]
        vl = [sb(f"vl{i}", [TP, NHN, VW]) for i in range(3)]
        qx = [sb(f"qx{b}", [WN, NHN, TP]) for b in range(2)]
        nl = [sb(f"nl{q}", [TP, NHN, KW]) for q in range(4)]
        nm = [sb(f"nm{b}", [TP, NHN]) for b in range(2)]
        nn = [sb(f"nn{b}", [TP, NHN]) for b in range(2)]
        nsum = [sb(f"nsum{b}", [TP, NHN]) for b in range(2)]
        nr = [sb(f"nr{b}", [TP, NHN]) for b in range(2)]
        pTa = [sb(f"pTa{b}", [TP, NHN, 2, TP]) for b in range(2)]
        pTb = [sb(f"pTb{b}", [S, NHN, TP]) for b in range(2)]
        noT = [sb(f"noT{b}", [NHN * VW, TP]) for b in range(2)]
        nz = [sb(f"nz{b}", [WN, TP]) for b in range(2)]
        h2 = [sb(f"h2{b}", [TP, ED]) for b in range(2)]
        close_scope()

        open_scope()
        zk = sb("zk", [TP, T, ED])
        zsq = sb("zsq", [TP, T])
        zrt = sb("zrt", [TP, T])
        zs = sb("zs", [TP, T])
        eps6 = sb("eps6", [TP, 1])
        top = sb("top", [TP, 2, T])
        eq = sb("eq", [TP, T, EX])
        key = sb("key", [TP, T, EX])
        lg2 = sb("lg2", [TP, T, EX])
        expert = sb("expert", [TP, 2, T])
        hot = sb("hot", [TP, 2, T, EX])
        hots = sb("hots", [TP, T, EX])
        sums = [sb(f"sums{b}", [TP, T, EX]) for b in range(2)]
        place = sb("place", [TP, T, EX])
        picked = sb("picked", [TP, 2, T, EX])
        pk = sb("pk", [TP, 2, T])
        kept = sb("kept", [TP, 2, T])
        slot = sb("slot", [TP, 2, T])
        away = sb("away", [TP, 2, T])
        last_slot = sb("last_slot", [TP, 2, T])
        to = sb("to", [TP, 2, T], I32)
        frm = sb("frm", [TP, 2, T], I32)
        wexp = sb("wexp", [TP, T])
        wdif = sb("wdif", [TP, T])
        wsum = sb("wsum", [TP, T])
        wts = sb("wts", [TP, 2, T])
        own = sb("own", [TP, 2, T])
        zr = [sb(f"zr{b}", [SP_, SJ, ED]) for b in range(2)]
        zT = [sb(f"zT{b}", [HALF, 2, CAPP]) for b in range(2)]
        sg = [sb(f"sg{b}", [128, CAPP // 2]) for b in range(2)]
        hT = sb("hT", [128, EH // 128, CAPP])
        yr = [sb(f"yr{b}", [SP_, SJ, ED]) for b in range(2)]
        back = [[sb(f"back{k}{q}", [TP, ED]) for q in range(4)] for k in range(2)]
        acc = [sb(f"acc{b}", [TP, ED]) for b in range(2)]
        close_scope()
        close_scope()

        ys = nc.dram_tensor("ys", [NPAIR, 2 * B, ED], F32, kind="Internal").ap()
        ys_of = ys.rearrange("p (e m) d -> (p e) m d", e=2)

        buf = nc.dram_tensor("buf", [EX * CAPP, ED], F32, kind="Internal").ap()
        ybuf = nc.dram_tensor("ybuf", [EX * CAPP, ED], F32, kind="Internal").ap()

        buf_of = buf.rearrange("(e p j) d -> e p (j d)", e=EX, p=SP_)
        ybuf_of = ybuf.rearrange("(e p j) d -> e p (j d)", e=EX, p=SP_)

        s_cci = sem("constants_c_in")
        s_bz = sem("buffer_zeroed")
        s_nin = sem("near_tables_in")
        s_nb = sem("near_biases_ready")
        s_pad = sem("near_padding_set")
        s_f1 = sem("fc1_product")
        s_f1c = sem("fc1_biased")
        s_fA = sem("conva_product")
        s_fAc = sem("conva_biased")
        s_fB = sem("convb_product")
        s_fs = sem("convb_biased_summed")
        s_fg = sem("near_gelu")
        s_fK = sem("key_product")
        s_fKc = sem("keys_stored")
        s_fv = sem("value_source_copied")
        s_fV = sem("value_product")
        s_fVc = sem("values_stored")
        s_nQ = sem("query_product")
        s_nq = sem("queries_spread")
        s_nS = sem("near_scores")
        s_nl = sem("near_logits")
        s_nm = sem("near_maxima_negated")
        s_ne = sem("near_exp")
        s_nT = sem("near_weights_transposed")
        s_nTa = sem("near_wT_copied_act")
        s_nTd = sem("near_wT_copied_dve")
        s_nA = sem("near_av")
        s_nr = sem("near_reciprocal")
        s_nw = sem("near_weights_normalized")
        s_noc = sem("near_oT_copied")
        s_nP = sem("near_projected")
        s_nz = sem("near_projection_biased")
        s_nF = sem("fc2_product")
        s_ha = sem("h_plus_normalized")
        s_nh2 = sem("h_plus_fc2_bias")
        s_w13 = [sem(f"w13_in{b}") for b in range(2)]
        s_w2r = [sem(f"w2r_in{b}") for b in range(2)]
        s_gz = sem("z_stored")
        s_gl = sem("router_logits")
        s_r = sem("routing_steps")
        s_re = sem("routing_exp")
        s_rt = sem("routing_results")
        s_rp = sem("routing_prefix_product")
        s_sc = sem("rows_scattered")
        s_zr = [sem(f"slot_rows_in{b}") for b in range(2)]
        s_zT = sem("slot_rows_transposed")
        s_zc = [sem("zT_stored_act"), sem("zT_stored_dve")]
        s_gu = sem("gate_up_product")
        s_sg = sem("gate_silu")
        s_hT = sem("hidden_stored")
        s_yp = sem("routed_output_product")
        s_yc = [sem("routed_output_copied_act"), sem("routed_output_copied_dve")]
        s_eo = [sem(f"expert_output_out{b}") for b in range(2)]
        n_eo = 16 * NPAIR // 2
        s_g = [sem(f"rows_gathered{q}") for q in range(4)]
        s_o1 = sem("output_steps")
        s_o = sem("output_ready")

        s_ph = sem("norm_constants_steps")
        s_phn = sem("phi_norms")
        s_phs = sem("phi_norm_roots")
        s_cns = sem("dispatch_norm_roots")
        s_cl = sem("dispatch_logits")
        s_ccm = sem("combine_max")
        s_cce = sem("combine_exp")
        s_ccr = sem("combine_reciprocal")
        s_ccw = sem("combine_weights")
        s_cdm = sem("dispatch_max")
        s_cdl = sem("dispatch_shifted")
        s_cde = sem("dispatch_exp")
        s_cds = sem("dispatch_sum_steps")
        s_cdT = sem("dispatch_weights_T")
        s_cdt = sem("dispatch_weights_transposed")
        s_cdw = sem("dispatch_weights_spread")
        s_cxs = sem("expert_input_product")
        s_cxc = sem("expert_input_stored")
        s_w1 = [sem(f"w1_in_then_expert_rows_in{q}") for q in range(RING)]
        n_w1 = 16 * NPAIR // RING
        s_w2 = [sem(f"w2_in{q}") for q in range(RING)]
        s_dx = sem("expert_inputs_staged")
        s_dh = sem("expert_hidden_product")
        s_dc = [sem("expert_hidden_copied_act"), sem("expert_hidden_copied_dve")]
        s_dt = sem("expert_hidden_transposed")
        s_db = sem("expert_hidden_biased")
        s_dg = sem("expert_hidden_gelu")
        s_dy = sem("expert_output_product")
        s_do = sem("expert_output_stored")
        s_eb = sem("expert_outputs_biased")
        s_ecw = sem("combine_weights_spread")
        s_eT = sem("combine_transposed")
        s_eTa = sem("combine_copied_act")
        s_eTd = sem("combine_copied_dve")
        s_ey = sem("combine_product")

        s_ln = sem("ln_constants_steps")
        s_cbi = sem("constants_b_in")
        s_hst = sem("h_stats")
        s_hsd = sem("h_std")
        s_hn = sem("h_normalized")
        s_hTr = sem("h_transposed")
        s_hTc = sem("hT_copied")
        s_bqk = sem("attn_qk_product")
        s_bvg = sem("attn_vg_product")
        s_bf = sem("attn_exp_relu")
        s_bq = sem("attn_qk_features")
        s_bv = sem("attn_v_gate")
        s_bs = sem("attn_scores")
        s_bam = sem("attn_scores_masked")
        s_bav = sem("attn_av")
        s_bd = sem("attn_den_steps")
        s_bon = sem("attn_out_normalized")
        s_bwo = sem("attn_projected")
        s_brg = sem("attn_gated")

        s_ca = sem("constants_a_in")
        s_eps = sem("eps_set")
        s_wg = sem("wtok_scaled")
        s_cb = sem("tok_bias_product")
        s_tb = sem("tok_bias_ready")
        s_pb = sem("pos_bias_ready")
        s_x = [sem(f"x_in_then_output_out{q}") for q in range(4)]
        n_x = 16 * -(-T // 4)
        s_xr = [sem(f"xT_in{q}") for q in range(4)]
        s_xsh = sem("y_shift_steps")
        s_xst = sem("x_stats")
        s_xmv = sem("x_mean_var")
        s_xsd = sem("x_std")
        s_xrs = sem("x_rstd")
        s_typ = sem("y_product")
        s_y = sem("y_biased")
        s_yst = sem("y_stats")
        s_ymv = sem("y_mean_var")
        s_ysd = sem("y_std")
        s_yrs = sem("y_rstd")
        s_yn = sem("y_normalized")
        s_yg = sem("y_gained")
        s_h = sem("h_updated")

        def embed_sp(sp):
            sp.dma_start(ca[:], ins["ca"]).then_inc(s_ca, 16)

            def load_x(t, q):
                if after(t, 4):
                    sp.wait_ge(s_xst, t - 3)
                sp.dma_start(xt[q][:], ins["x"][t]).then_inc(s_x[q], 16)
                if after(t, 4):
                    sp.wait_ge(s_typ, t - 3)
                sp.dma_start(xT[q][:], ins["xT"][t]).then_inc(s_xr[q], 16)

            over_tiles(sp, [(0, load_x)], T, unroll=4)
            sp.dma_start(cb[:], ins["cb"]).then_inc(s_cbi, 16)
            sp.dma_start(cc[:], ins["cc"]).then_inc(s_cci, 16)

        def embed_pool(pool):
            nc.gpsimd.memset(eps5[:], 1e-5)
            nc.gpsimd.memset(ones[:], 1.0).then_inc(s_eps, 1)

            def gain(t, b):
                pool.wait_ge(s_yn, t + 1)
                pool.wait_ge(s_pb, 2)
                nc.gpsimd.tensor_tensor(yn[b][:], yn[b][:], A["g2m"], ALU.mult).then_inc(s_yg, 1)
                pool.wait_ge(s_yg, t + 1)
                nc.gpsimd.tensor_tensor(h[:, t, :], yn[b][:], pos_bias[:], ALU.add).then_inc(s_h, 1)

            over_tiles(pool, [(0, gain)], T)

        def h_std(act, layer):
            act.wait_ge(s_ln, 5 * layer + 4)
            nc.scalar.activation(hsd[:], hvar[:], ACT.Sqrt, bias=eps5[0:TP, :]).then_inc(s_hsd, 1)

        def h_norm_constants(dve, layer):
            n0 = 5 * layer
            dve.wait_ge(s_hst, T * (layer + 1))
            nc.vector.tensor_tensor(hmean[:], hst[:, :, 1], hst[:, :, 4], ALU.add)
            nc.vector.tensor_tensor(hdif[:], hst[:, :, 1], hst[:, :, 4], ALU.subtract)
            nc.vector.tensor_tensor(hvar[:], hst[:, :, 2], hst[:, :, 5], ALU.add).then_inc(s_ln, 1)
            dve.wait_ge(s_ln, n0 + 1)
            nc.vector.tensor_scalar(hmean[:], hmean[:], 0.5, None, ALU.mult)
            nc.vector.tensor_scalar(hvar[:], hvar[:], 1.0 / ED, None, ALU.mult)
            nc.vector.scalar_tensor_tensor(out=hdif[:], in0=hdif[:], scalar=0.25, in1=hdif[:], op0=ALU.mult, op1=ALU.mult).then_inc(s_ln, 2)
            dve.wait_ge(s_ln, n0 + 3)
            nc.vector.tensor_tensor(hvar[:], hvar[:], hdif[:], ALU.add).then_inc(s_ln, 1)
            dve.wait_ge(s_hsd, layer + 1)
            nc.vector.reciprocal(hrs[:], hsd[:]).then_inc(s_ln, 1)

        def attention_act(act):
            h_std(act, 0)

            def copy_hT(t, b):
                act.wait_ge(s_hTr, t + 1)
                if after(t, 2):
                    act.wait_ge(s_bvg, t - 1)
                nc.scalar.copy(hnT[b][:], bank[0][0:HALF, 0:2 * TP].rearrange("p (c q) -> p c q", c=2)).then_inc(s_hTc, 1)

            def features(t, b):
                act.wait_ge(s_bqk, t + 1)
                if after(t, 2):
                    act.wait_ge(s_bq, t - 1)
                p = bank[1][:, 0:4 * TP].rearrange("p (c q) -> p c q", c=4)
                nc.scalar.activation(fe[b][:], p, ACT.Exp)
                nc.scalar.activation(fr[b][:], p, ACT.Relu).then_inc(s_bf, 1)

            def values(t, b):
                act.wait_ge(s_bvg, t + 1)
                if after(t, 2):
                    act.wait_ge(s_bav, t - 1)
                nc.scalar.activation(gate[:, t, :], bank[2][0:TP, NH * DH:VGW], ACT.Tanh, scale=0.5)
                nc.scalar.copy(vx[b][:], bank[2][0:TP, 0:NH * DH].rearrange("p (h d) -> p h d", h=NH)).then_inc(s_bv, 1)

            over_tiles(act, [(0, copy_hT), (1, features), (1, values)], T)

        def embed_act(act):
            act.wait_ge(s_eps, 1)

            def std_x(t, b):
                act.wait_ge(s_xmv, t + 1)
                if after(t, 2):
                    act.wait_ge(s_xrs, t - 1)
                nc.scalar.activation(xsd[b][:], xmv[b][:, 1:2], ACT.Sqrt, bias=eps5[0:TP, :]).then_inc(s_xsd, 1)

            def std_y(t, b):
                act.wait_ge(s_ymv, t + 1)
                if after(t, 2):
                    act.wait_ge(s_yrs, t - 1)
                nc.scalar.activation(ysd[b][:], ymv[b][:, 1:2], ACT.Sqrt, bias=eps5[0:TP, :]).then_inc(s_ysd, 1)

            over_tiles(act, [(0, std_x), (2, std_y)], T)

        def embed_dve(dve):
            dve.wait_ge(s_ca, 16)
            for k in range(KC):
                last = nc.vector.tensor_scalar(wtok_g[:, k, :], wtok[:, k, :], A["g1"][:, k:k + 1], None, ALU.mult)
            last.then_inc(s_wg, 1)
            nc.vector.tensor_tensor(pos_bias[:], A["pos"], A["b2m"], ALU.add).then_inc(s_pb, 1)
            dve.wait_ge(s_pb, 1)
            nc.vector.tensor_tensor(pos_bias[:], pos_bias[:], A["cls"], ALU.add).then_inc(s_pb, 1)
            dve.wait_ge(s_cb, 2)
            nc.vector.tensor_copy(wsums[:], bank[6][0:TP, 0:ED])
            nc.vector.tensor_tensor(tok_bias[:], A["btok"], bank[7][0:TP, 0:ED], ALU.add).then_inc(s_tb, 1)
            dve.wait_ge(s_tb, 1)

            def stats_x(t, q):
                b = q % 2
                dve.wait_ge(s_x[q], (t - q) * 4 + 16)
                if after(t, 2):
                    dve.wait_ge(s_xmv, t - 1)
                nc.vector.bn_stats(xst[b][:, 0, :], xt[q][:, 0:PD // 2])
                nc.vector.bn_stats(xst[b][:, 1, :], xt[q][:, PD // 2:PD]).then_inc(s_xst, 1)
                dve.wait_ge(s_xst, t + 1)
                nc.vector.memset(tick[:, 4:5], 0.0)
                nc.vector.bn_aggr(xmv[b][:], xst[b][:]).then_inc(s_xmv, 1)

            def shift(t, q):
                b = q % 2
                dve.wait_ge(s_xsd, t + 1)
                nc.vector.reciprocal(xrs[b][:], xsd[b][:]).then_inc(s_xrs, 1)
                dve.wait_ge(s_xrs, t + 1)
                nc.vector.scalar_tensor_tensor(out=xnm[b][:], in0=xmv[b][:, 0:1], scalar=-1.0, in1=xrs[b][:], op0=ALU.mult, op1=ALU.mult).then_inc(s_xsh, 1)
                dve.wait_ge(s_xsh, 2 * t + 1)
                nc.vector.scalar_tensor_tensor(out=yb[b][:], in0=wsums[:], scalar=xnm[b][:], in1=tok_bias[:], op0=ALU.mult, op1=ALU.add).then_inc(s_xsh, 1)

            def bias_y(t, q):
                b = q % 2
                dve.wait_ge(s_typ, t + 1)
                dve.wait_ge(s_xsh, 2 * t + 2)
                if after(t, 2):
                    dve.wait_ge(s_yn, t - 1)
                nc.vector.scalar_tensor_tensor(out=y[b][:], in0=bank[2 + b][0:TP, 0:ED], scalar=xrs[b][:], in1=yb[b][:], op0=ALU.mult, op1=ALU.add).then_inc(s_y, 1)
                dve.wait_ge(s_y, t + 1)
                nc.vector.bn_stats(yst[b][:], y[b][:]).then_inc(s_yst, 1)
                dve.wait_ge(s_yst, t + 1)
                nc.vector.memset(tick[:, 5:6], 0.0)
                nc.vector.bn_aggr(ymv[b][:], yst[b][:]).then_inc(s_ymv, 1)

            def norm_y(t, q):
                b = q % 2
                dve.wait_ge(s_ysd, t + 1)
                nc.vector.reciprocal(yrs[b][:], ysd[b][:]).then_inc(s_yrs, 1)
                dve.wait_ge(s_yrs, t + 1)
                if after(t, 2):
                    dve.wait_ge(s_h, t - 1)
                nc.vector.tensor_scalar(yn[b][:], y[b][:], ymv[b][:, 0:1], yrs[b][:], ALU.subtract, ALU.mult).then_inc(s_yn, 1)

            def stats_h(t, b):
                dve.wait_ge(s_h, t + 1)
                nc.vector.bn_stats(hst[:, t, :], h[:, t, :]).then_inc(s_hst, 1)

            over_tiles(dve, [(0, stats_x), (1, shift), (2, bias_y), (3, norm_y), (4, stats_h)], T, unroll=4)

        def attention_dve(dve):
            h_norm_constants(dve, 0)
            dve.wait_ge(s_ln, 5)
            dve.wait_ge(s_cbi, 16)
            phi = Bc["phi"].rearrange("p (c n) -> p c n", c=2)
            nc.vector.tensor_tensor(phisq[:], phi, phi, ALU.mult).then_inc(s_ph, 1)

            def normalize(t, b):
                if after(t, 2):
                    dve.wait_ge(s_hTr, t - 1)
                nc.vector.tensor_scalar(hn[b][:], h[:, t, :], hmean[:, bass.ds(t, 1)], hrs[:, bass.ds(t, 1)], ALU.subtract, ALU.mult).then_inc(s_hn, 1)

            def feature(t, b):
                dve.wait_ge(s_bf, t + 1)
                if after(t, 2):
                    dve.wait_ge(s_bs, t - 1)
                nc.vector.scalar_tensor_tensor(out=qk[b][:], in0=fe[b][:], scalar=1.0, in1=fr[b][:], op0=ALU.min, op1=ALU.add).then_inc(s_bq, 1)

            def mask(t, b):
                dve.wait_ge(s_bs, t + 1)
                if after(t, 2):
                    dve.wait_ge(s_bav, t - 1)
                for half in range(2):
                    last = nc.vector.tensor_tensor(am[b][:, 2 * half:2 * half + 2, :], bank[3 + half][0:TP, 0:2 * TP].rearrange("p (c q) -> p c q", c=2), causal, ALU.mult)
                last.then_inc(s_bam, 1)

            def normalize_out(t, b):
                dve.wait_ge(s_bav, t + 1)
                nc.vector.tensor_scalar(den[b][:], bank[6][:, 0:2 * TP].rearrange("p (j q) -> p j q", j=2), 1e-6, None, ALU.max).then_inc(s_bd, 1)
                dve.wait_ge(s_bd, 2 * t + 1)
                nc.vector.reciprocal(rden[b][:], den[b][:]).then_inc(s_bd, 1)
                dve.wait_ge(s_bd, 2 * t + 2)
                if after(t, 2):
                    dve.wait_ge(s_bwo, t - 1)
                nc.vector.tensor_tensor(oT[b][:], bank[5][:, 0:2 * TP].rearrange("p (j q) -> p j q", j=2), rden[b][:], ALU.mult).then_inc(s_bon, 1)

            def residual(t, b):
                dve.wait_ge(s_bwo, t + 1)
                nc.vector.scalar_tensor_tensor(out=rg[b][:], in0=gate[:, t, :], scalar=1.0, in1=bank[7][0:TP, 0:ED], op0=ALU.add, op1=ALU.mult).then_inc(s_brg, 1)
                dve.wait_ge(s_brg, t + 1)
                nc.vector.scalar_tensor_tensor(out=h[:, t, :], in0=rg[b][:], scalar=0.5, in1=h[:, t, :], op0=ALU.mult, op1=ALU.add).then_inc(s_h, 1)
                dve.wait_ge(s_h, T + t + 1)
                nc.vector.bn_stats(hst[:, t, :], h[:, t, :]).then_inc(s_hst, 1)

            over_tiles(dve, [(0, normalize), (3, mask), (2, feature), (4, residual), (3, normalize_out)], T)

        def embed_pe(pe):
            pe.wait_ge(s_ca, 16)
            for k in range(KC):
                last = nc.tensor.matmul(bank[7][0:TP, 0:ED], A["b1"][:, k:k + 1].to_broadcast([128, TP]), wtok[:, k, :],
                                        start=(k == 0), stop=(k == KC - 1))
            last.then_inc(s_cb, 1)
            pe.wait_ge(s_wg, 1)
            pe.wait_ge(s_eps, 1)
            for k in range(KC):
                last = nc.tensor.matmul(bank[6][0:TP, 0:ED], ones[:, 0:TP], wtok_g[:, k, :], start=(k == 0), stop=(k == KC - 1))
            last.then_inc(s_cb, 1)

            def product(t, q):
                pe.wait_ge(s_xr[q], (t - q) * 4 + 16)
                if after(t, 2):
                    pe.wait_ge(s_y, t - 1)
                for k in range(KC):
                    last = nc.tensor.matmul(bank[2 + q % 2][0:TP, 0:ED], xT[q][:, k, :], wtok_g[:, k, :], start=(k == 0), stop=(k == KC - 1))
                last.then_inc(s_typ, 1)

            over_tiles(pe, [(0, product)], T, unroll=4)

        def attention_pe(pe):
            pe.wait_ge(s_cbi, 16)

            def transpose_h(t, b):
                pe.wait_ge(s_hn, t + 1)
                if after(t, 1):
                    pe.wait_ge(s_hTc, t)
                for c in range(2):
                    last = nc.tensor.transpose(bank[0][0:HALF, c * TP:(c + 1) * TP], hn[b][:, c * HALF:(c + 1) * HALF], ident[0:TP, 0:TP])
                last.then_inc(s_hTr, 1)

            def products(t, b):
                pe.wait_ge(s_hTc, t + 1)
                if after(t, 1):
                    pe.wait_ge(s_bf, t)
                for j in range(4):
                    for c in range(2):
                        last = nc.tensor.matmul(bank[1][:, j * TP:(j + 1) * TP], wqk[:, c, j * 128:(j + 1) * 128], hnT[b][:, c, :], start=(c == 0), stop=(c == 1))
                last.then_inc(s_bqk, 1)
                if after(t, 1):
                    pe.wait_ge(s_bv, t)
                for c in range(2):
                    last = nc.tensor.matmul(bank[2][0:TP, 0:VGW], hnT[b][:, c, :], wvg[:, c, :], start=(c == 0), stop=(c == 1))
                last.then_inc(s_bvg, 1)

            def scores(t, b):
                pe.wait_ge(s_bq, t + 1)
                if after(t, 1):
                    pe.wait_ge(s_bam, t)
                for j in range(2):
                    for r in range(2):
                        last = nc.tensor.matmul(bank[3 + r][0:TP, j * TP:(j + 1) * TP], qk[b][64 * r:64 * r + 64, 2 + j, :], qk[b][64 * r:64 * r + 64, j, :], start=True, stop=True)
                last.then_inc(s_bs, 1)

            def values(t, b):
                pe.wait_ge(s_bam, t + 1)
                pe.wait_ge(s_bv, t + 1)
                if after(t, 1):
                    pe.wait_ge(s_bon, t)
                for j in range(2):
                    for r in range(2):
                        half = slice(64 * r, 64 * r + 64)
                        nc.tensor.matmul(bank[5][half, j * TP:(j + 1) * TP], vx[b][:, 2 * j + r, :], am[b][:, 2 * r + j, :], start=True, stop=True)
                for r in range(2):
                    last = nc.tensor.matmul(bank[6][64 * r:64 * r + 64, 0:2 * TP], ones[0:TP, 0:64], am[b][:, 2 * r:2 * r + 2, :].rearrange("p j q -> p (j q)"), start=True, stop=True)
                last.then_inc(s_bav, 1)

            def project(t, b):
                pe.wait_ge(s_bon, t + 1)
                if after(t, 1):
                    pe.wait_ge(s_brg, t)
                for j in range(2):
                    last = nc.tensor.matmul(bank[7][0:TP, 0:ED], oT[b][:, j, :], wo[:, j, :], start=(j == 0), stop=(j == 1))
                last.then_inc(s_bwo, 1)

            over_tiles(pe, [(0, transpose_h), (2, scores), (1, products), (3, project), (2, values)], T)

        def dispatch_act(act):
            act.wait_ge(s_phn, 1)
            nc.scalar.activation(phinv[:], bank[7][0:HALF, 0:NE], ACT.Sqrt).then_inc(s_phs, 1)
            h_std(act, 1)
            act.wait_ge(s_ln, 5 + 4)
            nc.scalar.activation(hnorm[:], hvar[:], ACT.Sqrt, scale=float(ED)).then_inc(s_cns, 1)

            def copy_T(t, q):
                b = q % 2
                act.wait_ge(s_hTr, T + t + 1)
                if after(t, 2):
                    act.wait_ge(s_cl, t - 1)
                nc.scalar.copy(hnT[b][:], bank[0][0:HALF, 0:2 * TP].rearrange("p (c q) -> p c q", c=2)).then_inc(s_hTc, 1)

            def exps(t, q):
                b = q % 2
                act.wait_ge(s_ccm, t + 1)
                if after(t, 2):
                    act.wait_ge(s_ccw, t - 1)
                nc.scalar.activation(cexp[b][:], bank[1][0:TP, 0:NE], ACT.Exp, bias=cneg[b][:], accum_out=csum[b][:]).then_inc(s_cce, 1)
                act.wait_ge(s_cdl, t + 1)
                nc.scalar.activation(dexp[b][:], dlog[b][:], ACT.Exp).then_inc(s_cde, 1)

            def store(t, q):
                b = q % 2
                act.wait_ge(s_cxs, t + 1)
                p = bank[4][0:HALF, 0:2 * GB * NE].rearrange("p (c g n) -> p c g n", c=2, g=GB)
                for c in range(2):
                    last = nc.scalar.copy(xy[:, c, :, bass.ds(t * GB, GB)].rearrange("p n g -> p g n"), p[:, c])
                last.then_inc(s_cxc, 1)

            over_tiles(act, [(0, copy_T), (1, exps), (3, store)], T, unroll=4)

        def dispatch_dve(dve):
            dve.wait_ge(s_phs, 1)
            nc.vector.tensor_scalar(phinv[:], phinv[:], 1e-12, None, ALU.max).then_inc(s_ph, 1)
            dve.wait_ge(s_ph, 2)
            nc.vector.reciprocal(phinv[:], phinv[:]).then_inc(s_ph, 1)
            dve.wait_ge(s_ph, 3)
            nc.vector.tensor_scalar(phinv[:], phinv[:], Bc["scale"], None, ALU.mult).then_inc(s_ph, 1)
            dve.wait_ge(s_ph, 4)
            for b in range(2):
                nc.vector.memset(dT[b][NE:128], 0.0)
            nc.vector.tensor_tensor(phin[:], Bc["phi"].rearrange("p (c n) -> p c n", c=2), phinv[:].unsqueeze(1).to_broadcast([HALF, 2, NE]), ALU.mult).then_inc(s_ph, 1)
            h_norm_constants(dve, 1)
            dve.wait_ge(s_ln, 10)
            dve.wait_ge(s_cns, 1)
            nc.vector.tensor_tensor(hnorm[:], hnorm[:], hrs[:], ALU.mult).then_inc(s_ph, 1)
            dve.wait_ge(s_ph, 6)
            nc.vector.tensor_scalar(hnorm[:], hnorm[:], 1e-12, None, ALU.max).then_inc(s_ph, 1)
            dve.wait_ge(s_ph, 7)
            nc.vector.reciprocal(hnorm[:], hnorm[:]).then_inc(s_ph, 1)
            dve.wait_ge(s_ph, 8)
            nc.vector.tensor_tensor(hnorm[:], hnorm[:], hrs[:], ALU.mult).then_inc(s_ph, 1)
            dve.wait_ge(s_ph, 9)

            def normalize(t, q):
                b = q % 2
                if after(t, 4):
                    dve.wait_ge(s_cxs, t - 3)
                nc.vector.tensor_scalar(xn[q][:], h[:, t, :], hmean[:, bass.ds(t, 1)], hnorm[:, bass.ds(t, 1)], ALU.subtract, ALU.mult).then_inc(s_hn, 1)

            def maxima(t, q):
                b = q % 2
                dve.wait_ge(s_cl, t + 1)
                if after(t, 2):
                    dve.wait_ge(s_cce, t - 1)
                nc.vector.tensor_reduce(cneg[b][:], bank[1][0:TP, 0:NE], AX.X, ALU.max, negate=True).then_inc(s_ccm, 1)
                p = bank[2][0:NE, 0:TP].rearrange("p (g m) -> p g m", g=GB)
                nc.vector.tensor_reduce(dmax[b][:], p, AX.X, ALU.max).then_inc(s_cdm, 1)
                dve.wait_ge(s_cdm, t + 1)
                if after(t, 2):
                    dve.wait_ge(s_cde, t - 1)
                nc.vector.tensor_tensor(dlog[b][:], p, dmax[b][:].unsqueeze(2).to_broadcast([NE, GB, S]), ALU.subtract).then_inc(s_cdl, 1)

            def weights(t, q):
                b = q % 2
                dve.wait_ge(s_cce, t + 1)
                nc.vector.reciprocal(crec[b][:], csum[b][:]).then_inc(s_ccr, 1)
                dve.wait_ge(s_cde, t + 1)
                nc.vector.tensor_reduce(dsum[b][:], dexp[b][:], AX.X, ALU.add).then_inc(s_cds, 1)
                dve.wait_ge(s_ccr, t + 1)
                nc.vector.tensor_scalar(ce[:, t, :], cexp[b][:], crec[b][:], None, ALU.mult).then_inc(s_ccw, 1)
                dve.wait_ge(s_cds, 2 * t + 1)
                nc.vector.reciprocal(drec[b][:], dsum[b][:]).then_inc(s_cds, 1)
                dve.wait_ge(s_cds, 2 * t + 2)
                if after(t, 2):
                    dve.wait_ge(s_cdt, t - 1)
                nc.vector.tensor_tensor(dT[b][0:NE], dexp[b][:], drec[b][:].unsqueeze(2).to_broadcast([NE, GB, S]), ALU.mult).then_inc(s_cdT, 1)

            def spread(t, q):
                b = q % 2
                dve.wait_ge(s_cdt, t + 1)
                if after(t, 2):
                    dve.wait_ge(s_cxs, t - 1)
                nc.vector.tensor_tensor(dw[b][:], bank[3][0:TP, 0:NE].unsqueeze(1).to_broadcast([TP, GB, NE]), image.unsqueeze(2).to_broadcast([TP, GB, NE]), ALU.mult).then_inc(s_cdw, 1)

            over_tiles(dve, [(0, normalize), (3, spread), (1, maxima), (1, weights)], T, unroll=4)

        def dispatch_pe(pe):
            pe.wait_ge(s_ph, 1)
            pe.wait_ge(s_brg, T)
            for c in range(2):
                last = nc.tensor.matmul(bank[7][0:HALF, 0:NE], ones[0:HALF, 0:HALF], phisq[:, c, :], start=(c == 0), stop=(c == 1))
            last.then_inc(s_phn, 1)
            pe.wait_ge(s_ph, 5)

            def transpose_x(t, q):
                b = q % 2
                pe.wait_ge(s_hn, T + t + 1)
                if after(t, 1):
                    pe.wait_ge(s_hTc, T + t)
                for c in range(2):
                    last = nc.tensor.transpose(bank[0][0:HALF, c * TP:(c + 1) * TP], xn[q][:, c * HALF:(c + 1) * HALF], ident[0:TP, 0:TP])
                last.then_inc(s_hTr, 1)

            def logits(t, q):
                b = q % 2
                pe.wait_ge(s_hTc, T + t + 1)
                if after(t, 1):
                    pe.wait_ge(s_cce, t)
                    pe.wait_ge(s_cdl, t)
                for c in range(2):
                    nc.tensor.matmul(bank[1][0:TP, 0:NE], hnT[b][:, c, :], phin[:, c, :], start=(c == 0), stop=(c == 1))
                for c in range(2):
                    last = nc.tensor.matmul(bank[2][0:NE, 0:TP], phin[:, c, :], hnT[b][:, c, :], start=(c == 0), stop=(c == 1))
                last.then_inc(s_cl, 1)

            def transpose_d(t, q):
                b = q % 2
                pe.wait_ge(s_cdT, t + 1)
                if after(t, 1):
                    pe.wait_ge(s_cdw, t)
                nc.tensor.transpose(bank[3][0:TP, 0:128], dT[b][:].rearrange("p g m -> p (g m)"), ident).then_inc(s_cdt, 1)

            def inputs(t, q):
                b = q % 2
                pe.wait_ge(s_cdw, t + 1)
                if after(t, 1):
                    pe.wait_ge(s_cxc, t)
                for c in range(2):
                    last = nc.tensor.matmul(bank[4][0:HALF, c * GB * NE:(c + 1) * GB * NE], xn[q][:, c * HALF:(c + 1) * HALF], dw[b][:].rearrange("p g n -> p (g n)"), start=True, stop=True)
                last.then_inc(s_cxs, 1)

            over_tiles(pe, [(1, logits), (0, transpose_x), (3, inputs), (2, transpose_d)], T, unroll=4)

        def experts_sp(sp):
            def load(p, q):
                if isinstance(p, int) and p == RING // 2:
                    sp.wait_ge(s_h, 2 * T)
                if after(p, RING):
                    sp.wait_ge(s_dh, p - RING + 1)
                sp.dma_start(w1s[q][:], ins["w1"][p]).then_inc(s_w1[q], 16)
                if after(p, RING):
                    sp.wait_ge(s_dy, p - RING + 1)
                sp.dma_start(w2s[q][:], ins["w2"][p]).then_inc(s_w2[q], 16)

            def store(p, q):
                b = q % 2
                sp.wait_ge(s_do, p + 1)
                sp.dma_start(ys[p], eo[b][:]).then_inc(s_eo[b], 16)

            over_tiles(sp, [(0, load), (RING, store)], NPAIR, unroll=RING)

        def experts_pool(pool):
            pool.wait_ge(s_cxc, T)

            def stage(p, q):
                b = q % 2
                if after(p, 2):
                    pool.wait_ge(s_dh, p - 1)
                nc.gpsimd.tensor_copy(xs[b][:], xy[:, :, bass.ds(2 * p, 2), 0:B]).then_inc(s_dx, 1)

            over_tiles(pool, [(0, stage)], NPAIR, unroll=RING)

        def experts_act(act):
            def copy_h(p, q):
                b = q % 2
                act.wait_ge(s_dh, p + 1)
                if after(p, 2):
                    act.wait_ge(s_dt, p - 1)
                nc.scalar.copy(eh[b][:, 0:HB // 2], hidden_bank(b, 0)).then_inc(s_dc[0], 1)

            def gelu(p, q):
                b = q % 2
                act.wait_ge(s_db, p + 1)
                nc.scalar.activation(eg[b][:], eg[b][:], ACT.Gelu).then_inc(s_dg, 1)

            def output(p, q):
                b = q % 2
                act.wait_ge(s_dy, p + 1)
                if after(p, 2):
                    act.wait_ge(s_eo[b], 8 * (p - b))
                nc.scalar.copy(eo[b][:], bank[6 + b][:, 0:ED]).then_inc(s_do, 1)

            over_tiles(act, [(0, copy_h), (1, gelu), (2, output)], NPAIR, unroll=RING)

        def hidden_bank(b, part):
            return bank[2 * b + part][:, 0:HB // 2 * 128].rearrange("p (j k) -> p j k", j=HB // 2)

        def experts_dve(dve):
            def copy_h(p, q):
                b = q % 2
                dve.wait_ge(s_dh, p + 1)
                if after(p, 2):
                    dve.wait_ge(s_dt, p - 1)
                nc.vector.tensor_copy(eh[b][:, HB // 2:HB], hidden_bank(b, 1)).then_inc(s_dc[1], 1)

            def bias(p, q):
                b = q % 2
                dve.wait_ge(s_dt, p + 1)
                if after(p, 2):
                    dve.wait_ge(s_dy, p - 1)
                for g in range(2):
                    js = slice(g * HB // 2, (g + 1) * HB // 2)
                    h4 = bank[4 + g][:, 0:HB // 2 * 128].rearrange("p (j e m) -> p j e m", j=HB // 2, e=2)
                    b4 = b1s[:, bass.ds(2 * p, 2), js].rearrange("p e j -> p j e").unsqueeze(3).to_broadcast([128, HB // 2, 2, B])
                    last = nc.vector.tensor_tensor(eg[b][:, js], h4, b4, ALU.add)
                last.then_inc(s_db, 1)

            over_tiles(dve, [(0, copy_h), (1, bias)], NPAIR, unroll=RING)

        def experts_pe(pe):
            pe.wait_ge(s_cxc, T)

            def hidden(p, q):
                b = q % 2
                pe.wait_ge(s_w1[q], 16 // RING * (p - q) + 16)
                pe.wait_ge(s_dx, p + 1)
                if after(p, 2):
                    pe.wait_ge(s_dc[0], p - 1)
                    pe.wait_ge(s_dc[1], p - 1)
                for part in range(2):
                    cols = slice(part * HID // 2, (part + 1) * HID // 2)
                    for c in range(2):
                        for e in range(2):
                            last = nc.tensor.matmul(bank[2 * b + part][e * B:(e + 1) * B, 0:HID // 2], xs[b][:, c, e, :], w1s[q][:, e, c, cols], start=(c == 0), stop=(c == 1))
                last.then_inc(s_dh, 1)

            def transposes(p, q):
                b = q % 2
                pe.wait_ge(s_dc[0], p + 1)
                pe.wait_ge(s_dc[1], p + 1)
                if after(p, 1):
                    pe.wait_ge(s_db, p)
                for j in range(HB):
                    k = j % (HB // 2) * 128
                    last = nc.tensor.transpose(bank[4 + j // (HB // 2)][:, k:k + 128], eh[b][:, j, :], ident)
                last.then_inc(s_dt, 1)

            def output(p, q):
                b = q % 2
                pe.wait_ge(s_w2[q], 16 // RING * (p - q) + 16)
                pe.wait_ge(s_dg, p + 1)
                if after(p, 2):
                    pe.wait_ge(s_do, p - 1)
                for j in range(HB):
                    for e in range(2):
                        last = nc.tensor.matmul(bank[6 + b][e * B:(e + 1) * B, 0:ED], eg[b][:, j, e, :], w2s[q][:, e, j, :], start=(j == 0), stop=(j == HB - 1))
                last.then_inc(s_dy, 1)

            over_tiles(pe, [(0, hidden), (1, transposes), (2, output)], NPAIR, unroll=RING)

        def combine_sp(sp):
            for b in range(2):
                sp.wait_ge(s_eo[b], 16 * NPAIR // 2)

            def load(t, q):
                if after(t, 4):
                    sp.wait_ge(s_ey, t - 3)
                m = t * GB
                sp.dma_start(e1[q][0:NE], ys_of[:, bass.ds(m, 1), :]).then_inc(s_w1[q], 16)
                if not (isinstance(t, int) and t == T - 1):
                    sp.dma_start(e1[q][NE:2 * NE], ys_of[:, bass.ds(m + 1, 1), :]).then_inc(s_w1[q], 16)
                    sp.dma_start(e2[q][:], ys_of[:, bass.ds(m + 2, 1), :]).then_inc(s_w1[q], 16)

            over_tiles(sp, [(0, load)], T, unroll=4, tail=1)

        def combine_pool(pool):
            def bias(t, q):
                pool.wait_ge(s_w1[q], 12 * (t - q) + n_w1 + (48 if not (isinstance(t, int) and t == T - 1) else 16))
                nc.gpsimd.tensor_tensor(e1[q][:], e1[q][:], Bc["b2r"], ALU.add)
                nc.gpsimd.tensor_tensor(e2[q][:], e2[q][:], Bc["b2r"][0:NE], ALU.add).then_inc(s_eb, 1)

            over_tiles(pool, [(0, bias)], T, unroll=4, tail=1)

        def combine_act(act):
            def copy(t, b):
                act.wait_ge(s_eT, t + 1)
                if after(t, 2):
                    act.wait_ge(s_ey, t - 1)
                nc.scalar.copy(c1[b][:], bank[6][:, 0:TP]).then_inc(s_eTa, 1)

            over_tiles(act, [(0, copy)], T)

        def combine_dve(dve):
            def spread(t, b):
                if after(t, 2):
                    dve.wait_ge(s_eT, t - 1)
                nc.vector.tensor_tensor(cw[b][:], ce[:, t, :].unsqueeze(1).to_broadcast([TP, GB, NE]), image.unsqueeze(2).to_broadcast([TP, GB, NE]), ALU.mult).then_inc(s_ecw, 1)

            def copy(t, b):
                dve.wait_ge(s_eT, t + 1)
                if after(t, 2):
                    dve.wait_ge(s_ey, t - 1)
                nc.vector.tensor_copy(c2[b][:], bank[7][0:NE, 0:TP]).then_inc(s_eTd, 1)

            def residual(t, b):
                dve.wait_ge(s_ey, t + 1)
                nc.vector.tensor_tensor(h[:, t, :], h[:, t, :], bank[b][0:TP, 0:ED], ALU.add).then_inc(s_h, 1)
                dve.wait_ge(s_h, 2 * T + t + 1)
                nc.vector.bn_stats(hst[:, t, :], h[:, t, :]).then_inc(s_hst, 1)

            over_tiles(dve, [(0, spread), (1, copy), (2, residual)], T)

        def combine_pe(pe):
            pe.wait_ge(s_do, NPAIR)

            def transposes(t, q):
                b = q % 2
                pe.wait_ge(s_ecw, t + 1)
                if after(t, 1):
                    pe.wait_ge(s_eTa, t)
                    pe.wait_ge(s_eTd, t)
                spread = cw[b][:].rearrange("p g n -> p (g n)")
                nc.tensor.transpose(bank[6][:, 0:TP], spread[:, 0:128], ident[0:TP, 0:TP])
                nc.tensor.transpose(bank[7][0:NE, 0:TP], spread[:, 128:3 * NE], ident[0:TP, 0:TP]).then_inc(s_eT, 1)

            def product(t, q):
                b = q % 2
                pe.wait_ge(s_eTa, t + 1)
                pe.wait_ge(s_eTd, t + 1)
                pe.wait_ge(s_eb, t + 1)
                if after(t, 2):
                    pe.wait_ge(s_h, 2 * T + t - 1)
                nc.tensor.matmul(bank[b][0:TP, 0:ED], c1[b][:], e1[q][:], start=True, stop=False)
                nc.tensor.matmul(bank[b][0:TP, 0:ED], c2[b][:], e2[q][:], start=False, stop=True).then_inc(s_ey, 1)

            over_tiles(pe, [(0, transposes), (1, product)], T, unroll=4)

        def value_columns(j):
            return j * TP if not isinstance(j, int) or j <= T else (B - WIN + PADR) * S + (j - T - 1) * TP

        def value_tiles(t):
            if isinstance(t, int):
                return {0: [0, 1, 2], T - 1: [T + 1, T + 2, T + 3]}.get(t, [t + 2])
            return [t + 2]

        def near_sp(sp):
            sp.wait_ge(s_ey, T)
            sp.dma_start(masks[:], ins["masks"]).then_inc(s_nin, 16)
            for v in range(2):
                sp.dma_start(near[v][:], ins["near"][v]).then_inc(s_nin, 16)
            sp.wait_ge(s_pad, 1)
            for e in range(EX):
                sp.dma_start(buf_of[e], zero[:]).then_inc(s_bz, 16)
            for b in range(2):
                sp.dma_start(w13[b][:], ins["w13"][b]).then_inc(s_w13[b], 16)
                sp.dma_start(w2r[b][:], ins["w2r"][b]).then_inc(s_w2r[b], 16)

        def near_pool(pool):
            pool.wait_ge(s_ey, T)
            nc.gpsimd.memset(zero[:], 0.0)
            nc.gpsimd.memset(xg[:, 0:PADR * S], 0.0)
            nc.gpsimd.memset(xg[:, XCOLS - PADR * S:XCOLS], 0.0)
            nc.gpsimd.memset(kT[:, 0:PADR * S], 0.0)
            nc.gpsimd.memset(kT[:, XCOLS - PADR * S:XCOLS], 0.0)
            for v in vn + vl:
                last = nc.gpsimd.memset(v[:], 0.0)
            last.then_inc(s_pad, 1)

            def add_normalized(p, b):
                pool.wait_ge(s_hn, 2 * T + 2 * p + 2)
                nc.gpsimd.tensor_tensor(h[:, bass.ds(2 * p, 2), :], h[:, bass.ds(2 * p, 2), :], hp[b][:], ALU.add).then_inc(s_ha, 1)

            over_tiles(pool, [(0, add_normalized)], T // 2)
            pool.wait_ge(s_ha, T // 2)
            pool.wait_ge(s_fg, T // 2)

            def source(j):
                if after(j, 2):
                    pool.wait_ge(s_fV, j - 1)
                nc.gpsimd.tensor_copy(vsrc[j % 2 if isinstance(j, int) else source.b][:], xg[:, bass.ds(value_columns(j), TP)]).then_inc(s_fv, 1)

            def sources(t, q):
                source.b = q % 2
                for j in value_tiles(t):
                    source(j)

            def normalize_w(t, q):
                b = q % 2
                pool.wait_ge(s_nr, t + 1)
                nc.gpsimd.tensor_tensor(nl[q][:], nl[q][:], nr[b][:].unsqueeze(2).to_broadcast([TP, NHN, KW]), ALU.mult).then_inc(s_nw, 1)

            def residual(t, q):
                b = q % 2
                if after(t, 2):
                    pool.wait_ge(s_h, 3 * T + t - 1)
                nc.gpsimd.tensor_tensor(h2[b][:], h[:, t, :], Cc["bfc2"], ALU.add).then_inc(s_nh2, 1)

            over_tiles(pool, [(2, sources), (2, normalize_w), (5, residual)], T, unroll=4, tail=2)

        def near_act(act):
            h_std(act, 2)

            def copy_T(p, b):
                act.wait_ge(s_hTr, 2 * T + p + 1)
                if after(p, 2):
                    act.wait_ge(s_f1, p - 1)
                nc.scalar.copy(hpT[b][:], bank[0][0:HALF, 0:2 * PAIR].rearrange("p (c q) -> p c q", c=2)).then_inc(s_hTc, 1)

            def conva(p, b):
                act.wait_ge(s_fA, p + 1)
                if after(p, 2):
                    act.wait_ge(s_fB, p - 1)
                nc.scalar.activation(fa[b][:], bank[2][0:CONV, 0:PAIR], ACT.Identity, bias=Cc["bconva"]).then_inc(s_fAc, 1)

            def gelu(p, b):
                act.wait_ge(s_fs, p + 1)
                nc.scalar.activation(xg[:, bass.ds(PADR * S + p * PAIR, PAIR)], fs[b][:], ACT.Gelu).then_inc(s_fg, 1)

            over_tiles(act, [(0, copy_T), (2, conva), (3, gelu)], T // 2)

        def near_dve(dve):
            h_norm_constants(dve, 2)
            dve.wait_ge(s_ln, 15)
            dve.wait_ge(s_cci, 16)
            dve.wait_ge(s_pad, 1)

            def normalize(p, b):
                if after(p, 2):
                    dve.wait_ge(s_hTr, 2 * T + p - 1)
                    dve.wait_ge(s_ha, p - 1)
                for i in range(2):
                    last = nc.vector.tensor_scalar(hp[b][:, i, :], h[:, 2 * p + i, :], hmean[:, bass.ds(2 * p + i, 1)], hrs[:, bass.ds(2 * p + i, 1)], ALU.subtract, ALU.mult)
                last.then_inc(s_hn, 2)

            def fc1(p, b):
                dve.wait_ge(s_f1, p + 1)
                if after(p, 2):
                    dve.wait_ge(s_fs, p - 1)
                    dve.wait_ge(s_fA, p - 1)
                nc.vector.tensor_scalar(fx[b][:], bank[1][0:WN, 0:PAIR], Cc["bfc1"], None, ALU.add).then_inc(s_f1c, 1)

            def convb(p, b):
                dve.wait_ge(s_fB, p + 1)
                if after(p, 2):
                    dve.wait_ge(s_fg, p - 1)
                nc.vector.scalar_tensor_tensor(out=fs[b][:], in0=bank[3][0:WN, 0:PAIR], scalar=Cc["bconvb"], in1=fx[b][:], op0=ALU.add, op1=ALU.add).then_inc(s_fs, 1)

            def keys(p, b):
                dve.wait_ge(s_fK, p + 1)
                nc.vector.tensor_scalar(kT[:, bass.ds(PADR * S + p * PAIR, PAIR)], bank[4][0:WN, 0:PAIR], Cc["bk"], None, ALU.add).then_inc(s_fKc, 1)

            over_tiles(dve, [(0, normalize), (3, convb), (1, fc1), (4, keys)], T // 2)

            dve.wait_ge(s_nin, 48)
            for v in range(4):
                last = nc.vector.tensor_tensor(bias[v][:], near[v == 3][:], masks[:, v, :].unsqueeze(1).to_broadcast([TP, NHN, KW]), ALU.add)
            last.then_inc(s_nb, 1)
            dve.wait_ge(s_nb, 1)

            def spread(t, q):
                b = q % 2
                dve.wait_ge(s_nQ, t + 1)
                if after(t, 2):
                    dve.wait_ge(s_nS, 4 * t - 4)
                nc.vector.scalar_tensor_tensor(out=qx[b][:], in0=bank[0][0:WN, 0:TP].unsqueeze(1).to_broadcast([WN, NHN, TP]), scalar=Cc["bq"], in1=Cc["head"].unsqueeze(2).to_broadcast([WN, NHN, TP]), op0=ALU.add, op1=ALU.mult).then_inc(s_nq, 1)

            def values(t, q):
                for i, j in enumerate(value_tiles(t)):
                    dst = vl[i] if isinstance(t, int) and t == T - 1 else vn[(q + 2 if len(value_tiles(t)) == 1 else j) % 4]
                    dve.wait_ge(s_fV, j + 1)
                    if after(j, 4):
                        dve.wait_ge(s_nA, j - 3 if isinstance(j, int) and j <= T else t - 1)
                    nc.vector.tensor_tensor(dst[:, :, 0:DN], bank[6][0:TP, 128:128 + WN].rearrange("p (h d) -> p h d", h=NHN), Cc["bv"].rearrange("p (h d) -> p h d", h=NHN), ALU.add).then_inc(s_fVc, 1)

            def logits(t, q):
                b = q % 2
                v = {0: 0, T - 2: 2, T - 1: 3}.get(t, 1) if isinstance(t, int) else 1
                if after(t, 2):
                    dve.wait_ge(s_ne, t - 1)
                if after(t, 4):
                    dve.wait_ge(s_nT, t - 3)
                for head in range(NHN):
                    dve.wait_ge(s_nS, 4 * t + head + 1)
                    nc.vector.memset(tick[:, head:head + 1], 0.0)
                    nc.vector.tensor_tensor_reduce(nl[q][:, head, :], bank[1 + head % 2][0:TP, 0:KW], bias[v][:, head, :], 1.0, -3.0e38, ALU.add, ALU.max, nm[b][:, head:head + 1]).then_inc(s_nl, 1)
                dve.wait_ge(s_nl, 4 * t + 4)
                nc.vector.tensor_scalar(nn[b][:], nm[b][:], -1.0, None, ALU.mult).then_inc(s_nm, 1)

            def reciprocal(t, q):
                b = q % 2
                dve.wait_ge(s_ne, t + 1)
                if after(t, 2):
                    dve.wait_ge(s_nw, t - 1)
                nc.vector.reciprocal(nr[b][:], nsum[b][:]).then_inc(s_nr, 1)

            def copy_w(t, q):
                b = q % 2
                dve.wait_ge(s_nT, t + 1)
                if after(t, 2):
                    dve.wait_ge(s_nA, t - 1)
                nc.vector.tensor_copy(pTa[b][:, 2:4], bank[4][0:TP, 0:4 * TP].rearrange("p (h c q) -> p h c q", h=2, c=2)).then_inc(s_nTd, 1)

            def residual(t, q):
                b = q % 2
                dve.wait_ge(s_nF, t + 1)
                dve.wait_ge(s_nh2, t + 1)
                nc.vector.tensor_tensor(h[:, t, :], bank[7][0:TP, 0:ED], h2[b][:], ALU.add).then_inc(s_h, 1)
                dve.wait_ge(s_h, 3 * T + t + 1)
                nc.vector.bn_stats(hst[:, t, :], h[:, t, :]).then_inc(s_hst, 1)

            over_tiles(dve, [(0, spread), (2, reciprocal), (3, values), (1, logits), (3, copy_w), (5, residual)], T, unroll=4, tail=2)

        def near_act2(act):
            def exps(t, q):
                b = q % 2
                act.wait_ge(s_nm, t + 1)
                if after(t, 2):
                    act.wait_ge(s_nr, t - 1)
                for head in range(NHN):
                    last = nc.scalar.activation(nl[q][:, head, :], nl[q][:, head, :], ACT.Exp, bias=nn[b][:, head:head + 1], accum_out=nsum[b][:, head:head + 1])
                last.then_inc(s_ne, 1)

            def copy_w(t, q):
                b = q % 2
                act.wait_ge(s_nT, t + 1)
                if after(t, 2):
                    act.wait_ge(s_nA, t - 1)
                nc.scalar.copy(pTa[b][:, 0:2], bank[3][0:TP, 0:4 * TP].rearrange("p (h c q) -> p h c q", h=2, c=2))
                nc.scalar.copy(pTb[b][:], bank[5][0:S, 0:4 * TP].rearrange("p (h q) -> p h q", h=NHN)).then_inc(s_nTa, 1)

            def copy_o(t, q):
                b = q % 2
                act.wait_ge(s_nA, t + 1)
                if after(t, 2):
                    act.wait_ge(s_nP, t - 1)
                nc.scalar.copy(noT[b][:], bank[6][:, 0:TP]).then_inc(s_noc, 1)

            def proj(t, q):
                b = q % 2
                act.wait_ge(s_nP, t + 1)
                if after(t, 2):
                    act.wait_ge(s_nF, t - 1)
                nc.scalar.activation(nz[b][:], bank[7][0:WN, 0:TP], ACT.Identity, bias=Cc["bproj"]).then_inc(s_nz, 1)

            over_tiles(act, [(5, copy_o), (5, proj), (1, exps), (3, copy_w)], T, unroll=4, tail=2)

        def near_pe(pe):
            pe.wait_ge(s_cci, 16)
            pe.wait_ge(s_h, 2 * T + T)

            def transpose_h(p, b):
                pe.wait_ge(s_hn, 2 * T + 2 * p + 2)
                if after(p, 1):
                    pe.wait_ge(s_hTc, 2 * T + p)
                for c in range(2):
                    for i in range(2):
                        last = nc.tensor.transpose(bank[0][0:HALF, c * PAIR + i * TP:c * PAIR + (i + 1) * TP], hp[b][:, i, c * HALF:(c + 1) * HALF], ident[0:TP, 0:TP])
                last.then_inc(s_hTr, 1)

            def fc1(p, b):
                pe.wait_ge(s_hTc, 2 * T + p + 1)
                if after(p, 1):
                    pe.wait_ge(s_f1c, p)
                for c in range(2):
                    last = nc.tensor.matmul(bank[1][0:WN, 0:PAIR], Cc["fc1"][:, c * WN:(c + 1) * WN], hpT[b][:, c, :], start=(c == 0), stop=(c == 1))
                last.then_inc(s_f1, 1)

            def conva(p, b):
                pe.wait_ge(s_f1c, p + 1)
                if after(p, 1):
                    pe.wait_ge(s_fAc, p)
                nc.tensor.matmul(bank[2][0:CONV, 0:PAIR], Cc["conva"], fx[b][:], start=True, stop=True).then_inc(s_fA, 1)

            def convb(p, b):
                pe.wait_ge(s_fAc, p + 1)
                if after(p, 1):
                    pe.wait_ge(s_fs, p)
                nc.tensor.matmul(bank[3][0:WN, 0:PAIR], Cc["convb"], fa[b][:], start=True, stop=True).then_inc(s_fB, 1)

            def keys(p, b):
                pe.wait_ge(s_fg, p + 1)
                if after(p, 1):
                    pe.wait_ge(s_fKc, p)
                nc.tensor.matmul(bank[4][0:WN, 0:PAIR], Cc["wk"], xg[:, bass.ds(PADR * S + p * PAIR, PAIR)], start=True, stop=True).then_inc(s_fK, 1)

            over_tiles(pe, [(3, convb), (0, transpose_h), (1, fc1), (2, conva), (4, keys)], T // 2)
            pe.wait_ge(s_fKc, T // 2)
            pe.wait_ge(s_hTc, 2 * T + T // 2)

            def query(t, q):
                if after(t, 1):
                    pe.wait_ge(s_nq, t)
                nc.tensor.matmul(bank[0][0:WN, 0:TP], Cc["wq"], xg[:, bass.ds(PADR * S + t * TP, TP)], start=True, stop=True).then_inc(s_nQ, 1)

            def values(t, q):
                for j in value_tiles(t):
                    pe.wait_ge(s_fv, j + 1)
                    if after(j, 1):
                        pe.wait_ge(s_fVc, j)
                    if after(t, 2):
                        pe.wait_ge(s_noc, t - 1)
                    b = (j if isinstance(j, int) else q) % 2
                    nc.tensor.matmul(bank[6][0:TP, 128:128 + WN], vsrc[b][:], Cc["wv"], start=True, stop=True).then_inc(s_fV, 1)

            def scores(t, q, heads):
                first = (B - WIN + PADR) * S if isinstance(t, int) and t == T - 1 else t * TP
                pe.wait_ge(s_nq, t + 1)
                for head in heads:
                    if after(t, 1) or head >= 2:
                        pe.wait_ge(s_nl, 4 * t + head - 1)
                    nc.tensor.matmul(bank[1 + head % 2][0:TP, 0:KW], qx[q % 2][:, head, :], kT[:, bass.ds(first, KW)], start=True, stop=True).then_inc(s_nS, 1)

            def transpose_w(t, q):
                pe.wait_ge(s_nw, t + 1)
                if after(t, 1):
                    pe.wait_ge(s_nTa, t)
                    pe.wait_ge(s_nTd, t)
                for head in range(NHN):
                    for c in range(2):
                        k = (head % 2 * 2 + c) * TP
                        nc.tensor.transpose(bank[3 + head // 2][0:TP, k:k + TP], nl[q][:, head, c * TP:(c + 1) * TP], ident[0:TP, 0:TP])
                    last = nc.tensor.transpose(bank[5][0:S, head * TP:(head + 1) * TP], nl[q][:, head, 2 * TP:KW], ident[0:TP, 0:TP])
                last.then_inc(s_nT, 1)

            def values_out(t, q):
                b = q % 2
                pe.wait_ge(s_nTa, t + 1)
                pe.wait_ge(s_nTd, t + 1)
                tiles = vl if isinstance(t, int) and t == T - 1 else [vn[(q + i) % 4] for i in range(3)]
                made = VT if isinstance(t, int) and t >= T - 2 else t + 4
                pe.wait_ge(s_fVc, made)
                if after(t, 1):
                    pe.wait_ge(s_noc, t)
                for i in range(3):
                    for head in range(NHN):
                        p = pTa[b][:, head, i, :] if i < 2 else pTb[b][:, head, :]
                        v = tiles[i][:, head, :] if i < 2 else tiles[i][0:S, head, :]
                        last = nc.tensor.matmul(bank[6][head * VW:(head + 1) * VW, 0:TP], v, p, start=(i == 0), stop=(i == 2))
                last.then_inc(s_nA, 1)

            def proj(t, q):
                pe.wait_ge(s_noc, t + 1)
                if after(t, 1):
                    pe.wait_ge(s_h, 3 * T + t)
                nc.tensor.matmul(bank[7][0:WN, 0:TP], Cc["proj"], noT[q % 2][:], start=True, stop=True).then_inc(s_nP, 1)

            def fc2(t, q):
                pe.wait_ge(s_nz, t + 1)
                nc.tensor.matmul(bank[7][0:TP, 0:ED], nz[q % 2][:], Cc["fc2"], start=True, stop=True).then_inc(s_nF, 1)

            over_tiles(pe, [(0, query), (3, values), (1, lambda t, q: scores(t, q, (0, 1))), (5, proj),
                            (1, lambda t, q: scores(t, q, (2, 3))), (3, transpose_w), (5, fc2), (4, values_out)], T, unroll=4, tail=2)

        def route_act(act):
            h_std(act, 3)
            act.wait_ge(s_ph, 9 + 2)
            nc.scalar.activation(zrt[:], zsq[:], ACT.Sqrt, bias=eps6[:], scale=4.0).then_inc(s_hsd, 1)

            def copy_T(t, b):
                act.wait_ge(s_hTr, 5 * T // 2 + t + 1)
                if after(t, 2):
                    act.wait_ge(s_gl, t - 1)
                nc.scalar.copy(hnT[b][:], bank[0][0:HALF, 0:2 * TP].rearrange("p (c q) -> p c q", c=2)).then_inc(s_hTc, 1)

            over_tiles(act, [(0, copy_T)], T)
            act.wait_ge(s_rt, 1)
            nc.scalar.activation(wexp[:], wdif[:], ACT.Exp).then_inc(s_re, 1)

        def route_pe(pe):
            def transpose_h(t, b):
                pe.wait_ge(s_hn, 3 * T + t + 1)
                if after(t, 1):
                    pe.wait_ge(s_hTc, 5 * T // 2 + t)
                for c in range(2):
                    last = nc.tensor.transpose(bank[0][0:HALF, c * TP:(c + 1) * TP], hn[b][:, c * HALF:(c + 1) * HALF], ident[0:TP, 0:TP])
                last.then_inc(s_hTr, 1)

            def router(t, b):
                pe.wait_ge(s_hTc, 5 * T // 2 + t + 1)
                for c in range(2):
                    last = nc.tensor.matmul(bank[1][0:TP, bass.ds(t * EX, EX)], hnT[b][:, c, :], Cc["router"][:, c * EX:(c + 1) * EX], start=(c == 0), stop=(c == 1))
                last.then_inc(s_gl, 1)

            over_tiles(pe, [(0, transpose_h), (1, router)], T)
            pe.wait_ge(s_rt, 2)
            marks = hots[:].rearrange("p t e -> p (t e)")
            nc.tensor.matmul(bank[2][0:TP, 0:T * EX], Cc["before"], marks, start=True, stop=True)
            nc.tensor.matmul(bank[3][0:TP, 0:T * EX], ones[0:TP, 0:TP], marks, start=True, stop=True).then_inc(s_rp, 1)

        def route_dve(dve):
            h_norm_constants(dve, 3)
            dve.wait_ge(s_ln, 20)
            nc.vector.memset(eps6[:], 1e-6)
            nc.vector.tensor_tensor(zsq[:], hvar[:], hrs[:], ALU.mult).then_inc(s_ph, 1)
            dve.wait_ge(s_ph, 9 + 1)
            nc.vector.tensor_tensor(zsq[:], zsq[:], hrs[:], ALU.mult).then_inc(s_ph, 1)
            dve.wait_ge(s_hsd, 5)
            nc.vector.reciprocal(zs[:], zrt[:]).then_inc(s_ph, 1)
            dve.wait_ge(s_ph, 9 + 3)
            nc.vector.scalar_tensor_tensor(out=zs[:], in0=zs[:], scalar=2.0, in1=hrs[:], op0=ALU.mult, op1=ALU.mult).then_inc(s_ph, 1)
            dve.wait_ge(s_ph, 9 + 4)

            def normalize(t, b):
                if after(t, 2):
                    dve.wait_ge(s_hTr, 5 * T // 2 + t - 1)
                nc.vector.tensor_scalar(hn[b][:], h[:, t, :], hmean[:, bass.ds(t, 1)], hrs[:, bass.ds(t, 1)], ALU.subtract, ALU.mult).then_inc(s_hn, 1)
                nc.vector.tensor_scalar(zk[:, t, :], h[:, t, :], hmean[:, bass.ds(t, 1)], zs[:, bass.ds(t, 1)], ALU.subtract, ALU.mult).then_inc(s_gz, 1)

            over_tiles(dve, [(0, normalize)], T)

            per_row = lambda a: a.unsqueeze(2).to_broadcast([TP, T, EX])
            index = Cc["index"].unsqueeze(1).to_broadcast([TP, T, EX])
            real = Cc["real"].unsqueeze(1).to_broadcast([TP, 2, T])
            dve.wait_ge(s_gl, T)
            logits = bank[1][0:TP, 0:T * EX].rearrange("p (t e) -> p t e", e=EX)
            r = 0
            for k in range(2):
                lg = lg2[:] if k else logits
                nc.vector.tensor_reduce(top[:, k, :], lg, AX.X, ALU.max).then_inc(s_r, 1)
                dve.wait_ge(s_r, r + 1)
                if k == 1:
                    nc.vector.tensor_tensor(wdif[:], top[:, 1, :], top[:, 0, :], ALU.subtract).then_inc(s_rt, 1)
                nc.vector.tensor_tensor(eq[:], lg, per_row(top[:, k, :]), ALU.is_equal).then_inc(s_r, 1)
                dve.wait_ge(s_r, r + 2)
                nc.vector.scalar_tensor_tensor(out=key[:], in0=eq[:], scalar=-float(EX), in1=index, op0=ALU.mult, op1=ALU.add).then_inc(s_r, 1)
                dve.wait_ge(s_r, r + 3)
                nc.vector.tensor_reduce(expert[:, k, :], key[:], AX.X, ALU.min).then_inc(s_r, 1)
                dve.wait_ge(s_r, r + 4)
                nc.vector.tensor_tensor(hot[:, k], key[:], per_row(expert[:, k, :]), ALU.is_equal).then_inc(s_r, 1)
                dve.wait_ge(s_r, r + 5)
                r += 5
                if k == 0:
                    nc.vector.scalar_tensor_tensor(out=lg2[:], in0=hot[:, 0], scalar=-1e30, in1=logits, op0=ALU.mult, op1=ALU.add).then_inc(s_r, 1)
                    dve.wait_ge(s_r, r + 1)
                    r += 1
            nc.vector.tensor_tensor(hots[:], hot[:, 0], hot[:, 1], ALU.add).then_inc(s_r, 1)
            dve.wait_ge(s_r, r + 1)
            nc.vector.tensor_tensor(hots[:], hots[:], per_row(Cc["real"]), ALU.mult).then_inc(s_rt, 1)

            dve.wait_ge(s_rp, 1)
            prior = bank[2][0:TP, 0:T * EX].rearrange("p (t e) -> p t e", e=EX)
            totals = bank[3][0:TP, 0:T * EX].rearrange("p (t e) -> p t e", e=EX)
            nc.vector.memset(sums[0][:, 0:1, :], 0.0)
            nc.vector.tensor_copy(sums[0][:, 1:T, :], totals[:, 0:T - 1, :]).then_inc(s_r, 1)
            r += 2
            dve.wait_ge(s_r, r)
            step, b = 1, 0
            while step < T:
                nc.vector.tensor_copy(sums[1 - b][:, 0:step, :], sums[b][:, 0:step, :])
                nc.vector.tensor_tensor(sums[1 - b][:, step:T, :], sums[b][:, step:T, :], sums[b][:, 0:T - step, :], ALU.add).then_inc(s_r, 1)
                r += 1
                dve.wait_ge(s_r, r)
                step, b = 2 * step, 1 - b
            nc.vector.tensor_tensor(place[:], prior, sums[b][:], ALU.add).then_inc(s_r, 1)
            dve.wait_ge(s_r, r + 1)
            nc.vector.tensor_tensor(picked[:], hot[:], place[:].unsqueeze(1).to_broadcast([TP, 2, T, EX]), ALU.mult).then_inc(s_r, 1)
            dve.wait_ge(s_r, r + 2)
            nc.vector.tensor_reduce(pk[:], picked[:], AX.X, ALU.add).then_inc(s_r, 1)
            dve.wait_ge(s_r, r + 3)
            nc.vector.scalar_tensor_tensor(out=kept[:], in0=pk[:], scalar=float(CAP), in1=real, op0=ALU.is_lt, op1=ALU.mult)
            nc.vector.scalar_tensor_tensor(out=slot[:], in0=expert[:], scalar=float(CAPP), in1=pk[:], op0=ALU.mult, op1=ALU.add)
            nc.vector.tensor_scalar(last_slot[:], pk[:], float(CAP - 1), float(EX * CAPP), ALU.min, ALU.add).then_inc(s_r, 1)
            dve.wait_ge(s_r, r + 4)
            nc.vector.tensor_scalar(away[:], kept[:], -SKIP, SKIP + EX * CAPP, ALU.mult, ALU.add)
            nc.vector.scalar_tensor_tensor(out=last_slot[:], in0=expert[:], scalar=float(CAPP), in1=last_slot[:], op0=ALU.mult, op1=ALU.add).then_inc(s_r, 1)
            dve.wait_ge(s_r, r + 5)
            nc.vector.tensor_tensor(slot[:], slot[:], away[:], ALU.add).then_inc(s_r, 1)
            dve.wait_ge(s_r, r + 6)
            nc.vector.tensor_copy(to[:], slot[:])
            nc.vector.tensor_copy(frm[:], last_slot[:]).then_inc(s_rt, 1)

            dve.wait_ge(s_re, 1)
            nc.vector.tensor_scalar(wsum[:], wexp[:], 1.0, None, ALU.add).then_inc(s_r, 1)
            dve.wait_ge(s_r, r + 7)
            nc.vector.reciprocal(wts[:, 0, :], wsum[:]).then_inc(s_r, 1)
            dve.wait_ge(s_r, r + 8)
            nc.vector.tensor_tensor(wts[:, 1, :], wexp[:], wts[:, 0, :], ALU.mult).then_inc(s_r, 1)
            dve.wait_ge(s_r, r + 9)
            nc.vector.tensor_tensor(wts[:], wts[:], kept[:], ALU.mult).then_inc(s_r, 1)
            dve.wait_ge(s_r, r + 10)
            nc.vector.tensor_tensor(wsum[:], wts[:, 0, :], wts[:, 1, :], ALU.add).then_inc(s_r, 1)
            dve.wait_ge(s_r, r + 11)
            nc.vector.tensor_tensor(wsum[:], wsum[:], hrs[:], ALU.mult).then_inc(s_r, 1)
            dve.wait_ge(s_r, r + 12)
            nc.vector.tensor_scalar(own[:, 0, :], wsum[:], 1.0, None, ALU.add)
            nc.vector.tensor_tensor(own[:, 1, :], wsum[:], hmean[:], ALU.mult).then_inc(s_rt, 1)

        def rows_pool(pool):
            pool.wait_ge(s_rt, 3)
            pool.wait_ge(s_gz, T)
            pool.wait_ge(s_bz, 16 * EX)
            for t in range(T):
                for k in range(2):
                    nc.gpsimd.indirect_dma_start(buf, bass.IndirectOffsetOnAxis(ap=to[:, k, t:t + 1], axis=0), zk[:, t, :], None, bounds_check=EX * CAPP - 1, oob_is_err=False).then_inc(s_sc, 16)
            for b in range(2):
                pool.wait_ge(s_eo[b], n_eo + 16 * EX // 2)
            for t in range(T):
                if t >= 4:
                    pool.wait_ge(s_o, t - 3)
                for k in range(2):
                    nc.gpsimd.indirect_dma_start(back[k][t % 4][:], None, ybuf, bass.IndirectOffsetOnAxis(ap=frm[:, k, t:t + 1], axis=0), bounds_check=EX * CAPP - 1, oob_is_err=False).then_inc(s_g[t % 4], 16)

        def routed_sp(sp):
            sp.wait_ge(s_sc, 16 * 2 * T)

            def load(e, b):
                if after(e, 2):
                    sp.wait_ge(s_zT, 4 * e - 4)
                sp.dma_start(zr[b][:].rearrange("p j d -> p (j d)"), buf_of[e]).then_inc(s_zr[b], 16)
                if after(e, 2):
                    sp.wait_ge(s_gu, 16 * e - 16)
                    sp.dma_start(w13[b][:], ins["w13"][e]).then_inc(s_w13[b], 16)
                    sp.wait_ge(s_yp, SJ * (e - 1))
                    sp.dma_start(w2r[b][:], ins["w2r"][e]).then_inc(s_w2r[b], 16)

            def store(e, b):
                sp.wait_ge(s_yc[0], SJ // 2 * (e + 1))
                sp.wait_ge(s_yc[1], SJ // 2 * (e + 1))
                sp.dma_start(ybuf_of[e], yr[b][:].rearrange("p j d -> p (j d)")).then_inc(s_eo[b], 16)

            over_tiles(sp, [(0, load), (2, store)], EX)

            def result(t, b):
                sp.wait_ge(s_o, t + 1)
                if after(t, T - 1) and isinstance(t, int):
                    sp.dma_start(rows_out[t * TP:B * S], acc[b][0:B * S - t * TP]).then_inc(s_x[b], 16)
                else:
                    sp.dma_start(rows_out[bass.ds(t * TP, TP)], acc[b][:]).then_inc(s_x[b], 16)

            over_tiles(sp, [(0, result)], T, tail=1)
            for b in range(2):
                sp.wait_ge(s_x[b], n_x + 16 * T // 2)

        def routed_pe(pe):
            def transposes(e, b):
                pe.wait_ge(s_zr[b], 8 * (e - b) + 16)
                for g in range(2):
                    for c in range(2):
                        if after(e, 1) or g:
                            pe.wait_ge(s_zc[c], 2 * e + g)
                        for j in range(SJ // 2):
                            last = nc.tensor.transpose(bank[c][0:HALF, j * SP_:(j + 1) * SP_], zr[b][:, g * SJ // 2 + j, c * HALF:(c + 1) * HALF], ident[0:SP_, 0:SP_])
                        last.then_inc(s_zT, 1)

            def gate_up(e, b):
                pe.wait_ge(s_w13[b], 8 * (e - b) + 16)
                for half in range(2):
                    for c in range(2):
                        pe.wait_ge(s_zc[c], 2 * e + half + 1)
                    for m in range(EH // 128):
                        k = half * (EH // 128) + m
                        if after(e, 1) or k >= 2:
                            pe.wait_ge(s_hT, 8 * e + k - 1)
                        for part in range(2):
                            at = part * EH + m * 128
                            for c in range(2):
                                last = nc.tensor.matmul(bank[2 + 2 * (m % 2) + part][:, 0:HS], w13[b][:, c, at:at + 128], zT[b][:, c, half * HS:(half + 1) * HS], start=(c == 0), stop=(c == 1))
                            last.then_inc(s_gu, 1)

            def outputs(e, b):
                pe.wait_ge(s_w2r[b], 8 * (e - b) + 16)
                for j in range(SJ):
                    pe.wait_ge(s_hT, 8 * e + 4 * (j * 2 // SJ + 1))
                    if after(e, 1) or j >= 2:
                        pe.wait_ge(s_yc[j % 2], SJ // 2 * e + j // 2)
                    for m in range(EH // 128):
                        last = nc.tensor.matmul(bank[6 + j % 2][0:SP_, 0:ED], hT[:, m, j * SP_:(j + 1) * SP_], w2r[b][:, m, :], start=(m == 0), stop=(m == EH // 128 - 1))
                    last.then_inc(s_yp, 1)

            over_tiles(pe, [(1, gate_up), (0, transposes), (1, outputs)], EX)

        def routed_act(act):
            def store_z(e, b):
                for g in range(2):
                    act.wait_ge(s_zT, 4 * e + 2 * g + 1)
                    if after(e, 2):
                        act.wait_ge(s_gu, 16 * e - 16)
                    nc.scalar.copy(act_tick[:], eps5[:])
                    nc.scalar.activation(zT[b][:, 0, g * HS:(g + 1) * HS], bank[0][0:HALF, 0:HS], ACT.Copy, scale=Cc["gain"][:, bass.ds(e, 1)]).then_inc(s_zc[0], 1)

            def silu(e, b):
                for k in range(8):
                    act.wait_ge(s_gu, 16 * e + 2 * k + 1)
                    if after(e, 1) or k >= 2:
                        act.wait_ge(s_hT, 8 * e + k - 1)
                    nc.scalar.activation(sg[k % 2][:], bank[2 + 2 * (k % 2)][:, 0:HS], ACT.Silu).then_inc(s_sg, 1)

            def copy_y(e, b):
                for j in range(0, SJ, 2):
                    act.wait_ge(s_yp, SJ * e + j + 1)
                    if after(e, 2):
                        act.wait_ge(s_eo[b], 8 * (e - b) + n_eo)
                    nc.scalar.copy(yr[b][:, j, :], bank[6][0:SP_, 0:ED]).then_inc(s_yc[0], 1)

            over_tiles(act, [(1, silu), (0, store_z), (1, copy_y)], EX)

        def routed_dve(dve):
            def store_z(e, b):
                for g in range(2):
                    dve.wait_ge(s_zT, 4 * e + 2 * g + 2)
                    if after(e, 2):
                        dve.wait_ge(s_gu, 16 * e - 16)
                    nc.vector.tensor_scalar(zT[b][:, 1, g * HS:(g + 1) * HS], bank[1][0:HALF, 0:HS], Cc["gain"][:, bass.ds(e + EX, 1)], None, ALU.mult).then_inc(s_zc[1], 1)

            def hidden(e, b):
                for k in range(8):
                    half, m = k // 4, k % 4
                    dve.wait_ge(s_sg, 8 * e + k + 1)
                    dve.wait_ge(s_gu, 16 * e + 2 * k + 2)
                    if after(e, 1):
                        dve.wait_ge(s_yp, SJ * e)
                    nc.vector.tensor_tensor(hT[:, m, half * HS:(half + 1) * HS], sg[k % 2][:], bank[3 + 2 * (k % 2)][:, 0:HS], ALU.mult).then_inc(s_hT, 1)

            def copy_y(e, b):
                for j in range(1, SJ, 2):
                    dve.wait_ge(s_yp, SJ * e + j + 1)
                    if after(e, 2):
                        dve.wait_ge(s_eo[b], 8 * (e - b) + n_eo)
                    nc.vector.tensor_copy(yr[b][:, j, :], bank[7][0:SP_, 0:ED]).then_inc(s_yc[1], 1)

            over_tiles(dve, [(1, hidden), (0, store_z), (1, copy_y)], EX)

            dve.wait_ge(s_rt, 4)

            def add(t, q):
                b = q % 2
                dve.wait_ge(s_g[q], 8 * (t - q) + 32)
                if after(t, 2):
                    dve.wait_ge(s_x[b], 8 * (t - b) + n_x)
                nc.vector.tensor_scalar(acc[b][:], h[:, t, :], own[:, 0, bass.ds(t, 1)], own[:, 1, bass.ds(t, 1)], ALU.mult, ALU.subtract).then_inc(s_o1, 1)
                dve.wait_ge(s_o1, 2 * t + 1)
                nc.vector.scalar_tensor_tensor(out=acc[b][:], in0=back[0][q][:], scalar=wts[:, 0, bass.ds(t, 1)], in1=acc[b][:], op0=ALU.mult, op1=ALU.add).then_inc(s_o1, 1)
                dve.wait_ge(s_o1, 2 * t + 2)
                nc.vector.scalar_tensor_tensor(out=acc[b][:], in0=back[1][q][:], scalar=wts[:, 1, bass.ds(t, 1)], in1=acc[b][:], op0=ALU.mult, op1=ALU.add).then_inc(s_o, 1)

            over_tiles(dve, [(0, add)], T, unroll=4)

        block = ctx.enter_context(nc.Block())

        @block.sync
        def _(sp):
            embed_sp(sp)
            sp.wait_ge(s_cbi, 16)
            experts_sp(sp)
            combine_sp(sp)
            near_sp(sp)
            routed_sp(sp)

        @block.gpsimd
        def _(pool):
            embed_pool(pool)
            experts_pool(pool)
            combine_pool(pool)
            near_pool(pool)
            rows_pool(pool)

        @block.scalar
        def _(act):
            embed_act(act)
            attention_act(act)
            dispatch_act(act)
            experts_act(act)
            combine_act(act)
            near_act(act)
            near_act2(act)
            route_act(act)
            routed_act(act)

        @block.vector
        def _(dve):
            embed_dve(dve)
            attention_dve(dve)
            dispatch_dve(dve)
            experts_dve(dve)
            combine_dve(dve)
            near_dve(dve)
            route_dve(dve)
            routed_dve(dve)

        @block.tensor
        def _(pe):
            embed_pe(pe)
            attention_pe(pe)
            dispatch_pe(pe)
            experts_pe(pe)
            combine_pe(pe)
            near_pe(pe)
            route_pe(pe)
            routed_pe(pe)


def pack_rows(pack, parts):
    at, n = columns(pack)
    a = np.zeros((128, n), np.float32)
    for name, (rows, off, cols) in at.items():
        a[0:rows, off:off + cols] = parts[name]
    return a


def lay_out(i):
    f = {k: np.asarray(v) for k, v in i.items()}
    x = f["x"].reshape(B, C_IN, 6, PATCH, 6, PATCH).transpose(0, 2, 4, 3, 5, 1).reshape(B, NP_, PD)
    xr = np.zeros((T * GB, S, PD), np.float32)
    xr[0:B, 1:] = x
    per_image = lambda first, rest: np.tile(np.concatenate([first, rest]), (GB, 1))
    zero = np.zeros((1, ED), np.float32)
    rows = lambda v, n: np.tile(v[None, :], (n, 1))
    cls = f["L0_tok_cls_token"][None, :]
    ca = pack_rows(PACK_A, {
        "ident": np.eye(128, dtype=np.float32),
        "g1": f["L0_tok_ln1_g"].reshape(KC, 128).T, "b1": f["L0_tok_ln1_b"].reshape(KC, 128).T,
        "wtok": f["L0_tok_W"].reshape(KC, 128, ED).transpose(1, 0, 2).reshape(128, KC * ED),
        "btok": rows(f["L0_tok_b"], TP),
        "g2m": per_image(zero, rows(f["L0_tok_ln2_g"], NP_)), "b2m": per_image(zero, rows(f["L0_tok_ln2_b"], NP_)),
        "pos": np.tile(f["L0_tok_pos_embed"][0], (GB, 1)), "cls": per_image(cls, np.zeros((NP_, ED), np.float32)),
    })
    chunks = lambda w, n=2: w.reshape(n, -1, w.shape[1]).transpose(1, 0, 2).reshape(w.shape[0] // n, -1)
    wq, wk = (f["L0_attn_Wq"], f["L0_attn_Wk"])
    own = np.arange(TP)[:, None] // S == np.arange(TP)[None, :] // S
    causal = (own & (np.arange(TP)[:, None] <= np.arange(TP)[None, :])).astype(np.float32)
    cb = pack_rows(PACK_B, {
        "wqk": chunks(np.concatenate([wq, wk], 1)), "wvg": chunks(np.concatenate([f["L0_attn_Wv"], f["L0_attn_Wg"]], 1)),
        "wo": chunks(f["L0_attn_Wo"]), "causal": np.tile(causal, (1, 2)),
        "phi": chunks(f["L0_ffn_phi"][:, :, 0]), "scale": np.tile(f["L0_ffn_scale"][None, :], (HALF, 1)),
        "image": (np.arange(TP)[:, None] // S == np.arange(GB)[None, :]).astype(np.float32),
        "b2r": np.tile(f["L0_ffn_b2"], (2, 1)), "b1s": f["L0_ffn_b1"].reshape(NE, HB, 128).transpose(2, 0, 1).reshape(128, NE * HB),
    })
    w1 = f["L0_ffn_w1"].reshape(NPAIR, 2, 2, HALF, HID).transpose(0, 3, 1, 2, 4)
    w2 = f["L0_ffn_w2"].reshape(NPAIR, 2, HB, 128, ED).transpose(0, 3, 1, 2, 4)
    col = lambda v: v[:, None]
    w = np.arange(TP)
    row, tok = w // S, w % S
    krow, ktok = np.arange(KW) // S, np.arange(KW) % S
    masks, near = np.zeros((TP, 4, KW), np.float32), np.zeros((2, TP, NHN, KW), np.float32)
    rpb = f["L1_attn_rpb"]
    for v, (q0, k0) in enumerate([(0, -PADR), (GB, GB - PADR), ((T - 2) * GB, (T - 2) * GB - PADR), ((T - 1) * GB, B - WIN)]):
        qr = q0 + row
        hs, ws = np.clip(qr - PADR, 0, B - WIN)[:, None], np.clip(tok - PADR, 0, S - WIN)[:, None]
        kr = (k0 + krow)[None, :]
        inside = (kr >= hs) & (kr < hs + WIN) & (ktok[None] >= ws) & (ktok[None] < ws + WIN)
        masks[:, v][(qr < B)[:, None] & ~inside] = -1e30
        if v in (1, 3):
            dr, dt = kr - qr[:, None] + WIN - 1, ktok[None] - tok[:, None] + WIN - 1
            ok = (dr >= 0) & (dr < 2 * WIN - 1) & (dt >= 0) & (dt < 2 * WIN - 1)
            for n in range(NHN):
                near[v // 2, :, n] = np.where(ok, rpb[n][np.where(ok, dr, 0), np.where(ok, dt, 0)], 0)
    qkv, bqkv = f["L1_attn_qkv_w"], f["L1_attn_qkv_b"]
    cc = pack_rows(PACK_C, {
        "fc1": chunks(f["L1_attn_fc1_w"].T), "conva": f["L1_attn_convA_w"].T, "convb": f["L1_attn_convB_w"].T,
        "wq": qkv[0:WN].T, "wk": qkv[WN:2 * WN].T, "wv": qkv[2 * WN:].T, 
        "proj": np.pad(f["L1_attn_proj_w"].T.reshape(NHN, DN, WN), ((0, 0), (0, VW - DN), (0, 0))).reshape(NHN * VW, WN),
        "fc2": f["L1_attn_fc2_w"].T, "bv": rows(bqkv[2 * WN:], TP), "bfc2": rows(f["L1_attn_fc2_b"], TP),
        "bfc1": col(f["L1_attn_fc1_b"]), "bconva": col(f["L1_attn_convA_b"]), "bconvb": col(f["L1_attn_convB_b"]),
        "bq": col(bqkv[0:WN]), "bk": col(bqkv[WN:2 * WN]), "bproj": col(f["L1_attn_proj_b"]),
        "head": (np.arange(WN)[:, None] // DN == np.arange(NHN)[None, :]).astype(np.float32) * np.float32(DN ** -0.5),
        "router": chunks(f["L1_ffn_gate_w"].T), "before": (w[:, None] < w[None, :]).astype(np.float32),
        "index": np.tile(np.arange(EX, dtype=np.float32)[None, :], (TP, 1)),
        "real": (w[:, None] + TP * np.arange(T)[None, :] < B * S).astype(np.float32),
        "gain": chunks(f["L1_ffn_norm_w"].T),
    })
    w13 = f["L1_ffn_w13"].transpose(0, 2, 1).reshape(EX, 2, HALF, 2 * EH).transpose(0, 2, 1, 3)
    w2r = f["L1_ffn_w2"].transpose(0, 2, 1).reshape(EX, EH // 128, 128, ED).transpose(0, 2, 1, 3)
    return {"cc": cc, "masks": masks, "near": near, "w13": np.ascontiguousarray(w13), "w2r": np.ascontiguousarray(w2r),
            "w1": np.ascontiguousarray(w1), "w2": np.ascontiguousarray(w2), "x": xr.reshape(T, TP, PD),
            "xT": np.ascontiguousarray(xr.reshape(T, TP, KC, 128).transpose(0, 3, 2, 1)), "ca": ca, "cb": cb}


_INS = ("cc", "masks", "near", "w13", "w2r", "w1", "w2", "x", "xT", "ca", "cb")


def kernel(**inputs):
    import numpy as _np
    import concourse.bacc as _bacc
    from concourse import mybir as _mybir
    from concourse.bass_utils import run_bass_kernel_spmd as _run

    nc = _bacc.Bacc("TRN2", target_bir_lowering=False, num_devices=1)
    laid = lay_out(inputs)
    arrays, args = {}, {}
    for name in _INS:
        a = _np.ascontiguousarray(laid[name])
        arrays[f"in_{name}_dram"] = a
        args[name] = nc.dram_tensor(f"in_{name}_dram", a.shape, _mybir.dt.from_np(a.dtype), kind="ExternalInput").ap()
    out = nc.dram_tensor("out_0_dram", (B * S, ED), _mybir.dt.float32, kind="ExternalOutput").ap()
    tower(nc, args, out)
    r = _run(nc, [arrays], core_ids=[0])
    return r.results[0]["out_0_dram"].reshape(B, S, ED)
```

```python
from contextlib import ExitStack

import concourse.bass as bass
from concourse import mybir
from concourse.alu_op_type import AluOpType as ALU
import numpy as np

ACT = mybir.ActivationFunctionType
AX = mybir.AxisListType
F32 = mybir.dt.float32
I32 = mybir.dt.int32

B, C_IN, IMG, PATCH = 64, 3, 96, 16
NP_ = (IMG // PATCH) ** 2
S = NP_ + 1
PD = C_IN * PATCH * PATCH
ED = 192
HALF = ED // 2
GB = 3
TP = GB * S
T = 22
NROW = T * TP
KC = PD // 128
NH, DH = 4, 64
NE, HID = 64, 768
HB = HID // 128
NPAIR = NE // 2
RING = 4
QKW = 2 * NH * DH
VGW = NH * DH + ED
WN, CONV, NHN = 96, 64, 4
DN = WN // NHN
WIN = 5
KR = GB + WIN - 1
KW = KR * S
PADR = WIN // 2
XCOLS = (T * GB + 2 * PADR) * S
VT = T + 4
VW = 32
PAIR = 2 * TP
EX, EH = 8, 512
CAP = int(np.ceil(1.25 * 2 * B * S / EX))
SJ = 6
SP_ = -(-CAP // SJ)
HS = SJ * SP_ // 2
CAPP = SJ * SP_
NST = EX * SJ
OUT = B * S + CAPP

PACK_A = [("g1", 128, KC), ("b1", 128, KC), ("wtok", 128, KC * ED),
          ("btok", TP, ED), ("g2m", TP, ED), ("b2m", TP, ED), ("pos", TP, ED), ("cls", TP, ED)]

PACK_B = [("wqk", HALF, 2 * QKW), ("wvg", HALF, 2 * VGW), ("wo", 128, 2 * ED), ("causal", TP, 2 * TP),
          ("phi", HALF, 2 * NE), ("scale", HALF, 1), ("image", TP, GB + 1), ("b1s", 128, NE * HB)]

PACK_C = [("fc1", HALF, 2 * WN), ("conva", WN, CONV), ("convb", CONV, WN), ("wq", WN, WN), ("wk", WN, WN),
          ("wv", WN, WN), ("proj", NHN * VW, WN), ("fc2", WN, ED), ("bv", TP, WN), ("bfc2", TP, ED),
          ("bfc1", WN, 1), ("bconva", CONV, 1), ("bconvb", WN, 1), ("bq", WN, 1), ("bk", WN, 1), ("bproj", WN, 1),
          ("head", WN, NHN), ("router", HALF, 2 * EX), ("before", TP, TP),
          ("count", TP, SP_), ("number", TP, T), ("spare", SP_, NST), ("real", TP, T),
          ("gain", HALF, 2 * EX)]


def columns(pack):
    at, off = {}, 0
    for name, rows, cols in pack:
        at[name] = (rows, off, cols)
        off += cols
    return at, off


def after(t, k):
    return not isinstance(t, int) or t >= k


def over_tiles(eng, stages, n, unroll=2, tail=0):
    lags = max(lag for lag, _ in stages)
    head = -(-(lags + 2) // unroll) * unroll
    stop = head + (n - tail - head) // unroll * unroll

    def turn(s):
        for lag, step in stages:
            if 0 <= s - lag < n:
                step(s - lag, (s - lag) % unroll)

    for s in range(head):
        turn(s)
    with eng.Fori(head, stop - unroll + 1, unroll) as i:
        for u in range(unroll):
            for lag, step in stages:
                step(i + (u - lag), (u - lag) % unroll)
    for s in range(stop, n + lags):
        turn(s)


def tower(nc, ins, rows_out):
    with ExitStack() as ctx:
        scope = [ctx]

        def sb(name, shape, dt=F32):
            return scope[-1].enter_context(nc.sbuf_tensor(name, shape, dt))

        def open_scope():
            scope.append(ExitStack())

        def close_scope():
            scope.pop().close()

        def sem(name):
            return ctx.enter_context(nc.semaphore(name))

        bank = [ctx.enter_context(nc.psum_tensor(f"bank{i}", [128, 512], F32)) for i in range(8)]

        h = sb("h", [TP, T, ED])

        def of(pack, at, name):
            rows, off, cols = at[name]
            return pack[0:rows, off:off + cols]

        identity = sb("identity", [128, 128])
        ident = identity[:]
        eps5 = sb("eps5", [128, 1])
        ones = sb("ones", [128, 128])

        tick = sb("tick", [TP, 8])
        pool_tick = sb("pool_tick", [TP, 2])
        act_tick = sb("act_tick", [128, 8])
        hst = sb("hst", [TP, T, 6])
        hmean = sb("hmean", [TP, T])
        hvar = sb("hvar", [TP, T])
        hdif = sb("hdif", [TP, T])
        hsd = sb("hsd", [TP, T])
        hrs = sb("hrs", [TP, T])
        hn = [sb(f"hn{b}", [TP, ED]) for b in range(2)]
        hnT = [sb(f"hnT{b}", [HALF, 2, TP]) for b in range(2)]

        colC, nC = columns(PACK_C)
        cc = sb("cc", [128, nC])
        Cc = {name: of(cc, colC, name) for name in colC}

        open_scope()
        colB, nB = columns(PACK_B)
        cb = sb("cb", [128, nB])
        Bc = {name: of(cb, colB, name) for name in colB}
        wqk = Bc["wqk"].rearrange("p (c n) -> p c n", c=2)
        wvg = Bc["wvg"].rearrange("p (c n) -> p c n", c=2)
        wo = Bc["wo"].rearrange("p (c n) -> p c n", c=2)
        causal = Bc["causal"].rearrange("p (c n) -> p c n", c=2)
        xy = sb("xy", [HALF, 2, NE, T * GB])
        phisq = sb("phisq", [HALF, 2, NE])
        ce = sb("ce", [TP, T, NE])
        image = Bc["image"][:, 0:GB]
        image_or_any = Bc["image"]
        w1s = [sb(f"w1s{q}", [HALF, 2, 2, HID]) for q in range(RING // 2)]
        w2s = [sb(f"w2s{q}", [128, 2, HB, ED]) for q in range(RING // 2)]
        b1s = Bc["b1s"].rearrange("p (n j) -> p n j", n=NE)

        open_scope()
        colA, nA = columns(PACK_A)
        ca = sb("ca", [128, nA])
        A = {name: of(ca, colA, name) for name in colA}
        wtok = A["wtok"].rearrange("p (k e) -> p k e", k=KC)
        xt = [sb(f"xt{q}", [TP, PD]) for q in range(4)]
        xT = [sb(f"xT{q}", [128, KC, TP]) for q in range(4)]
        wsums = sb("wsums", [TP, ED])
        xnm = [sb(f"xnm{b}", [TP, 1]) for b in range(2)]
        ybm = [sb(f"ybm{b}", [TP, ED]) for b in range(2)]
        yb = [sb(f"yb{b}", [TP, ED]) for b in range(2)]
        wtok_g = sb("wtok_g", [128, KC, ED])
        tok_bias = sb("tok_bias", [TP, ED])
        pos_bias = sb("pos_bias", [TP, ED])
        xst = [sb(f"xst{b}", [TP, 2, 6]) for b in range(2)]
        xmv = [sb(f"xmv{b}", [TP, 2]) for b in range(2)]
        xsd = [sb(f"xsd{b}", [TP, 1]) for b in range(2)]
        xrs = [sb(f"xrs{b}", [TP, 1]) for b in range(2)]
        y = [sb(f"y{b}", [TP, ED]) for b in range(2)]
        yn = [sb(f"yn{b}", [TP, ED]) for b in range(2)]
        yst = [sb(f"yst{b}", [TP, 6]) for b in range(2)]
        ymv = [sb(f"ymv{b}", [TP, 2]) for b in range(2)]
        ysd = [sb(f"ysd{b}", [TP, 1]) for b in range(2)]
        ynm = [sb(f"ynm{b}", [TP, 1]) for b in range(2)]
        yrs = [sb(f"yrs{b}", [TP, 1]) for b in range(2)]
        close_scope()

        open_scope()
        gate = sb("gate", [TP, T, ED])
        fe = [sb(f"fe{b}", [128, 4, TP]) for b in range(2)]
        fr = [sb(f"fr{b}", [128, 4, TP]) for b in range(2)]
        qk = [sb(f"qk{b}", [128, 4, TP]) for b in range(2)]
        vx = [sb(f"vx{b}", [TP, NH, DH]) for b in range(2)]
        am = [sb(f"am{b}", [TP, NH, TP]) for b in range(2)]
        den = [sb(f"den{b}", [128, 2, TP]) for b in range(2)]
        rden = [sb(f"rden{b}", [128, 2, TP]) for b in range(2)]
        oT = [sb(f"oT{b}", [128, 2, TP]) for b in range(2)]
        rg = [sb(f"rg{b}", [TP, ED]) for b in range(2)]
        close_scope()

        open_scope()
        phin = sb("phin", [HALF, 2, NE])
        phinv = sb("phinv", [HALF, NE])
        hnorm = sb("hnorm", [TP, T])
        xn = [sb(f"xn{q}", [TP, ED]) for q in range(8)]
        cneg = [sb(f"cneg{b}", [TP, 1]) for b in range(2)]
        cexp = [sb(f"cexp{b}", [TP, NE]) for b in range(2)]
        csum = [sb(f"csum{b}", [TP, 1]) for b in range(2)]
        crec = [sb(f"crec{b}", [TP, 1]) for b in range(2)]
        dmax = [sb(f"dmax{b}", [NE, GB]) for b in range(2)]
        dlog = [sb(f"dlog{b}", [NE, GB, S]) for b in range(2)]
        dexp = [sb(f"dexp{b}", [NE, GB, S]) for b in range(2)]
        dsum = [sb(f"dsum{b}", [NE, GB]) for b in range(2)]
        drec = [sb(f"drec{b}", [NE, GB]) for b in range(2)]
        dT = [sb(f"dT{b}", [128, GB, S]) for b in range(2)]
        dw = [sb(f"dw{b}", [TP, GB, NE]) for b in range(2)]

        w1s += [sb(f"w1s{q}", [HALF, 2, 2, HID]) for q in range(RING // 2, RING)]
        w2s += [sb(f"w2s{q}", [128, 2, HB, ED]) for q in range(RING // 2, RING)]
        xs = [sb(f"xs{b}", [HALF, 2, 2, B]) for b in range(2)]
        eh = [sb(f"eh{b}", [128, HB, 128]) for b in range(2)]
        eg = [sb(f"eg{b}", [128, HB, 2, B]) for b in range(2)]
        eo = [sb(f"eo{b}", [128, ED]) for b in range(2)]

        cw = [sb(f"cw{b}", [TP, GB + 1, NE]) for b in range(2)]
        e1 = [sb(f"e1{q}", [128, ED]) for q in range(4)]
        e2 = [sb(f"e2{q}", [128, ED]) for q in range(4)]
        c1 = [sb(f"c1{b}", [128, TP]) for b in range(2)]
        c2 = [sb(f"c2{b}", [128, TP]) for b in range(2)]
        close_scope()
        close_scope()

        open_scope()
        w13 = [sb(f"w13{b}", [HALF, 2, 2 * EH]) for b in range(2)]
        w2r = [sb(f"w2r{b}", [128, EH // 128, ED]) for b in range(2)]

        open_scope()
        masks = sb("masks", [TP, 4, KW])
        near = [sb(f"near{v}", [TP, NHN, KW]) for v in range(2)]
        bias = [sb(f"bias{v}", [TP, NHN, KW]) for v in range(4)]
        xg = sb("xg", [WN, XCOLS])
        kT = sb("kT", [WN, XCOLS])
        hp = [sb(f"hp{b}", [TP, 2, ED]) for b in range(2)]
        hpT = [sb(f"hpT{b}", [HALF, 2, PAIR]) for b in range(2)]
        fx = [sb(f"fx{b}", [WN, PAIR]) for b in range(2)]
        fa = [sb(f"fa{b}", [CONV, PAIR]) for b in range(2)]
        fs = [sb(f"fs{b}", [WN, PAIR]) for b in range(2)]
        vsrc = [sb(f"vsrc{b}", [WN, TP]) for b in range(2)]
        vn = [sb(f"vn{q}", [TP, NHN, VW]) for q in range(4)]
        vl = [sb(f"vl{i}", [TP, NHN, VW]) for i in range(3)]
        qx = [sb(f"qx{b}", [WN, NHN, TP]) for b in range(2)]
        nl = [sb(f"nl{q}", [TP, NHN, KW]) for q in range(4)]
        nm = [sb(f"nm{b}", [TP, NHN]) for b in range(2)]
        nn = [sb(f"nn{b}", [TP, NHN]) for b in range(2)]
        nsum = [sb(f"nsum{b}", [TP, NHN]) for b in range(2)]
        nr = [sb(f"nr{b}", [TP, NHN]) for b in range(2)]
        pTa = [sb(f"pTa{b}", [TP, NHN, 2, TP]) for b in range(2)]
        pTb = [sb(f"pTb{b}", [S, NHN, TP]) for b in range(2)]
        noT = [sb(f"noT{b}", [NHN * VW, TP]) for b in range(2)]
        nz = [sb(f"nz{b}", [WN, TP]) for b in range(2)]
        h2 = [sb(f"h2{b}", [TP, ED]) for b in range(2)]
        close_scope()

        open_scope()
        zk = sb("zk", [TP, T, ED])
        zsq = sb("zsq", [TP, T])
        zrt = sb("zrt", [TP, T])
        zs = sb("zs", [TP, T])
        eps6 = sb("eps6", [TP, 1])
        top = sb("top", [TP, 2, T])
        eq = sb("eq", [TP, T, EX])
        key = sb("key", [TP, T, EX])
        lg2 = sb("lg2", [TP, T, EX])
        expert = sb("expert", [TP, 2, T])
        hot = sb("hot", [TP, 2, T, EX])
        hots = sb("hots", [TP, T, EX])
        sums = [sb(f"sums{b}", [TP, T, EX]) for b in range(2)]
        place = sb("place", [TP, T, EX])
        picked = sb("picked", [TP, 2, T, EX])
        pk = sb("pk", [TP, 2, T])
        kept = sb("kept", [TP, 2, T])
        jt = sb("jt", [TP, 2, T])
        prow = sb("prow", [TP, 2, T])
        col = sb("col", [TP, 2, T])
        ohp = [sb(f"ohp{b}", [TP, 2, 2, SP_]) for b in range(2)]
        oht = [sb(f"oht{b}", [TP, 2, 2, NST]) for b in range(2)]
        ohc = [sb(f"ohc{b}", [TP, 2, 2, 2 * NST]) for b in range(2)]
        wslot = sb("wslot", [SP_, NST])
        empty = sb("empty", [SP_, NST])
        take_f = sb("take_f", [SP_, NST])
        put_f = sb("put_f", [SP_, NST])
        take = sb("take", [SP_, NST], I32)
        put = sb("put", [SP_, NST], I32)
        wexp = sb("wexp", [TP, T])
        wdif = sb("wdif", [TP, T])
        wsum = sb("wsum", [TP, T])
        wts = sb("wts", [TP, 2, T])
        own = sb("own", [TP, 2, T])
        zr = [sb(f"zr{b}", [SP_, SJ, ED]) for b in range(2)]
        zT = [sb(f"zT{b}", [HALF, 2, CAPP]) for b in range(2)]
        sg = [sb(f"sg{b}", [128, CAPP // 2]) for b in range(2)]
        hT = sb("hT", [128, EH // 128, CAPP])
        yr = [sb(f"yr{b}", [SP_, SJ, ED]) for b in range(2)]
        close_scope()
        close_scope()

        ys = nc.dram_tensor("ys", [B * NE, ED], F32, kind="Internal").ap()
        ys_of = ys.rearrange("(m n) d -> m n d", n=NE)

        z_rows = nc.dram_tensor("z_rows", [NROW, ED], F32, kind="Internal").ap()

        s_cci = sem("constants_c_in")
        s_nin = sem("near_tables_in")
        s_nb = sem("near_biases_ready")
        s_pad = sem("near_padding_set")
        s_f1 = sem("fc1_product")
        s_f1c = sem("fc1_biased")
        s_fA = sem("conva_product")
        s_fAc = sem("conva_biased")
        s_fB = sem("convb_product")
        s_fs = sem("convb_biased_summed")
        s_fg = sem("near_gelu")
        s_fK = sem("key_product")
        s_fKc = sem("keys_stored")
        s_fv = sem("value_source_copied")
        s_fV = sem("value_product")
        s_fVc = sem("values_stored")
        s_nQ = sem("query_product")
        s_nq = sem("queries_spread")
        s_nS = sem("near_scores")
        s_nl = sem("near_logits")
        s_nm = sem("near_maxima_negated")
        s_ne = sem("near_exp")
        s_nT = sem("near_weights_transposed")
        s_nTa = sem("near_wT_copied_act")
        s_nTd = sem("near_wT_copied_dve")
        s_nA = sem("near_av")
        s_nr = sem("near_reciprocal")
        s_nw = sem("near_weights_normalized")
        s_noc = sem("near_oT_copied")
        s_nP = sem("near_projected")
        s_nz = sem("near_projection_biased")
        s_nF = sem("fc2_product")
        s_ha = sem("h_plus_normalized")
        s_nh2 = sem("h_plus_fc2_bias")
        s_w13 = [sem(f"w13_in{b}") for b in range(2)]
        s_w2r = [sem(f"w2r_in{b}") for b in range(2)]
        s_gz = sem("z_stored")
        s_gl = sem("router_logits")
        s_r = sem("routing_steps")
        s_re = sem("routing_exp")
        s_rt = sem("routing_results")
        s_rp = sem("routing_prefix_product")
        s_oh = sem("slot_marks_made")
        s_oht = sem("slot_tile_marks_made")
        s_ohp = sem("slot_marks_product")
        s_zd = sem("z_rows_out")
        s_id = sem("own_rows_ready")
        s_ido = sem("own_rows_out")
        s_ad = sem("outputs_added")
        s_zr = [sem(f"slot_rows_in{b}") for b in range(2)]
        s_zT = sem("slot_rows_transposed")
        s_zc = [sem("zT_stored_act"), sem("zT_stored_dve")]
        s_gu = sem("gate_up_product")
        s_sg = sem("gate_silu")
        s_hT = sem("hidden_stored")
        s_yp = sem("routed_output_product")
        s_yc = [sem("routed_output_copied_act"), sem("routed_output_copied_dve")]
        s_eo = [sem(f"expert_output_out{b}") for b in range(2)]

        s_ph = sem("norm_constants_steps")
        s_phn = sem("phi_norms")
        s_phs = sem("phi_norm_roots")
        s_cns = sem("dispatch_norm_roots")
        s_cl = sem("dispatch_logits")
        s_ccm = sem("combine_max")
        s_cce = sem("combine_exp")
        s_ccr = sem("combine_reciprocal")
        s_ccw = sem("combine_weights")
        s_cdm = sem("dispatch_max")
        s_cdl = sem("dispatch_shifted")
        s_cde = sem("dispatch_exp")
        s_cds = sem("dispatch_sum_steps")
        s_cdT = sem("dispatch_weights_T")
        s_cdt = sem("dispatch_weights_transposed")
        s_cdw = sem("dispatch_weights_spread")
        s_cxs = sem("expert_input_product")
        s_cxc = sem("expert_input_stored")
        s_w1 = [sem(f"w1_in_then_expert_rows_in{q}") for q in range(RING)]
        n_w1 = 16 * NPAIR // RING
        s_w2 = [sem(f"w2_in{q}") for q in range(RING)]
        s_dx = sem("expert_inputs_staged")
        s_dh = sem("expert_hidden_product")
        s_dc = [sem("expert_hidden_copied_act"), sem("expert_hidden_copied_dve")]
        s_dt = sem("expert_hidden_transposed")
        s_db = sem("expert_hidden_biased")
        s_dg = sem("expert_hidden_gelu")
        s_dy = sem("expert_output_product")
        s_do = sem("expert_output_stored")
        s_ecw = sem("combine_weights_spread")
        s_eT = sem("combine_transposed")
        s_eTa = sem("combine_copied_act")
        s_eTd = sem("combine_copied_dve")
        s_ey = sem("combine_product")

        s_ln = sem("ln_constants_steps")
        s_cbi = sem("constants_b_in")
        s_hst = sem("h_stats")
        s_hsd = sem("h_std")
        s_hn = sem("h_normalized")
        s_hTr = sem("h_transposed")
        s_hTc = sem("hT_copied")
        s_bqk = sem("attn_qk_product")
        s_bvg = sem("attn_vg_product")
        s_bf = sem("attn_exp_relu")
        s_bq = sem("attn_qk_features")
        s_bv = sem("attn_v_gate")
        s_bs = sem("attn_scores")
        s_bam = sem("attn_scores_masked")
        s_bav = sem("attn_av")
        s_bd = sem("attn_den_steps")
        s_bon = sem("attn_out_normalized")
        s_bwo = sem("attn_projected")
        s_brg = sem("attn_gated")

        s_ca = sem("constants_a_in")
        s_eps = sem("eps_set")
        s_wg = sem("wtok_scaled")
        s_cb = sem("tok_bias_product")
        s_tb = sem("tok_bias_ready")
        s_pb = sem("pos_bias_ready")
        s_x = [sem(f"x_in{q}") for q in range(4)]
        s_xr = [sem(f"xT_in{q}") for q in range(4)]
        s_xsh = sem("x_shift_ready")
        s_ybm = sem("y_shift_product")
        s_yb = sem("y_shift_ready")
        s_xst = sem("x_stats")
        s_xmv = sem("x_mean_var")
        s_xsd = sem("x_std")
        s_xrs = sem("x_rstd")
        s_typ = sem("y_product")
        s_y = sem("y_biased")
        s_yst = sem("y_stats")
        s_ymv = sem("y_mean_var")
        s_ysd = sem("y_std")
        s_yrs = sem("y_rstd")
        s_ynm = sem("y_shift_factor")
        s_yn = sem("y_normalized")
        s_yg = sem("y_gained")
        s_h = sem("h_updated")

        def embed_sp(sp):
            sp.dma_start(ca[:], ins["ca"]).then_inc(s_ca, 16)
            sp.dma_start(ident, ins["ident"]).then_inc(s_ca, 16)

            def load_x(t, q):
                if after(t, 4):
                    sp.wait_ge(s_xst, t - 3)
                sp.dma_start(xt[q][:], ins["x"][t]).then_inc(s_x[q], 16)
                if after(t, 4):
                    sp.wait_ge(s_typ, t - 3)
                sp.dma_start(xT[q][:], ins["xT"][t]).then_inc(s_xr[q], 16)

            over_tiles(sp, [(0, load_x)], T, unroll=4)
            sp.dma_start(cb[:], ins["cb"]).then_inc(s_cbi, 16)
            sp.dma_start(cc[:], ins["cc"]).then_inc(s_cci, 16)

        def embed_pool(pool):
            nc.gpsimd.memset(eps5[:], 1e-5)
            nc.gpsimd.memset(ones[:], 1.0).then_inc(s_eps, 1)

            def shift(t, b):
                pool.wait_ge(s_xsh, t + 1)
                pool.wait_ge(s_tb, 1)
                if after(t, 2):
                    pool.wait_ge(s_y, t - 1)
                nc.gpsimd.tensor_tensor(pool_tick[:, b:b + 1], eps5[0:TP], eps5[0:TP], ALU.mult)
                nc.gpsimd.tensor_scalar(ybm[b][:], wsums[:], xnm[b][:], None, ALU.mult).then_inc(s_ybm, 1)
                pool.wait_ge(s_ybm, t + 1)
                nc.gpsimd.tensor_tensor(yb[b][:], ybm[b][:], tok_bias[:], ALU.add).then_inc(s_yb, 1)

            def gain(t, b):
                pool.wait_ge(s_yn, t + 1)
                pool.wait_ge(s_pb, 2)
                nc.gpsimd.tensor_tensor(yn[b][:], yn[b][:], A["g2m"], ALU.mult).then_inc(s_yg, 1)
                pool.wait_ge(s_yg, t + 1)
                nc.gpsimd.tensor_tensor(h[:, t, :], yn[b][:], pos_bias[:], ALU.add).then_inc(s_h, 1)

            over_tiles(pool, [(0, shift), (2, gain)], T)

        def h_std(act, layer):
            act.wait_ge(s_ln, 5 * layer + 4)
            nc.scalar.activation(hsd[:], hvar[:], ACT.Sqrt, bias=eps5[0:TP, :]).then_inc(s_hsd, 1)

        def h_norm_constants(dve, layer):
            n0 = 5 * layer
            dve.wait_ge(s_hst, T * (layer + 1))
            nc.vector.tensor_tensor(hmean[:], hst[:, :, 1], hst[:, :, 4], ALU.add)
            nc.vector.tensor_tensor(hdif[:], hst[:, :, 1], hst[:, :, 4], ALU.subtract)
            nc.vector.tensor_tensor(hvar[:], hst[:, :, 2], hst[:, :, 5], ALU.add).then_inc(s_ln, 1)
            dve.wait_ge(s_ln, n0 + 1)
            nc.vector.tensor_scalar(hmean[:], hmean[:], 0.5, None, ALU.mult)
            nc.vector.tensor_scalar(hvar[:], hvar[:], 1.0 / ED, None, ALU.mult)
            nc.vector.scalar_tensor_tensor(out=hdif[:], in0=hdif[:], scalar=0.25, in1=hdif[:], op0=ALU.mult, op1=ALU.mult).then_inc(s_ln, 2)
            dve.wait_ge(s_ln, n0 + 3)
            nc.vector.tensor_tensor(hvar[:], hvar[:], hdif[:], ALU.add).then_inc(s_ln, 1)
            dve.wait_ge(s_hsd, layer + 1)
            nc.vector.reciprocal(hrs[:], hsd[:]).then_inc(s_ln, 1)

        def attention_act(act):
            h_std(act, 0)

            def copy_hT(t, b):
                act.wait_ge(s_hTr, t + 1)
                if after(t, 2):
                    act.wait_ge(s_bvg, t - 1)
                nc.scalar.copy(hnT[b][:], bank[0][0:HALF, 0:2 * TP].rearrange("p (c q) -> p c q", c=2)).then_inc(s_hTc, 1)

            def features(t, b):
                act.wait_ge(s_bqk, t + 1)
                if after(t, 2):
                    act.wait_ge(s_bq, t - 1)
                p = bank[1][:, 0:4 * TP].rearrange("p (c q) -> p c q", c=4)
                nc.scalar.activation(fe[b][:], p, ACT.Exp)
                nc.scalar.activation(fr[b][:], p, ACT.Relu).then_inc(s_bf, 1)

            def values(t, b):
                act.wait_ge(s_bvg, t + 1)
                if after(t, 2):
                    act.wait_ge(s_bav, t - 1)
                nc.scalar.activation(gate[:, t, :], bank[2][0:TP, NH * DH:VGW], ACT.Tanh, scale=0.5)
                nc.scalar.copy(vx[b][:], bank[2][0:TP, 0:NH * DH].rearrange("p (h d) -> p h d", h=NH)).then_inc(s_bv, 1)

            over_tiles(act, [(0, copy_hT), (1, features), (1, values)], T)

        def embed_act(act):
            act.wait_ge(s_eps, 1)

            def std_x(t, b):
                act.wait_ge(s_xmv, t + 1)
                if after(t, 2):
                    act.wait_ge(s_xrs, t - 1)
                nc.scalar.activation(xsd[b][:], xmv[b][:, 1:2], ACT.Sqrt, bias=eps5[0:TP, :]).then_inc(s_xsd, 1)

            def std_y(t, b):
                act.wait_ge(s_ymv, t + 1)
                if after(t, 2):
                    act.wait_ge(s_yrs, t - 1)
                nc.scalar.activation(ysd[b][:], ymv[b][:, 1:2], ACT.Sqrt, bias=eps5[0:TP, :]).then_inc(s_ysd, 1)

            def norm_y(t, b):
                act.wait_ge(s_ynm, t + 1)
                if after(t, 2):
                    act.wait_ge(s_h, t - 1)
                nc.scalar.activation(yn[b][:], y[b][:], ACT.Identity, bias=ynm[b][:], scale=yrs[b][:]).then_inc(s_yn, 1)

            over_tiles(act, [(0, std_x), (2, std_y), (3, norm_y)], T)

        def embed_dve(dve):
            dve.wait_ge(s_ca, 32)
            for k in range(KC):
                last = nc.vector.tensor_scalar(wtok_g[:, k, :], wtok[:, k, :], A["g1"][:, k:k + 1], None, ALU.mult)
            last.then_inc(s_wg, 1)
            nc.vector.tensor_tensor(pos_bias[:], A["pos"], A["b2m"], ALU.add).then_inc(s_pb, 1)
            dve.wait_ge(s_pb, 1)
            nc.vector.tensor_tensor(pos_bias[:], pos_bias[:], A["cls"], ALU.add).then_inc(s_pb, 1)
            dve.wait_ge(s_cb, 2)
            nc.vector.tensor_copy(wsums[:], bank[6][0:TP, 0:ED])
            nc.vector.tensor_tensor(tok_bias[:], A["btok"], bank[7][0:TP, 0:ED], ALU.add).then_inc(s_tb, 1)
            dve.wait_ge(s_tb, 1)

            def stats_x(t, q):
                b = q % 2
                dve.wait_ge(s_x[q], (t - q) * 4 + 16)
                if after(t, 2):
                    dve.wait_ge(s_xmv, t - 1)
                nc.vector.bn_stats(xst[b][:, 0, :], xt[q][:, 0:PD // 2])
                nc.vector.bn_stats(xst[b][:, 1, :], xt[q][:, PD // 2:PD]).then_inc(s_xst, 1)
                dve.wait_ge(s_xst, t + 1)
                nc.vector.memset(tick[:, 4:5], 0.0)
                nc.vector.bn_aggr(xmv[b][:], xst[b][:]).then_inc(s_xmv, 1)

            def shift(t, q):
                b = q % 2
                dve.wait_ge(s_xsd, t + 1)
                if after(t, 2):
                    dve.wait_ge(s_yb, t - 1)
                nc.vector.reciprocal(xrs[b][:], xsd[b][:]).then_inc(s_xrs, 1)
                dve.wait_ge(s_xrs, t + 1)
                nc.vector.scalar_tensor_tensor(out=xnm[b][:], in0=xmv[b][:, 0:1], scalar=-1.0, in1=xrs[b][:], op0=ALU.mult, op1=ALU.mult).then_inc(s_xsh, 1)

            def bias_y(t, q):
                b = q % 2
                dve.wait_ge(s_typ, t + 1)
                dve.wait_ge(s_yb, t + 1)
                if after(t, 2):
                    dve.wait_ge(s_yn, t - 1)
                nc.vector.scalar_tensor_tensor(out=y[b][:], in0=bank[2 + b][0:TP, 0:ED], scalar=xrs[b][:], in1=yb[b][:], op0=ALU.mult, op1=ALU.add).then_inc(s_y, 1)
                dve.wait_ge(s_y, t + 1)
                nc.vector.bn_stats(yst[b][:], y[b][:]).then_inc(s_yst, 1)
                dve.wait_ge(s_yst, t + 1)
                nc.vector.memset(tick[:, 5:6], 0.0)
                nc.vector.bn_aggr(ymv[b][:], yst[b][:]).then_inc(s_ymv, 1)

            def norm_y(t, q):
                b = q % 2
                dve.wait_ge(s_ysd, t + 1)
                nc.vector.reciprocal(yrs[b][:], ysd[b][:]).then_inc(s_yrs, 1)
                dve.wait_ge(s_yrs, t + 1)
                if after(t, 2):
                    dve.wait_ge(s_yn, t - 1)
                nc.vector.scalar_tensor_tensor(out=ynm[b][:], in0=ymv[b][:, 0:1], scalar=-1.0, in1=yrs[b][:], op0=ALU.mult, op1=ALU.mult).then_inc(s_ynm, 1)

            def stats_h(t, b):
                dve.wait_ge(s_h, t + 1)
                nc.vector.bn_stats(hst[:, t, :], h[:, t, :]).then_inc(s_hst, 1)

            over_tiles(dve, [(0, stats_x), (1, shift), (2, bias_y), (3, norm_y), (4, stats_h)], T, unroll=4)

        def attention_dve(dve):
            h_norm_constants(dve, 0)
            dve.wait_ge(s_ln, 5)
            dve.wait_ge(s_cbi, 16)
            phi = Bc["phi"].rearrange("p (c n) -> p c n", c=2)
            nc.vector.tensor_tensor(phisq[:], phi, phi, ALU.mult).then_inc(s_ph, 1)

            def normalize(t, b):
                if after(t, 2):
                    dve.wait_ge(s_hTr, t - 1)
                nc.vector.tensor_scalar(hn[b][:], h[:, t, :], hmean[:, bass.ds(t, 1)], hrs[:, bass.ds(t, 1)], ALU.subtract, ALU.mult).then_inc(s_hn, 1)

            def feature(t, b):
                dve.wait_ge(s_bf, t + 1)
                if after(t, 2):
                    dve.wait_ge(s_bs, t - 1)
                nc.vector.scalar_tensor_tensor(out=qk[b][:], in0=fe[b][:], scalar=1.0, in1=fr[b][:], op0=ALU.min, op1=ALU.add).then_inc(s_bq, 1)

            def mask(t, b):
                dve.wait_ge(s_bs, t + 1)
                if after(t, 2):
                    dve.wait_ge(s_bav, t - 1)
                for half in range(2):
                    last = nc.vector.tensor_tensor(am[b][:, 2 * half:2 * half + 2, :], bank[3 + half][0:TP, 0:2 * TP].rearrange("p (c q) -> p c q", c=2), causal, ALU.mult)
                last.then_inc(s_bam, 1)

            def normalize_out(t, b):
                dve.wait_ge(s_bav, t + 1)
                nc.vector.tensor_scalar(den[b][:], bank[6][:, 0:2 * TP].rearrange("p (j q) -> p j q", j=2), 1e-6, None, ALU.max).then_inc(s_bd, 1)
                dve.wait_ge(s_bd, 2 * t + 1)
                nc.vector.reciprocal(rden[b][:], den[b][:]).then_inc(s_bd, 1)
                dve.wait_ge(s_bd, 2 * t + 2)
                if after(t, 2):
                    dve.wait_ge(s_bwo, t - 1)
                nc.vector.tensor_tensor(oT[b][:], bank[5][:, 0:2 * TP].rearrange("p (j q) -> p j q", j=2), rden[b][:], ALU.mult).then_inc(s_bon, 1)

            def residual(t, b):
                dve.wait_ge(s_bwo, t + 1)
                nc.vector.scalar_tensor_tensor(out=rg[b][:], in0=gate[:, t, :], scalar=1.0, in1=bank[7][0:TP, 0:ED], op0=ALU.add, op1=ALU.mult).then_inc(s_brg, 1)
                dve.wait_ge(s_brg, t + 1)
                nc.vector.scalar_tensor_tensor(out=h[:, t, :], in0=rg[b][:], scalar=0.5, in1=h[:, t, :], op0=ALU.mult, op1=ALU.add).then_inc(s_h, 1)
                dve.wait_ge(s_h, T + t + 1)
                nc.vector.bn_stats(hst[:, t, :], h[:, t, :]).then_inc(s_hst, 1)

            over_tiles(dve, [(0, normalize), (3, mask), (2, feature), (4, residual), (3, normalize_out)], T)

        def embed_pe(pe):
            pe.wait_ge(s_ca, 32)
            for k in range(KC):
                last = nc.tensor.matmul(bank[7][0:TP, 0:ED], A["b1"][:, k:k + 1].to_broadcast([128, TP]), wtok[:, k, :],
                                        start=(k == 0), stop=(k == KC - 1))
            last.then_inc(s_cb, 1)
            pe.wait_ge(s_wg, 1)
            pe.wait_ge(s_eps, 1)
            for k in range(KC):
                last = nc.tensor.matmul(bank[6][0:TP, 0:ED], ones[:, 0:TP], wtok_g[:, k, :], start=(k == 0), stop=(k == KC - 1))
            last.then_inc(s_cb, 1)

            def product(t, q):
                pe.wait_ge(s_xr[q], (t - q) * 4 + 16)
                if after(t, 2):
                    pe.wait_ge(s_y, t - 1)
                for k in range(KC):
                    last = nc.tensor.matmul(bank[2 + q % 2][0:TP, 0:ED], xT[q][:, k, :], wtok_g[:, k, :], start=(k == 0), stop=(k == KC - 1))
                last.then_inc(s_typ, 1)

            over_tiles(pe, [(0, product)], T, unroll=4)

        def attention_pe(pe):
            pe.wait_ge(s_cbi, 16)

            def transpose_h(t, b):
                pe.wait_ge(s_hn, t + 1)
                if after(t, 1):
                    pe.wait_ge(s_hTc, t)
                for c in range(2):
                    last = nc.tensor.transpose(bank[0][0:HALF, c * TP:(c + 1) * TP], hn[b][:, c * HALF:(c + 1) * HALF], ident[0:TP, 0:TP])
                last.then_inc(s_hTr, 1)

            def products(t, b):
                pe.wait_ge(s_hTc, t + 1)
                if after(t, 1):
                    pe.wait_ge(s_bf, t)
                for j in range(4):
                    for c in range(2):
                        last = nc.tensor.matmul(bank[1][:, j * TP:(j + 1) * TP], wqk[:, c, j * 128:(j + 1) * 128], hnT[b][:, c, :], start=(c == 0), stop=(c == 1))
                last.then_inc(s_bqk, 1)
                if after(t, 1):
                    pe.wait_ge(s_bv, t)
                for c in range(2):
                    last = nc.tensor.matmul(bank[2][0:TP, 0:VGW], hnT[b][:, c, :], wvg[:, c, :], start=(c == 0), stop=(c == 1))
                last.then_inc(s_bvg, 1)

            def scores(t, b):
                pe.wait_ge(s_bq, t + 1)
                if after(t, 1):
                    pe.wait_ge(s_bam, t)
                for j in range(2):
                    for r in range(2):
                        last = nc.tensor.matmul(bank[3 + r][0:TP, j * TP:(j + 1) * TP], qk[b][64 * r:64 * r + 64, 2 + j, :], qk[b][64 * r:64 * r + 64, j, :], start=True, stop=True)
                last.then_inc(s_bs, 1)

            def values(t, b):
                pe.wait_ge(s_bam, t + 1)
                pe.wait_ge(s_bv, t + 1)
                if after(t, 1):
                    pe.wait_ge(s_bon, t)
                for j in range(2):
                    for r in range(2):
                        half = slice(64 * r, 64 * r + 64)
                        nc.tensor.matmul(bank[5][half, j * TP:(j + 1) * TP], vx[b][:, 2 * j + r, :], am[b][:, 2 * r + j, :], start=True, stop=True)
                for r in range(2):
                    last = nc.tensor.matmul(bank[6][64 * r:64 * r + 64, 0:2 * TP], ones[0:TP, 0:64], am[b][:, 2 * r:2 * r + 2, :].rearrange("p j q -> p (j q)"), start=True, stop=True)
                last.then_inc(s_bav, 1)

            def project(t, b):
                pe.wait_ge(s_bon, t + 1)
                if after(t, 1):
                    pe.wait_ge(s_brg, t)
                for j in range(2):
                    last = nc.tensor.matmul(bank[7][0:TP, 0:ED], oT[b][:, j, :], wo[:, j, :], start=(j == 0), stop=(j == 1))
                last.then_inc(s_bwo, 1)

            over_tiles(pe, [(0, transpose_h), (2, scores), (1, products), (3, project), (2, values)], T)

        def dispatch_act(act):
            act.wait_ge(s_phn, 1)
            nc.scalar.activation(phinv[:], bank[7][0:HALF, 0:NE], ACT.Sqrt).then_inc(s_phs, 1)
            h_std(act, 1)
            act.wait_ge(s_ln, 5 + 4)
            nc.scalar.activation(hnorm[:], hvar[:], ACT.Sqrt, scale=float(ED)).then_inc(s_cns, 1)

            def copy_T(t, q):
                b = q % 2
                act.wait_ge(s_hTr, T + t + 1)
                if after(t, 2):
                    act.wait_ge(s_cl, t - 1)
                nc.scalar.copy(hnT[b][:], bank[0][0:HALF, 0:2 * TP].rearrange("p (c q) -> p c q", c=2)).then_inc(s_hTc, 1)

            def exps(t, q):
                b = q % 2
                act.wait_ge(s_ccm, t + 1)
                if after(t, 2):
                    act.wait_ge(s_ccw, t - 1)
                nc.scalar.activation(cexp[b][:], bank[1][0:TP, 0:NE], ACT.Exp, bias=cneg[b][:], accum_out=csum[b][:]).then_inc(s_cce, 1)
                act.wait_ge(s_cdl, t + 1)
                nc.scalar.activation(dexp[b][:], dlog[b][:], ACT.Exp).then_inc(s_cde, 1)

            def store(t, q):
                b = q % 2
                act.wait_ge(s_cxs, t + 1)
                p = bank[4][0:HALF, 0:2 * GB * NE].rearrange("p (c g n) -> p c g n", c=2, g=GB)
                for c in range(2):
                    last = nc.scalar.copy(xy[:, c, :, bass.ds(t * GB, GB)].rearrange("p n g -> p g n"), p[:, c])
                last.then_inc(s_cxc, 1)

            over_tiles(act, [(0, copy_T), (1, exps), (4, store)], T, unroll=8)

        def dispatch_dve(dve):
            dve.wait_ge(s_phs, 1)
            nc.vector.tensor_scalar(phinv[:], phinv[:], 1e-12, None, ALU.max).then_inc(s_ph, 1)
            dve.wait_ge(s_ph, 2)
            nc.vector.reciprocal(phinv[:], phinv[:]).then_inc(s_ph, 1)
            dve.wait_ge(s_ph, 3)
            nc.vector.tensor_scalar(phinv[:], phinv[:], Bc["scale"], None, ALU.mult).then_inc(s_ph, 1)
            dve.wait_ge(s_ph, 4)
            for b in range(2):
                nc.vector.memset(dT[b][NE:128], 0.0)
            nc.vector.tensor_tensor(phin[:], Bc["phi"].rearrange("p (c n) -> p c n", c=2), phinv[:].unsqueeze(1).to_broadcast([HALF, 2, NE]), ALU.mult).then_inc(s_ph, 1)
            h_norm_constants(dve, 1)
            dve.wait_ge(s_ln, 10)
            dve.wait_ge(s_cns, 1)
            nc.vector.tensor_tensor(hnorm[:], hnorm[:], hrs[:], ALU.mult).then_inc(s_ph, 1)
            dve.wait_ge(s_ph, 6)
            nc.vector.tensor_scalar(hnorm[:], hnorm[:], 1e-12, None, ALU.max).then_inc(s_ph, 1)
            dve.wait_ge(s_ph, 7)
            nc.vector.reciprocal(hnorm[:], hnorm[:]).then_inc(s_ph, 1)
            dve.wait_ge(s_ph, 8)
            nc.vector.tensor_tensor(hnorm[:], hnorm[:], hrs[:], ALU.mult).then_inc(s_ph, 1)
            dve.wait_ge(s_ph, 9)

            def normalize(t, q):
                b = q % 2
                if after(t, 8):
                    dve.wait_ge(s_cxs, t - 7)
                nc.vector.tensor_scalar(xn[q][:], h[:, t, :], hmean[:, bass.ds(t, 1)], hnorm[:, bass.ds(t, 1)], ALU.subtract, ALU.mult).then_inc(s_hn, 1)

            def maxima(t, q):
                b = q % 2
                dve.wait_ge(s_cl, t + 1)
                if after(t, 2):
                    dve.wait_ge(s_cce, t - 1)
                nc.vector.tensor_reduce(cneg[b][:], bank[1][0:TP, 0:NE], AX.X, ALU.max, negate=True).then_inc(s_ccm, 1)
                p = bank[2][0:NE, 0:TP].rearrange("p (g m) -> p g m", g=GB)
                nc.vector.tensor_reduce(dmax[b][:], p, AX.X, ALU.max).then_inc(s_cdm, 1)
                dve.wait_ge(s_cdm, t + 1)
                if after(t, 2):
                    dve.wait_ge(s_cde, t - 1)
                nc.vector.tensor_tensor(dlog[b][:], p, dmax[b][:].unsqueeze(2).to_broadcast([NE, GB, S]), ALU.subtract).then_inc(s_cdl, 1)

            def weights(t, q):
                b = q % 2
                dve.wait_ge(s_cce, t + 1)
                nc.vector.reciprocal(crec[b][:], csum[b][:]).then_inc(s_ccr, 1)
                dve.wait_ge(s_cde, t + 1)
                nc.vector.tensor_reduce(dsum[b][:], dexp[b][:], AX.X, ALU.add).then_inc(s_cds, 1)
                dve.wait_ge(s_ccr, t + 1)
                nc.vector.tensor_scalar(ce[:, t, :], cexp[b][:], crec[b][:], None, ALU.mult).then_inc(s_ccw, 1)
                dve.wait_ge(s_cds, 2 * t + 1)
                nc.vector.reciprocal(drec[b][:], dsum[b][:]).then_inc(s_cds, 1)
                dve.wait_ge(s_cds, 2 * t + 2)
                if after(t, 2):
                    dve.wait_ge(s_cdt, t - 1)
                nc.vector.tensor_tensor(dT[b][0:NE], dexp[b][:], drec[b][:].unsqueeze(2).to_broadcast([NE, GB, S]), ALU.mult).then_inc(s_cdT, 1)

            def spread(t, q):
                b = q % 2
                dve.wait_ge(s_cdt, t + 1)
                if after(t, 2):
                    dve.wait_ge(s_cxs, t - 1)
                nc.vector.tensor_tensor(dw[b][:], bank[3][0:TP, 0:NE].unsqueeze(1).to_broadcast([TP, GB, NE]), image.unsqueeze(2).to_broadcast([TP, GB, NE]), ALU.mult).then_inc(s_cdw, 1)

            over_tiles(dve, [(0, normalize), (4, spread), (1, maxima), (2, weights)], T, unroll=8)

        def dispatch_pe(pe):
            pe.wait_ge(s_ph, 1)
            pe.wait_ge(s_brg, T)
            for c in range(2):
                last = nc.tensor.matmul(bank[7][0:HALF, 0:NE], ones[0:HALF, 0:HALF], phisq[:, c, :], start=(c == 0), stop=(c == 1))
            last.then_inc(s_phn, 1)
            pe.wait_ge(s_ph, 5)

            def transpose_x(t, q):
                b = q % 2
                pe.wait_ge(s_hn, T + t + 1)
                if after(t, 1):
                    pe.wait_ge(s_hTc, T + t)
                for c in range(2):
                    last = nc.tensor.transpose(bank[0][0:HALF, c * TP:(c + 1) * TP], xn[q][:, c * HALF:(c + 1) * HALF], ident[0:TP, 0:TP])
                last.then_inc(s_hTr, 1)

            def logits(t, q):
                b = q % 2
                pe.wait_ge(s_hTc, T + t + 1)
                if after(t, 1):
                    pe.wait_ge(s_cce, t)
                    pe.wait_ge(s_cdl, t)
                for c in range(2):
                    nc.tensor.matmul(bank[1][0:TP, 0:NE], hnT[b][:, c, :], phin[:, c, :], start=(c == 0), stop=(c == 1))
                for c in range(2):
                    last = nc.tensor.matmul(bank[2][0:NE, 0:TP], phin[:, c, :], hnT[b][:, c, :], start=(c == 0), stop=(c == 1))
                last.then_inc(s_cl, 1)

            def transpose_d(t, q):
                b = q % 2
                pe.wait_ge(s_cdT, t + 1)
                if after(t, 1):
                    pe.wait_ge(s_cdw, t)
                nc.tensor.transpose(bank[3][0:TP, 0:128], dT[b][:].rearrange("p g m -> p (g m)"), ident).then_inc(s_cdt, 1)

            def inputs(t, q):
                b = q % 2
                pe.wait_ge(s_cdw, t + 1)
                if after(t, 1):
                    pe.wait_ge(s_cxc, t)
                for c in range(2):
                    last = nc.tensor.matmul(bank[4][0:HALF, c * GB * NE:(c + 1) * GB * NE], xn[q][:, c * HALF:(c + 1) * HALF], dw[b][:].rearrange("p g n -> p (g n)"), start=True, stop=True)
                last.then_inc(s_cxs, 1)

            over_tiles(pe, [(1, logits), (0, transpose_x), (4, inputs), (3, transpose_d)], T, unroll=8)

        def experts_sp(sp):
            def load(p, q):
                if isinstance(p, int) and p == RING // 2:
                    sp.wait_ge(s_h, 2 * T)
                if after(p, RING):
                    sp.wait_ge(s_dh, p - RING + 1)
                sp.dma_start(w1s[q][:], ins["w1"][p]).then_inc(s_w1[q], 16)
                if after(p, RING):
                    sp.wait_ge(s_dy, p - RING + 1)
                sp.dma_start(w2s[q][:], ins["w2"][p]).then_inc(s_w2[q], 16)

            def store(p, q):
                b = q % 2
                sp.wait_ge(s_do, p + 1)
                for e in range(2):
                    sp.dma_start(ys_of[:, bass.ds(2 * p + e, 1), :], eo[b][e * B:(e + 1) * B]).then_inc(s_eo[b], 16)

            over_tiles(sp, [(0, load), (RING, store)], NPAIR, unroll=RING)

        def experts_pool(pool):
            pool.wait_ge(s_cxc, T)

            def stage(p, q):
                b = q % 2
                if after(p, 2):
                    pool.wait_ge(s_dh, p - 1)
                nc.gpsimd.tensor_copy(xs[b][:], xy[:, :, bass.ds(2 * p, 2), 0:B]).then_inc(s_dx, 1)

            over_tiles(pool, [(0, stage)], NPAIR, unroll=RING)

        def experts_act(act):
            def copy_h(p, q):
                b = q % 2
                act.wait_ge(s_dh, p + 1)
                if after(p, 2):
                    act.wait_ge(s_dt, p - 1)
                nc.scalar.copy(eh[b][:, 0:HB // 2], hidden_bank(b, 0)).then_inc(s_dc[0], 1)

            def gelu(p, q):
                b = q % 2
                act.wait_ge(s_db, p + 1)
                nc.scalar.activation(eg[b][:], eg[b][:], ACT.Gelu).then_inc(s_dg, 1)

            def output(p, q):
                b = q % 2
                act.wait_ge(s_dy, p + 1)
                if after(p, 2):
                    act.wait_ge(s_eo[b], 16 * (p - b))
                nc.scalar.copy(eo[b][:], bank[6 + b][:, 0:ED]).then_inc(s_do, 1)

            over_tiles(act, [(0, copy_h), (1, gelu), (2, output)], NPAIR, unroll=RING)

        def hidden_bank(b, part):
            return bank[2 * b + part][:, 0:HB // 2 * 128].rearrange("p (j k) -> p j k", j=HB // 2)

        def experts_dve(dve):
            def copy_h(p, q):
                b = q % 2
                dve.wait_ge(s_dh, p + 1)
                if after(p, 2):
                    dve.wait_ge(s_dt, p - 1)
                nc.vector.tensor_copy(eh[b][:, HB // 2:HB], hidden_bank(b, 1)).then_inc(s_dc[1], 1)

            def bias(p, q):
                b = q % 2
                dve.wait_ge(s_dt, p + 1)
                if after(p, 2):
                    dve.wait_ge(s_dy, p - 1)
                for g in range(2):
                    js = slice(g * HB // 2, (g + 1) * HB // 2)
                    h4 = bank[4 + g][:, 0:HB // 2 * 128].rearrange("p (j e m) -> p j e m", j=HB // 2, e=2)
                    b4 = b1s[:, bass.ds(2 * p, 2), js].rearrange("p e j -> p j e").unsqueeze(3).to_broadcast([128, HB // 2, 2, B])
                    last = nc.vector.tensor_tensor(eg[b][:, js], h4, b4, ALU.add)
                last.then_inc(s_db, 1)

            over_tiles(dve, [(0, copy_h), (1, bias)], NPAIR, unroll=RING)

        def experts_pe(pe):
            pe.wait_ge(s_cxc, T)

            def hidden(p, q):
                b = q % 2
                pe.wait_ge(s_w1[q], 16 // RING * (p - q) + 16)
                pe.wait_ge(s_dx, p + 1)
                if after(p, 2):
                    pe.wait_ge(s_dc[0], p - 1)
                    pe.wait_ge(s_dc[1], p - 1)
                for part in range(2):
                    cols = slice(part * HID // 2, (part + 1) * HID // 2)
                    for c in range(2):
                        for e in range(2):
                            last = nc.tensor.matmul(bank[2 * b + part][e * B:(e + 1) * B, 0:HID // 2], xs[b][:, c, e, :], w1s[q][:, e, c, cols], start=(c == 0), stop=(c == 1))
                last.then_inc(s_dh, 1)

            def transposes(p, q):
                b = q % 2
                pe.wait_ge(s_dc[0], p + 1)
                pe.wait_ge(s_dc[1], p + 1)
                if after(p, 1):
                    pe.wait_ge(s_db, p)
                for j in range(HB):
                    k = j % (HB // 2) * 128
                    last = nc.tensor.transpose(bank[4 + j // (HB // 2)][:, k:k + 128], eh[b][:, j, :], ident)
                last.then_inc(s_dt, 1)

            def output(p, q):
                b = q % 2
                pe.wait_ge(s_w2[q], 16 // RING * (p - q) + 16)
                pe.wait_ge(s_dg, p + 1)
                if after(p, 2):
                    pe.wait_ge(s_do, p - 1)
                for j in range(HB):
                    for e in range(2):
                        last = nc.tensor.matmul(bank[6 + b][e * B:(e + 1) * B, 0:ED], eg[b][:, j, e, :], w2s[q][:, e, j, :], start=(j == 0), stop=(j == HB - 1))
                last.then_inc(s_dy, 1)

            over_tiles(pe, [(0, hidden), (1, transposes), (2, output)], NPAIR, unroll=RING)

        def combine_sp(sp):
            for q in range(4):
                sp.dma_start(e2[q][NE:2 * NE], ins["b2"]).then_inc(s_cbi, 16)
            for b in range(2):
                sp.wait_ge(s_eo[b], 16 * NPAIR)

            def load(t, q):
                if after(t, 4):
                    sp.wait_ge(s_ey, t - 3)
                first = t * GB * NE
                if isinstance(t, int) and t == T - 1:
                    sp.dma_start(e1[q][0:NE], ys[first:first + NE]).then_inc(s_w1[q], 16)
                else:
                    sp.dma_start(e1[q][:], ys[bass.ds(first, 2 * NE)]).then_inc(s_w1[q], 16)
                    sp.dma_start(e2[q][0:NE], ys[bass.ds(first + 2 * NE, NE)]).then_inc(s_w1[q], 16)

            over_tiles(sp, [(0, load)], T, unroll=4, tail=1)

        def combine_act(act):
            def copy(t, b):
                act.wait_ge(s_eT, t + 1)
                if after(t, 2):
                    act.wait_ge(s_ey, t - 1)
                nc.scalar.copy(c1[b][:], bank[6][:, 0:TP]).then_inc(s_eTa, 1)

            over_tiles(act, [(0, copy)], T)

        def combine_dve(dve):
            def spread(t, b):
                if after(t, 2):
                    dve.wait_ge(s_eT, t - 1)
                nc.vector.tensor_tensor(cw[b][:], ce[:, t, :].unsqueeze(1).to_broadcast([TP, GB + 1, NE]), image_or_any.unsqueeze(2).to_broadcast([TP, GB + 1, NE]), ALU.mult).then_inc(s_ecw, 1)

            def copy(t, b):
                dve.wait_ge(s_eT, t + 1)
                if after(t, 2):
                    dve.wait_ge(s_ey, t - 1)
                nc.vector.tensor_copy(c2[b][:], bank[7][:, 0:TP]).then_inc(s_eTd, 1)

            def residual(t, b):
                dve.wait_ge(s_ey, t + 1)
                nc.vector.tensor_tensor(h[:, t, :], h[:, t, :], bank[b][0:TP, 0:ED], ALU.add).then_inc(s_h, 1)
                dve.wait_ge(s_h, 2 * T + t + 1)
                nc.vector.bn_stats(hst[:, t, :], h[:, t, :]).then_inc(s_hst, 1)

            over_tiles(dve, [(0, spread), (1, copy), (2, residual)], T)

        def combine_pe(pe):
            pe.wait_ge(s_do, NPAIR)
            pe.wait_ge(s_cbi, 16 + 64)

            def transposes(t, q):
                b = q % 2
                pe.wait_ge(s_ecw, t + 1)
                if after(t, 1):
                    pe.wait_ge(s_eTa, t)
                    pe.wait_ge(s_eTd, t)
                spread = cw[b][:].rearrange("p g n -> p (g n)")
                nc.tensor.transpose(bank[6][:, 0:TP], spread[:, 0:128], ident[0:TP, 0:TP])
                nc.tensor.transpose(bank[7][:, 0:TP], spread[:, 128:4 * NE], ident[0:TP, 0:TP]).then_inc(s_eT, 1)

            def product(t, q):
                b = q % 2
                pe.wait_ge(s_eTa, t + 1)
                pe.wait_ge(s_eTd, t + 1)
                pe.wait_ge(s_w1[q], 8 * (t - q) + n_w1 + (16 if isinstance(t, int) and t == T - 1 else 32))
                if after(t, 2):
                    pe.wait_ge(s_h, 2 * T + t - 1)
                nc.tensor.matmul(bank[b][0:TP, 0:ED], c1[b][:], e1[q][:], start=True, stop=False)
                nc.tensor.matmul(bank[b][0:TP, 0:ED], c2[b][:], e2[q][:], start=False, stop=True).then_inc(s_ey, 1)

            over_tiles(pe, [(0, transposes), (1, product)], T, unroll=4)

        def value_columns(j):
            return j * TP if not isinstance(j, int) or j <= T else (B - WIN + PADR) * S + (j - T - 1) * TP

        def value_tiles(t):
            if isinstance(t, int):
                return [T + 1, T + 2, T + 3] if t == T - 1 else [t + 2]
            return [t + 2]

        def near_sp(sp):
            sp.wait_ge(s_ey, T)
            sp.dma_start(masks[:], ins["masks"]).then_inc(s_nin, 16)
            for v in range(2):
                sp.dma_start(near[v][:], ins["near"][v]).then_inc(s_nin, 16)
            for b in range(2):
                sp.dma_start(w13[b][:], ins["w13"][b]).then_inc(s_w13[b], 16)
                sp.dma_start(w2r[b][:], ins["w2r"][b]).then_inc(s_w2r[b], 16)

        def near_pool(pool):
            pool.wait_ge(s_ey, T)
            nc.gpsimd.memset(xg[:, 0:PADR * S], 0.0)
            nc.gpsimd.memset(xg[:, XCOLS - PADR * S:XCOLS], 0.0)
            nc.gpsimd.memset(kT[:, 0:PADR * S], 0.0)
            nc.gpsimd.memset(kT[:, XCOLS - PADR * S:XCOLS], 0.0)
            for v in vn + vl:
                last = nc.gpsimd.memset(v[:], 0.0)
            last.then_inc(s_pad, 1)

            def add_normalized(p, b):
                pool.wait_ge(s_hn, 2 * T + 2 * p + 2)
                nc.gpsimd.tensor_tensor(h[:, bass.ds(2 * p, 2), :], h[:, bass.ds(2 * p, 2), :], hp[b][:], ALU.add).then_inc(s_ha, 1)

            def tables(p, b):
                todo = {0: [2], 1: [3], T // 2 - 1: [0, 1]}.get(p, []) if isinstance(p, int) else []
                for v in todo:
                    pool.wait_ge(s_nin, 48)
                    nc.gpsimd.tensor_tensor(bias[v][:], near[v == 3][:], masks[:, v, :].unsqueeze(1).to_broadcast([TP, NHN, KW]), ALU.add).then_inc(s_nb, 1)

            over_tiles(pool, [(0, add_normalized), (0, tables)], T // 2)
            pool.wait_ge(s_ha, T // 2)
            pool.wait_ge(s_fg, T // 2)

            def source(j):
                if after(j, 2):
                    pool.wait_ge(s_fV, j - 1)
                nc.gpsimd.tensor_copy(vsrc[j % 2 if isinstance(j, int) else source.b][:], xg[:, bass.ds(value_columns(j), TP)]).then_inc(s_fv, 1)

            def sources(t, q):
                source.b = q % 2
                for j in value_tiles(t):
                    source(j)

            def normalize_w(t, q):
                b = q % 2
                pool.wait_ge(s_nr, t + 1)
                nc.gpsimd.tensor_tensor(nl[q][:], nl[q][:], nr[b][:].unsqueeze(2).to_broadcast([TP, NHN, KW]), ALU.mult).then_inc(s_nw, 1)

            def residual(t, q):
                b = q % 2
                if after(t, 2):
                    pool.wait_ge(s_h, 3 * T + t - 1)
                nc.gpsimd.tensor_tensor(h2[b][:], h[:, t, :], Cc["bfc2"], ALU.add).then_inc(s_nh2, 1)

            for j in range(2):
                source(j)
            over_tiles(pool, [(2, sources), (2, normalize_w), (5, residual)], T, unroll=4, tail=2)

        def near_act(act):
            h_std(act, 2)

            def copy_T(p, b):
                act.wait_ge(s_hTr, 2 * T + p + 1)
                if after(p, 2):
                    act.wait_ge(s_f1, p - 1)
                nc.scalar.copy(hpT[b][:], bank[0][0:HALF, 0:2 * PAIR].rearrange("p (c q) -> p c q", c=2)).then_inc(s_hTc, 1)

            def conva(p, b):
                act.wait_ge(s_fA, p + 1)
                if after(p, 2):
                    act.wait_ge(s_fB, p - 1)
                nc.scalar.activation(fa[b][:], bank[2][0:CONV, 0:PAIR], ACT.Identity, bias=Cc["bconva"]).then_inc(s_fAc, 1)

            def gelu(p, b):
                act.wait_ge(s_fs, p + 1)
                nc.scalar.activation(xg[:, bass.ds(PADR * S + p * PAIR, PAIR)], fs[b][:], ACT.Gelu).then_inc(s_fg, 1)

            over_tiles(act, [(0, copy_T), (2, conva), (3, gelu)], T // 2)

        def near_dve(dve):
            h_norm_constants(dve, 2)
            dve.wait_ge(s_ln, 15)
            dve.wait_ge(s_cci, 16)
            dve.wait_ge(s_pad, 1)

            def normalize(p, b):
                if after(p, 2):
                    dve.wait_ge(s_hTr, 2 * T + p - 1)
                    dve.wait_ge(s_ha, p - 1)
                for i in range(2):
                    last = nc.vector.tensor_scalar(hp[b][:, i, :], h[:, 2 * p + i, :], hmean[:, bass.ds(2 * p + i, 1)], hrs[:, bass.ds(2 * p + i, 1)], ALU.subtract, ALU.mult)
                last.then_inc(s_hn, 2)

            def fc1(p, b):
                dve.wait_ge(s_f1, p + 1)
                if after(p, 2):
                    dve.wait_ge(s_fs, p - 1)
                    dve.wait_ge(s_fA, p - 1)
                nc.vector.tensor_scalar(fx[b][:], bank[1][0:WN, 0:PAIR], Cc["bfc1"], None, ALU.add).then_inc(s_f1c, 1)

            def convb(p, b):
                dve.wait_ge(s_fB, p + 1)
                if after(p, 2):
                    dve.wait_ge(s_fg, p - 1)
                nc.vector.scalar_tensor_tensor(out=fs[b][:], in0=bank[3][0:WN, 0:PAIR], scalar=Cc["bconvb"], in1=fx[b][:], op0=ALU.add, op1=ALU.add).then_inc(s_fs, 1)

            def keys(p, b):
                dve.wait_ge(s_fK, p + 1)
                nc.vector.tensor_scalar(kT[:, bass.ds(PADR * S + p * PAIR, PAIR)], bank[4][0:WN, 0:PAIR], Cc["bk"], None, ALU.add).then_inc(s_fKc, 1)

            over_tiles(dve, [(0, normalize), (4, convb), (2, fc1), (5, keys)], T // 2)

            def spread(t, q):
                b = q % 2
                dve.wait_ge(s_nQ, t + 1)
                if after(t, 3):
                    dve.wait_ge(s_fV, t)
                if after(t, 2):
                    dve.wait_ge(s_nS, 4 * t - 4)
                nc.vector.scalar_tensor_tensor(out=qx[b][:], in0=bank[0][0:WN, 0:TP].unsqueeze(1).to_broadcast([WN, NHN, TP]), scalar=Cc["bq"], in1=Cc["head"].unsqueeze(2).to_broadcast([WN, NHN, TP]), op0=ALU.add, op1=ALU.mult).then_inc(s_nq, 1)

            def value(j, dst):
                dve.wait_ge(s_fV, j + 1)
                nc.vector.tensor_tensor(dst[:, :, 0:DN], bank[0][0:TP, 128:128 + WN].rearrange("p (h d) -> p h d", h=NHN), Cc["bv"].rearrange("p (h d) -> p h d", h=NHN), ALU.add).then_inc(s_fVc, 1)

            def values(t, q):
                if after(t, 2):
                    dve.wait_ge(s_nA, t - 1)
                for i, j in enumerate(value_tiles(t)):
                    value(j, vl[i] if isinstance(t, int) and t == T - 1 else vn[(q + 2) % 4])

            for j in range(2):
                value(j, vn[j])

            def logits(t, q):
                b = q % 2
                v = {0: 0, T - 2: 2, T - 1: 3}.get(t, 1) if isinstance(t, int) else 1
                if after(t, 2):
                    dve.wait_ge(s_ne, t - 1)
                if after(t, 4):
                    dve.wait_ge(s_nT, t - 3)
                for head in range(NHN):
                    dve.wait_ge(s_nS, 4 * t + head + 1)
                    if isinstance(t, int) and t < 2:
                        dve.wait_ge(s_nb, 3 + t)
                    nc.vector.memset(tick[:, head:head + 1], 0.0)
                    nc.vector.tensor_tensor_reduce(nl[q][:, head, :], bank[1 + head % 2][0:TP, 0:KW], bias[v][:, head, :], 1.0, -3.0e38, ALU.add, ALU.max, nm[b][:, head:head + 1]).then_inc(s_nl, 1)
                dve.wait_ge(s_nl, 4 * t + 4)
                nc.vector.tensor_scalar(nn[b][:], nm[b][:], -1.0, None, ALU.mult).then_inc(s_nm, 1)

            def reciprocal(t, q):
                b = q % 2
                dve.wait_ge(s_ne, t + 1)
                if after(t, 2):
                    dve.wait_ge(s_nw, t - 1)
                nc.vector.reciprocal(nr[b][:], nsum[b][:]).then_inc(s_nr, 1)

            def copy_w(t, q):
                b = q % 2
                dve.wait_ge(s_nT, t + 1)
                if after(t, 2):
                    dve.wait_ge(s_nA, t - 1)
                nc.vector.tensor_copy(pTa[b][:, 2:4], bank[4][0:TP, 0:4 * TP].rearrange("p (h c q) -> p h c q", h=2, c=2)).then_inc(s_nTd, 1)

            def residual(t, q):
                b = q % 2
                dve.wait_ge(s_nF, t + 1)
                dve.wait_ge(s_nh2, t + 1)
                nc.vector.tensor_tensor(h[:, t, :], bank[7][0:TP, 0:ED], h2[b][:], ALU.add).then_inc(s_h, 1)
                dve.wait_ge(s_h, 3 * T + t + 1)
                nc.vector.bn_stats(hst[:, t, :], h[:, t, :]).then_inc(s_hst, 1)

            over_tiles(dve, [(4, copy_w), (2, reciprocal), (1, logits), (3, values), (0, spread), (5, residual)], T, unroll=4, tail=2)

        def near_act2(act):
            def exps(t, q):
                b = q % 2
                act.wait_ge(s_nm, t + 1)
                if after(t, 2):
                    act.wait_ge(s_nr, t - 1)
                for head in range(NHN):
                    last = nc.scalar.activation(nl[q][:, head, :], nl[q][:, head, :], ACT.Exp, bias=nn[b][:, head:head + 1], accum_out=nsum[b][:, head:head + 1])
                last.then_inc(s_ne, 1)

            def copy_w(t, q):
                b = q % 2
                act.wait_ge(s_nT, t + 1)
                if after(t, 2):
                    act.wait_ge(s_nA, t - 1)
                nc.scalar.copy(pTa[b][:, 0:2], bank[3][0:TP, 0:4 * TP].rearrange("p (h c q) -> p h c q", h=2, c=2))
                nc.scalar.copy(pTb[b][:], bank[5][0:S, 0:4 * TP].rearrange("p (h q) -> p h q", h=NHN)).then_inc(s_nTa, 1)

            def copy_o(t, q):
                b = q % 2
                act.wait_ge(s_nA, t + 1)
                if after(t, 2):
                    act.wait_ge(s_nP, t - 1)
                nc.scalar.copy(noT[b][:], bank[6][:, 0:TP]).then_inc(s_noc, 1)

            def proj(t, q):
                b = q % 2
                act.wait_ge(s_nP, t + 1)
                if after(t, 2):
                    act.wait_ge(s_nF, t - 1)
                nc.scalar.activation(nz[b][:], bank[7][0:WN, 0:TP], ACT.Identity, bias=Cc["bproj"]).then_inc(s_nz, 1)

            over_tiles(act, [(5, copy_o), (4, copy_w), (5, proj), (1, exps)], T, unroll=4, tail=2)

        def near_pe(pe):
            pe.wait_ge(s_cci, 16)
            pe.wait_ge(s_h, 2 * T + T)

            def transpose_h(p, b):
                pe.wait_ge(s_hn, 2 * T + 2 * p + 2)
                if after(p, 1):
                    pe.wait_ge(s_hTc, 2 * T + p)
                for c in range(2):
                    for i in range(2):
                        last = nc.tensor.transpose(bank[0][0:HALF, c * PAIR + i * TP:c * PAIR + (i + 1) * TP], hp[b][:, i, c * HALF:(c + 1) * HALF], ident[0:TP, 0:TP])
                last.then_inc(s_hTr, 1)

            def fc1(p, b):
                pe.wait_ge(s_hTc, 2 * T + p + 1)
                if after(p, 1):
                    pe.wait_ge(s_f1c, p)
                for c in range(2):
                    last = nc.tensor.matmul(bank[1][0:WN, 0:PAIR], Cc["fc1"][:, c * WN:(c + 1) * WN], hpT[b][:, c, :], start=(c == 0), stop=(c == 1))
                last.then_inc(s_f1, 1)

            def conva(p, b):
                pe.wait_ge(s_f1c, p + 1)
                if after(p, 1):
                    pe.wait_ge(s_fAc, p)
                nc.tensor.matmul(bank[2][0:CONV, 0:PAIR], Cc["conva"], fx[b][:], start=True, stop=True).then_inc(s_fA, 1)

            def convb(p, b):
                pe.wait_ge(s_fAc, p + 1)
                if after(p, 1):
                    pe.wait_ge(s_fs, p)
                nc.tensor.matmul(bank[3][0:WN, 0:PAIR], Cc["convb"], fa[b][:], start=True, stop=True).then_inc(s_fB, 1)

            def keys(p, b):
                pe.wait_ge(s_fg, p + 1)
                if after(p, 1):
                    pe.wait_ge(s_fKc, p)
                nc.tensor.matmul(bank[4][0:WN, 0:PAIR], Cc["wk"], xg[:, bass.ds(PADR * S + p * PAIR, PAIR)], start=True, stop=True).then_inc(s_fK, 1)

            over_tiles(pe, [(3, convb), (0, transpose_h), (1, fc1), (2, conva), (4, keys)], T // 2)
            pe.wait_ge(s_fKc, T // 2)
            pe.wait_ge(s_hTc, 2 * T + T // 2)

            def query(t, q):
                if after(t, 1):
                    pe.wait_ge(s_nq, t)
                if after(t, 4):
                    pe.wait_ge(s_fVc, t - 1)
                elif t == 0:
                    pe.wait_ge(s_fVc, 2)
                nc.tensor.matmul(bank[0][0:WN, 0:TP], Cc["wq"], xg[:, bass.ds(PADR * S + t * TP, TP)], start=True, stop=True).then_inc(s_nQ, 1)

            def value(j, b):
                pe.wait_ge(s_fv, j + 1)
                if after(j, 1):
                    pe.wait_ge(s_fVc, j)
                nc.tensor.matmul(bank[0][0:TP, 128:128 + WN], vsrc[b][:], Cc["wv"], start=True, stop=True).then_inc(s_fV, 1)

            def values(t, q):
                if isinstance(t, int) and t + 3 >= T:
                    pe.wait_ge(s_nq, T)
                for j in value_tiles(t):
                    value(j, (j if isinstance(j, int) else q) % 2)

            for j in range(2):
                value(j, j)

            def scores(t, q, heads):
                first = (B - WIN + PADR) * S if isinstance(t, int) and t == T - 1 else t * TP
                pe.wait_ge(s_nq, t + 1)
                for head in heads:
                    if after(t, 1) or head >= 2:
                        pe.wait_ge(s_nl, 4 * t + head - 1)
                    nc.tensor.matmul(bank[1 + head % 2][0:TP, 0:KW], qx[q % 2][:, head, :], kT[:, bass.ds(first, KW)], start=True, stop=True).then_inc(s_nS, 1)

            def transpose_w(t, q):
                pe.wait_ge(s_nw, t + 1)
                if after(t, 1):
                    pe.wait_ge(s_nTa, t)
                    pe.wait_ge(s_nTd, t)
                for head in range(NHN):
                    for c in range(2):
                        k = (head % 2 * 2 + c) * TP
                        nc.tensor.transpose(bank[3 + head // 2][0:TP, k:k + TP], nl[q][:, head, c * TP:(c + 1) * TP], ident[0:TP, 0:TP])
                    last = nc.tensor.transpose(bank[5][0:S, head * TP:(head + 1) * TP], nl[q][:, head, 2 * TP:KW], ident[0:TP, 0:TP])
                last.then_inc(s_nT, 1)

            def values_out(t, q):
                b = q % 2
                pe.wait_ge(s_nTa, t + 1)
                pe.wait_ge(s_nTd, t + 1)
                tiles = vl if isinstance(t, int) and t == T - 1 else [vn[(q + i) % 4] for i in range(3)]
                pe.wait_ge(s_fVc, VT if isinstance(t, int) and t == T - 1 else t + 3)
                if after(t, 1):
                    pe.wait_ge(s_noc, t)
                for i in range(3):
                    for head in range(NHN):
                        p = pTa[b][:, head, i, :] if i < 2 else pTb[b][:, head, :]
                        v = tiles[i][:, head, :] if i < 2 else tiles[i][0:S, head, :]
                        last = nc.tensor.matmul(bank[6][head * VW:(head + 1) * VW, 0:TP], v, p, start=(i == 0), stop=(i == 2))
                last.then_inc(s_nA, 1)

            def proj(t, q):
                pe.wait_ge(s_noc, t + 1)
                if after(t, 1):
                    pe.wait_ge(s_h, 3 * T + t)
                nc.tensor.matmul(bank[7][0:WN, 0:TP], Cc["proj"], noT[q % 2][:], start=True, stop=True).then_inc(s_nP, 1)

            def fc2(t, q):
                pe.wait_ge(s_nz, t + 1)
                nc.tensor.matmul(bank[7][0:TP, 0:ED], nz[q % 2][:], Cc["fc2"], start=True, stop=True).then_inc(s_nF, 1)

            over_tiles(pe, [(0, query), (3, values), (1, lambda t, q: scores(t, q, (0, 1))), (5, proj),
                            (1, lambda t, q: scores(t, q, (2, 3))), (3, transpose_w), (5, fc2), (4, values_out)], T, unroll=4, tail=2)

        def route_act(act):
            h_std(act, 3)
            act.wait_ge(s_ph, 9 + 2)
            nc.scalar.activation(zrt[:], zsq[:], ACT.Sqrt, bias=eps6[:], scale=4.0).then_inc(s_hsd, 1)

            def copy_T(t, b):
                act.wait_ge(s_hTr, 5 * T // 2 + t + 1)
                if after(t, 2):
                    act.wait_ge(s_gl, t - 1)
                nc.scalar.copy(hnT[b][:], bank[5 * b][0:HALF, 0:2 * TP].rearrange("p (c q) -> p c q", c=2)).then_inc(s_hTc, 1)

            over_tiles(act, [(0, copy_T)], T)
            act.wait_ge(s_rt, 1)
            nc.scalar.activation(wexp[:], wdif[:], ACT.Exp).then_inc(s_re, 1)

        def route_pe(pe):
            def transpose_h(t, b):
                pe.wait_ge(s_hn, 3 * T + t + 1)
                if after(t, 2):
                    pe.wait_ge(s_hTc, 5 * T // 2 + t - 1)
                for c in range(2):
                    last = nc.tensor.transpose(bank[5 * b][0:HALF, c * TP:(c + 1) * TP], hn[b][:, c * HALF:(c + 1) * HALF], ident[0:TP, 0:TP])
                last.then_inc(s_hTr, 1)

            def router(t, b):
                pe.wait_ge(s_hTc, 5 * T // 2 + t + 1)
                for c in range(2):
                    last = nc.tensor.matmul(bank[1][0:TP, bass.ds(t * EX, EX)], hnT[b][:, c, :], Cc["router"][:, c * EX:(c + 1) * EX], start=(c == 0), stop=(c == 1))
                last.then_inc(s_gl, 1)

            over_tiles(pe, [(0, transpose_h), (1, router)], T)
            pe.wait_ge(s_rt, 2)
            marks = hots[:].rearrange("p t e -> p (t e)")
            nc.tensor.matmul(bank[2][0:TP, 0:T * EX], Cc["before"], marks, start=True, stop=True)
            nc.tensor.matmul(bank[3][0:TP, 0:T * EX], ones[0:TP, 0:TP], marks, start=True, stop=True).then_inc(s_rp, 1)

            def slots(p, b):
                pe.wait_ge(s_oh, p + 1)
                for i in range(2):
                    for k in range(2):
                        first = isinstance(p, int) and p == 0 and i == k == 0
                        final = isinstance(p, int) and p == T // 2 - 1 and i == k == 1
                        last = nc.tensor.matmul(bank[4][0:SP_, 0:2 * NST], ohp[b][:, k, i, :], ohc[b][:, k, i, :], start=first, stop=final)
                last.then_inc(s_ohp, 1)

            over_tiles(pe, [(0, slots)], T // 2, tail=1)

        def route_dve(dve):
            h_norm_constants(dve, 3)
            dve.wait_ge(s_ln, 20)
            nc.vector.memset(eps6[:], 1e-6)
            nc.vector.tensor_tensor(zsq[:], hvar[:], hrs[:], ALU.mult).then_inc(s_ph, 1)
            dve.wait_ge(s_ph, 9 + 1)
            nc.vector.tensor_tensor(zsq[:], zsq[:], hrs[:], ALU.mult).then_inc(s_ph, 1)
            dve.wait_ge(s_hsd, 5)
            nc.vector.reciprocal(zs[:], zrt[:]).then_inc(s_ph, 1)
            dve.wait_ge(s_ph, 9 + 3)
            nc.vector.scalar_tensor_tensor(out=zs[:], in0=zs[:], scalar=2.0, in1=hrs[:], op0=ALU.mult, op1=ALU.mult).then_inc(s_ph, 1)
            dve.wait_ge(s_ph, 9 + 4)

            def normalize(t, b):
                if after(t, 2):
                    dve.wait_ge(s_hTr, 5 * T // 2 + t - 1)
                nc.vector.tensor_scalar(hn[b][:], h[:, t, :], hmean[:, bass.ds(t, 1)], hrs[:, bass.ds(t, 1)], ALU.subtract, ALU.mult).then_inc(s_hn, 1)
                nc.vector.tensor_scalar(zk[:, t, :], h[:, t, :], hmean[:, bass.ds(t, 1)], zs[:, bass.ds(t, 1)], ALU.subtract, ALU.mult).then_inc(s_gz, 1)

            over_tiles(dve, [(0, normalize)], T)

            per_row = lambda a: a.unsqueeze(2).to_broadcast([TP, T, EX])
            index = Cc["count"][:, 0:EX].unsqueeze(1).to_broadcast([TP, T, EX])
            real = Cc["real"].unsqueeze(1).to_broadcast([TP, 2, T])
            dve.wait_ge(s_gl, T)
            logits = bank[1][0:TP, 0:T * EX].rearrange("p (t e) -> p t e", e=EX)
            r = 0
            for k in range(2):
                lg = lg2[:] if k else logits
                nc.vector.tensor_reduce(top[:, k, :], lg, AX.X, ALU.max).then_inc(s_r, 1)
                dve.wait_ge(s_r, r + 1)
                if k == 1:
                    nc.vector.tensor_tensor(wdif[:], top[:, 1, :], top[:, 0, :], ALU.subtract).then_inc(s_rt, 1)
                nc.vector.tensor_tensor(eq[:], lg, per_row(top[:, k, :]), ALU.is_equal).then_inc(s_r, 1)
                dve.wait_ge(s_r, r + 2)
                nc.vector.scalar_tensor_tensor(out=key[:], in0=eq[:], scalar=-float(EX), in1=index, op0=ALU.mult, op1=ALU.add).then_inc(s_r, 1)
                dve.wait_ge(s_r, r + 3)
                nc.vector.tensor_reduce(expert[:, k, :], key[:], AX.X, ALU.min).then_inc(s_r, 1)
                dve.wait_ge(s_r, r + 4)
                nc.vector.tensor_tensor(hot[:, k], key[:], per_row(expert[:, k, :]), ALU.is_equal).then_inc(s_r, 1)
                dve.wait_ge(s_r, r + 5)
                r += 5
                if k == 0:
                    nc.vector.scalar_tensor_tensor(out=lg2[:], in0=hot[:, 0], scalar=-1e30, in1=logits, op0=ALU.mult, op1=ALU.add).then_inc(s_r, 1)
                    dve.wait_ge(s_r, r + 1)
                    r += 1
            nc.vector.tensor_tensor(hots[:], hot[:, 0], hot[:, 1], ALU.add).then_inc(s_r, 1)
            dve.wait_ge(s_r, r + 1)
            nc.vector.tensor_tensor(hots[:], hots[:], per_row(Cc["real"]), ALU.mult).then_inc(s_rt, 1)

            dve.wait_ge(s_rp, 1)
            prior = bank[2][0:TP, 0:T * EX].rearrange("p (t e) -> p t e", e=EX)
            totals = bank[3][0:TP, 0:T * EX].rearrange("p (t e) -> p t e", e=EX)
            nc.vector.memset(sums[0][:, 0:1, :], 0.0)
            nc.vector.tensor_copy(sums[0][:, 1:T, :], totals[:, 0:T - 1, :]).then_inc(s_r, 1)
            r += 2
            dve.wait_ge(s_r, r)
            step, b = 1, 0
            while step < T:
                nc.vector.tensor_copy(sums[1 - b][:, 0:step, :], sums[b][:, 0:step, :])
                nc.vector.tensor_tensor(sums[1 - b][:, step:T, :], sums[b][:, step:T, :], sums[b][:, 0:T - step, :], ALU.add).then_inc(s_r, 1)
                r += 1
                dve.wait_ge(s_r, r)
                step, b = 2 * step, 1 - b
            nc.vector.tensor_tensor(place[:], prior, sums[b][:], ALU.add).then_inc(s_r, 1)
            dve.wait_ge(s_r, r + 1)
            nc.vector.tensor_tensor(picked[:], hot[:], place[:].unsqueeze(1).to_broadcast([TP, 2, T, EX]), ALU.mult).then_inc(s_r, 1)
            dve.wait_ge(s_r, r + 2)
            nc.vector.tensor_reduce(pk[:], picked[:], AX.X, ALU.add).then_inc(s_r, 1)
            dve.wait_ge(s_r, r + 3)
            nc.vector.scalar_tensor_tensor(out=kept[:], in0=pk[:], scalar=float(CAP), in1=real, op0=ALU.is_lt, op1=ALU.mult)
            nc.vector.tensor_scalar(jt[:], pk[:], float(SP_), None, ALU.is_ge).then_inc(s_r, 1)
            r += 4
            for i in range(2, SJ):
                dve.wait_ge(s_r, r)
                nc.vector.scalar_tensor_tensor(out=jt[:], in0=pk[:], scalar=float(i * SP_), in1=jt[:], op0=ALU.is_ge, op1=ALU.add).then_inc(s_r, 1)
                r += 1
            dve.wait_ge(s_r, r)
            nc.vector.scalar_tensor_tensor(out=prow[:], in0=jt[:], scalar=-float(SP_), in1=pk[:], op0=ALU.mult, op1=ALU.add)
            nc.vector.scalar_tensor_tensor(out=col[:], in0=expert[:], scalar=float(SJ), in1=jt[:], op0=ALU.mult, op1=ALU.add).then_inc(s_r, 1)
            dve.wait_ge(s_r, r + 1)
            nc.vector.scalar_tensor_tensor(out=col[:], in0=col[:], scalar=float(NST + 1), in1=kept[:], op0=ALU.add, op1=ALU.mult).then_inc(s_r, 1)
            dve.wait_ge(s_r, r + 2)
            nc.vector.tensor_scalar(col[:], col[:], -1.0, None, ALU.add)

            dve.wait_ge(s_re, 1)
            nc.vector.tensor_scalar(wsum[:], wexp[:], 1.0, None, ALU.add).then_inc(s_r, 1)
            dve.wait_ge(s_r, r + 3)
            nc.vector.reciprocal(wts[:, 0, :], wsum[:]).then_inc(s_r, 1)
            dve.wait_ge(s_r, r + 4)
            nc.vector.tensor_tensor(wts[:, 1, :], wexp[:], wts[:, 0, :], ALU.mult).then_inc(s_r, 1)
            dve.wait_ge(s_r, r + 5)
            nc.vector.tensor_tensor(wts[:], wts[:], kept[:], ALU.mult).then_inc(s_r, 1)
            dve.wait_ge(s_r, r + 6)

            def marks(p, b):
                if after(p, 2):
                    dve.wait_ge(s_ohp, p - 1)
                pair = bass.ds(2 * p, 2)
                count = Cc["count"].unsqueeze(1).unsqueeze(1)
                along = lambda a, n: a.unsqueeze(3).to_broadcast([TP, 2, 2, n])
                nc.vector.tensor_tensor(oht[b][:], count[:, :, :, 0:NST].to_broadcast([TP, 2, 2, NST]), along(col[:, :, pair], NST), ALU.is_equal).then_inc(s_oht, 1)
                nc.vector.tensor_tensor(ohp[b][:], count.to_broadcast([TP, 2, 2, SP_]), along(prow[:, :, pair], SP_), ALU.is_equal)
                dve.wait_ge(s_oht, p + 1)
                nc.vector.tensor_tensor(ohc[b][:, :, :, 0:NST], oht[b][:], along(Cc["number"][:, pair].unsqueeze(1).to_broadcast([TP, 2, 2]), NST), ALU.mult)
                nc.vector.tensor_tensor(ohc[b][:, :, :, NST:2 * NST], oht[b][:], along(wts[:, :, pair], NST), ALU.mult).then_inc(s_oh, 1)

            over_tiles(dve, [(0, marks)], T // 2)

            dve.wait_ge(s_ohp, T // 2)
            number = bank[4][0:SP_, 0:NST]
            nc.vector.scalar_tensor_tensor(out=empty[:], in0=number, scalar=0.5, in1=Cc["spare"], op0=ALU.is_lt, op1=ALU.mult)
            nc.vector.tensor_scalar(take_f[:], number, -1.0, 0.0, ALU.add, ALU.max)
            nc.vector.tensor_copy(wslot[:], bank[4][0:SP_, NST:2 * NST]).then_inc(s_r, 1)
            dve.wait_ge(s_r, r + 7)
            nc.vector.tensor_copy(take[:], take_f[:])
            nc.vector.scalar_tensor_tensor(out=put_f[:], in0=number, scalar=-1.0, in1=empty[:], op0=ALU.add, op1=ALU.add).then_inc(s_r, 1)
            dve.wait_ge(s_r, r + 8)
            nc.vector.tensor_copy(put[:], put_f[:]).then_inc(s_rt, 1)

            nc.vector.tensor_tensor(wsum[:], wts[:, 0, :], wts[:, 1, :], ALU.add).then_inc(s_r, 1)
            dve.wait_ge(s_r, r + 9)
            nc.vector.tensor_tensor(wsum[:], wsum[:], hrs[:], ALU.mult).then_inc(s_r, 1)
            dve.wait_ge(s_r, r + 10)
            nc.vector.tensor_scalar(own[:, 0, :], wsum[:], 1.0, None, ALU.add)
            nc.vector.tensor_tensor(own[:, 1, :], wsum[:], hmean[:], ALU.mult).then_inc(s_r, 1)
            dve.wait_ge(s_r, r + 11)

            def own_rows(t, b):
                nc.vector.tensor_scalar(h[:, t, :], h[:, t, :], own[:, 0, bass.ds(t, 1)], own[:, 1, bass.ds(t, 1)], ALU.mult, ALU.subtract).then_inc(s_id, 1)

            over_tiles(dve, [(0, own_rows)], T)

        def rows_pool(pool):
            pool.wait_ge(s_rt, 3)
            pool.wait_ge(s_zd, 16)

            def gather(e):
                b = e % 2
                if e >= 2:
                    pool.wait_ge(s_zT, 4 * e - 4)
                for j in range(SJ):
                    k = e * SJ + j
                    nc.gpsimd.indirect_dma_start(zr[b][:, j, :], None, z_rows, bass.IndirectOffsetOnAxis(ap=take[:, k:k + 1], axis=0), bounds_check=NROW - 1, oob_is_err=False).then_inc(s_zr[b], 16)

            gather(0)
            gather(1)
            pool.wait_ge(s_ido, 48)
            for e in range(EX):
                if e + 2 < EX:
                    gather(e + 2)
                pool.wait_ge(s_yc[0], SJ // 2 * (e + 1))
                pool.wait_ge(s_yc[1], SJ // 2 * (e + 1))
                if e:
                    pool.wait_ge(s_ad, 16 * SJ * e)
                for j in range(SJ):
                    k = e * SJ + j
                    nc.gpsimd.indirect_dma_start(rows_out, bass.IndirectOffsetOnAxis(ap=put[:, k:k + 1], axis=0), yr[e % 2][:, j, :], None, bounds_check=OUT - 1, oob_is_err=True, compute_op=ALU.add).then_inc(s_ad, 16)
            pool.wait_ge(s_ad, 16 * NST)

        def routed_sp(sp):
            sp.wait_ge(s_gz, T)
            sp.dma_start(z_rows.rearrange("(t p) d -> p t d", p=TP), zk[:]).then_inc(s_zd, 16)
            sp.wait_ge(s_id, T)
            sp.dma_start(rows_out[0:NROW].rearrange("(t p) d -> p t d", p=TP), h[:]).then_inc(s_ido, 16)
            n = (OUT - NROW) // TP
            sp.dma_start(rows_out[NROW:NROW + n * TP].rearrange("(t p) d -> p t d", p=TP), h[:, 0:n, :]).then_inc(s_ido, 16)
            sp.dma_start(rows_out[NROW + n * TP:OUT], h[0:OUT - NROW - n * TP, 0, :]).then_inc(s_ido, 16)

            def load(e, b):
                sp.wait_ge(s_gu, 16 * e - 16)
                sp.dma_start(w13[b][:], ins["w13"][e]).then_inc(s_w13[b], 16)
                sp.wait_ge(s_yp, SJ * (e - 1))
                sp.dma_start(w2r[b][:], ins["w2r"][e]).then_inc(s_w2r[b], 16)

            with sp.Fori(2, EX - 1, 2) as e:
                for b in range(2):
                    load(e + b, b)

        def routed_pe(pe):
            def transposes(e, b):
                pe.wait_ge(s_zr[b], 8 * SJ * (e - b) + 16 * SJ)
                for g in range(2):
                    for c in range(2):
                        if after(e, 1) or g:
                            pe.wait_ge(s_zc[c], 2 * e + g)
                        for j in range(SJ // 2):
                            last = nc.tensor.transpose(bank[c][0:HALF, j * SP_:(j + 1) * SP_], zr[b][:, g * SJ // 2 + j, c * HALF:(c + 1) * HALF], ident[0:SP_, 0:SP_])
                        last.then_inc(s_zT, 1)

            def gate_up(e, b):
                pe.wait_ge(s_w13[b], 8 * (e - b) + 16)
                for half in range(2):
                    for c in range(2):
                        pe.wait_ge(s_zc[c], 2 * e + half + 1)
                    for m in range(EH // 128):
                        k = half * (EH // 128) + m
                        if after(e, 1) or k >= 2:
                            pe.wait_ge(s_hT, 8 * e + k - 1)
                        for part in range(2):
                            at = part * EH + m * 128
                            for c in range(2):
                                last = nc.tensor.matmul(bank[2 + 2 * (m % 2) + part][:, 0:HS], w13[b][:, c, at:at + 128], zT[b][:, c, half * HS:(half + 1) * HS], start=(c == 0), stop=(c == 1))
                            last.then_inc(s_gu, 1)

            def outputs(e, b):
                pe.wait_ge(s_w2r[b], 8 * (e - b) + 16)
                for j in range(SJ):
                    pe.wait_ge(s_hT, 8 * e + 4 * (j * 2 // SJ + 1))
                    if after(e, 1) or j >= 2:
                        pe.wait_ge(s_yc[j % 2], SJ // 2 * e + j // 2)
                    for m in range(EH // 128):
                        last = nc.tensor.matmul(bank[6 + j % 2][0:SP_, 0:ED], hT[:, m, j * SP_:(j + 1) * SP_], w2r[b][:, m, :], start=(m == 0), stop=(m == EH // 128 - 1))
                    last.then_inc(s_yp, 1)

            over_tiles(pe, [(1, gate_up), (0, transposes), (1, outputs)], EX)

        def routed_act(act):
            def store_z(e, b):
                for g in range(2):
                    act.wait_ge(s_zT, 4 * e + 2 * g + 1)
                    if after(e, 2):
                        act.wait_ge(s_gu, 16 * e - 16)
                    nc.scalar.copy(act_tick[:, g:g + 1], eps5[:])
                    nc.scalar.activation(zT[b][:, 0, g * HS:(g + 1) * HS], bank[0][0:HALF, 0:HS], ACT.Copy, scale=Cc["gain"][:, bass.ds(e, 1)]).then_inc(s_zc[0], 1)

            def silu(e, b):
                for k in range(8):
                    act.wait_ge(s_gu, 16 * e + 2 * k + 1)
                    if after(e, 1) or k >= 2:
                        act.wait_ge(s_hT, 8 * e + k - 1)
                    nc.scalar.activation(sg[k % 2][:], bank[2 + 2 * (k % 2)][:, 0:HS], ACT.Silu).then_inc(s_sg, 1)

            def copy_y(e, b):
                for j in range(0, SJ, 2):
                    act.wait_ge(s_yp, SJ * e + j + 1)
                    if after(e, 2):
                        act.wait_ge(s_ad, 16 * SJ * (e - 1))
                    nc.scalar.copy(act_tick[:, 2 + j:3 + j], eps5[:])
                    nc.scalar.activation(yr[b][:, j, :], bank[6][0:SP_, 0:ED], ACT.Copy, scale=wslot[:, bass.ds(e * SJ + j, 1)]).then_inc(s_yc[0], 1)

            over_tiles(act, [(1, silu), (0, store_z), (1, copy_y)], EX)

        def routed_dve(dve):
            def store_z(e, b):
                for g in range(2):
                    dve.wait_ge(s_zT, 4 * e + 2 * g + 2)
                    if after(e, 2):
                        dve.wait_ge(s_gu, 16 * e - 16)
                    nc.vector.tensor_scalar(zT[b][:, 1, g * HS:(g + 1) * HS], bank[1][0:HALF, 0:HS], Cc["gain"][:, bass.ds(e + EX, 1)], None, ALU.mult).then_inc(s_zc[1], 1)

            def hidden(e, b):
                for k in range(8):
                    half, m = k // 4, k % 4
                    dve.wait_ge(s_sg, 8 * e + k + 1)
                    dve.wait_ge(s_gu, 16 * e + 2 * k + 2)
                    if after(e, 1):
                        dve.wait_ge(s_yp, SJ * e)
                    nc.vector.tensor_tensor(hT[:, m, half * HS:(half + 1) * HS], sg[k % 2][:], bank[3 + 2 * (k % 2)][:, 0:HS], ALU.mult).then_inc(s_hT, 1)

            def copy_y(e, b):
                for j in range(1, SJ, 2):
                    dve.wait_ge(s_yp, SJ * e + j + 1)
                    if after(e, 2):
                        dve.wait_ge(s_ad, 16 * SJ * (e - 1))
                    nc.vector.tensor_scalar(yr[b][:, j, :], bank[7][0:SP_, 0:ED], wslot[:, bass.ds(e * SJ + j, 1)], None, ALU.mult).then_inc(s_yc[1], 1)

            over_tiles(dve, [(1, hidden), (0, store_z), (1, copy_y)], EX)

        block = ctx.enter_context(nc.Block())

        @block.sync
        def _(sp):
            embed_sp(sp)
            sp.wait_ge(s_cbi, 16)
            experts_sp(sp)
            combine_sp(sp)
            near_sp(sp)
            routed_sp(sp)

        @block.gpsimd
        def _(pool):
            embed_pool(pool)
            experts_pool(pool)
            near_pool(pool)
            rows_pool(pool)

        @block.scalar
        def _(act):
            embed_act(act)
            attention_act(act)
            dispatch_act(act)
            experts_act(act)
            combine_act(act)
            near_act(act)
            near_act2(act)
            route_act(act)
            routed_act(act)

        @block.vector
        def _(dve):
            embed_dve(dve)
            attention_dve(dve)
            dispatch_dve(dve)
            experts_dve(dve)
            combine_dve(dve)
            near_dve(dve)
            route_dve(dve)
            routed_dve(dve)

        @block.tensor
        def _(pe):
            embed_pe(pe)
            attention_pe(pe)
            dispatch_pe(pe)
            experts_pe(pe)
            combine_pe(pe)
            near_pe(pe)
            route_pe(pe)
            routed_pe(pe)


def pack_rows(pack, parts):
    at, n = columns(pack)
    a = np.zeros((128, n), np.float32)
    for name, (rows, off, cols) in at.items():
        a[0:rows, off:off + cols] = parts[name]
    return a


def lay_out(i):
    f = {k: np.asarray(v) for k, v in i.items()}
    x = f["x"].reshape(B, C_IN, 6, PATCH, 6, PATCH).transpose(0, 2, 4, 3, 5, 1).reshape(B, NP_, PD)
    xr = np.zeros((T * GB, S, PD), np.float32)
    xr[0:B, 1:] = x
    per_image = lambda first, rest: np.tile(np.concatenate([first, rest]), (GB, 1))
    zero = np.zeros((1, ED), np.float32)
    rows = lambda v, n: np.tile(v[None, :], (n, 1))
    cls = f["L0_tok_cls_token"][None, :]
    ca = pack_rows(PACK_A, {
        "g1": f["L0_tok_ln1_g"].reshape(KC, 128).T, "b1": f["L0_tok_ln1_b"].reshape(KC, 128).T,
        "wtok": f["L0_tok_W"].reshape(KC, 128, ED).transpose(1, 0, 2).reshape(128, KC * ED),
        "btok": rows(f["L0_tok_b"], TP),
        "g2m": per_image(zero, rows(f["L0_tok_ln2_g"], NP_)), "b2m": per_image(zero, rows(f["L0_tok_ln2_b"], NP_)),
        "pos": np.tile(f["L0_tok_pos_embed"][0], (GB, 1)), "cls": per_image(cls, np.zeros((NP_, ED), np.float32)),
    })
    chunks = lambda w, n=2: w.reshape(n, -1, w.shape[1]).transpose(1, 0, 2).reshape(w.shape[0] // n, -1)
    wq, wk = (f["L0_attn_Wq"], f["L0_attn_Wk"])
    own = np.arange(TP)[:, None] // S == np.arange(TP)[None, :] // S
    causal = (own & (np.arange(TP)[:, None] <= np.arange(TP)[None, :])).astype(np.float32)
    cb = pack_rows(PACK_B, {
        "wqk": chunks(np.concatenate([wq, wk], 1)), "wvg": chunks(np.concatenate([f["L0_attn_Wv"], f["L0_attn_Wg"]], 1)),
        "wo": chunks(f["L0_attn_Wo"]), "causal": np.tile(causal, (1, 2)),
        "phi": chunks(f["L0_ffn_phi"][:, :, 0]), "scale": np.tile(f["L0_ffn_scale"][None, :], (HALF, 1)),
        "image": np.concatenate([np.arange(TP)[:, None] // S == np.arange(GB)[None, :], np.ones((TP, 1), bool)], 1).astype(np.float32),
        "b1s": f["L0_ffn_b1"].reshape(NE, HB, 128).transpose(2, 0, 1).reshape(128, NE * HB),
    })
    w1 = f["L0_ffn_w1"].reshape(NPAIR, 2, 2, HALF, HID).transpose(0, 3, 1, 2, 4)
    w2 = f["L0_ffn_w2"].reshape(NPAIR, 2, HB, 128, ED).transpose(0, 3, 1, 2, 4)
    col = lambda v: v[:, None]
    w = np.arange(TP)
    row, tok = w // S, w % S
    krow, ktok = np.arange(KW) // S, np.arange(KW) % S
    masks, near = np.zeros((TP, 4, KW), np.float32), np.zeros((2, TP, NHN, KW), np.float32)
    rpb = f["L1_attn_rpb"]
    for v, (q0, k0) in enumerate([(0, -PADR), (GB, GB - PADR), ((T - 2) * GB, (T - 2) * GB - PADR), ((T - 1) * GB, B - WIN)]):
        qr = q0 + row
        hs, ws = np.clip(qr - PADR, 0, B - WIN)[:, None], np.clip(tok - PADR, 0, S - WIN)[:, None]
        kr = (k0 + krow)[None, :]
        inside = (kr >= hs) & (kr < hs + WIN) & (ktok[None] >= ws) & (ktok[None] < ws + WIN)
        masks[:, v][(qr < B)[:, None] & ~inside] = -1e30
        if v in (1, 3):
            dr, dt = kr - qr[:, None] + WIN - 1, ktok[None] - tok[:, None] + WIN - 1
            ok = (dr >= 0) & (dr < 2 * WIN - 1) & (dt >= 0) & (dt < 2 * WIN - 1)
            for n in range(NHN):
                near[v // 2, :, n] = np.where(ok, rpb[n][np.where(ok, dr, 0), np.where(ok, dt, 0)], 0)
    qkv, bqkv = f["L1_attn_qkv_w"], f["L1_attn_qkv_b"]
    cc = pack_rows(PACK_C, {
        "fc1": chunks(f["L1_attn_fc1_w"].T), "conva": f["L1_attn_convA_w"].T, "convb": f["L1_attn_convB_w"].T,
        "wq": qkv[0:WN].T, "wk": qkv[WN:2 * WN].T, "wv": qkv[2 * WN:].T,
        "proj": np.pad(f["L1_attn_proj_w"].T.reshape(NHN, DN, WN), ((0, 0), (0, VW - DN), (0, 0))).reshape(NHN * VW, WN),
        "fc2": f["L1_attn_fc2_w"].T, "bv": rows(bqkv[2 * WN:], TP), "bfc2": rows(f["L1_attn_fc2_b"], TP),
        "bfc1": col(f["L1_attn_fc1_b"]), "bconva": col(f["L1_attn_convA_b"]), "bconvb": col(f["L1_attn_convB_b"]),
        "bq": col(bqkv[0:WN]), "bk": col(bqkv[WN:2 * WN]), "bproj": col(f["L1_attn_proj_b"]),
        "head": (np.arange(WN)[:, None] // DN == np.arange(NHN)[None, :]).astype(np.float32) * np.float32(DN ** -0.5),
        "router": chunks(f["L1_ffn_gate_w"].T), "before": (w[:, None] < w[None, :]).astype(np.float32),
        "count": np.tile(np.arange(SP_, dtype=np.float32)[None, :], (TP, 1)),
        "spare": 1.0 + B * S + np.arange(SP_)[:, None] + SP_ * (np.arange(NST) % SJ)[None, :],
        "number": (w[:, None] + TP * np.arange(T)[None, :] + 1).astype(np.float32),
        "real": (w[:, None] + TP * np.arange(T)[None, :] < B * S).astype(np.float32),
        "gain": chunks(f["L1_ffn_norm_w"].T),
    })
    w13 = f["L1_ffn_w13"].transpose(0, 2, 1).reshape(EX, 2, HALF, 2 * EH).transpose(0, 2, 1, 3)
    w2r = f["L1_ffn_w2"].transpose(0, 2, 1).reshape(EX, EH // 128, 128, ED).transpose(0, 2, 1, 3)
    return {"cc": cc, "masks": masks, "near": near, "w13": np.ascontiguousarray(w13), "w2r": np.ascontiguousarray(w2r),
            "w1": np.ascontiguousarray(w1), "w2": np.ascontiguousarray(w2), "x": xr.reshape(T, TP, PD),
            "xT": np.ascontiguousarray(xr.reshape(T, TP, KC, 128).transpose(0, 3, 2, 1)), "ca": ca, "cb": cb, "b2": np.ascontiguousarray(f["L0_ffn_b2"]),
            "ident": np.eye(128, dtype=np.float32)}


_INS = ("cc", "masks", "near", "w13", "w2r", "w1", "w2", "x", "xT", "ca", "cb", "b2", "ident")


def kernel(**inputs):
    import numpy as _np
    import concourse.bacc as _bacc
    from concourse import mybir as _mybir
    from concourse.bass_utils import run_bass_kernel_spmd as _run

    nc = _bacc.Bacc("TRN2", target_bir_lowering=False, num_devices=1)
    laid = lay_out(inputs)
    arrays, args = {}, {}
    for name in _INS:
        a = _np.ascontiguousarray(laid[name])
        arrays[f"in_{name}_dram"] = a
        args[name] = nc.dram_tensor(f"in_{name}_dram", a.shape, _mybir.dt.from_np(a.dtype), kind="ExternalInput").ap()
    out = nc.dram_tensor("out_0_dram", (OUT, ED), _mybir.dt.float32, kind="ExternalOutput").ap()
    tower(nc, args, out)
    r = _run(nc, [arrays], core_ids=[0])
    return r.results[0]["out_0_dram"][0:B * S].reshape(B, S, ED)
```
